# Optimizing a Trainium2 kernel written in Bass

```python
import numpy as np
import jax
import jax.numpy as jnp

def _softmax(x, axis=-1):
    return jax.nn.softmax(x, axis=axis)

def _gelu(x):
    return jax.nn.gelu(x, approximate=True)

def _silu(x):
    return jax.nn.silu(x)

def _sigmoid(x):
    return jax.nn.sigmoid(x)

def _layernorm(x, axis=-1, eps=1e-05):
    m = jnp.mean(x, axis=axis, keepdims=True)
    v = jnp.var(x, axis=axis, keepdims=True)
    return (x - m) / jnp.sqrt(v + eps)

def _scatter_add(tgt, idx, src, axis=0):
    return tgt.at[idx].add(src)

def _segment_sum(src, seg, n):
    return jax.ops.segment_sum(src, seg, n)
kernel_name = 'mk_gnn_resnorm_d2_gnn_r8_328b75'

def setup_inputs(seed: int=0):
    np.random.seed(seed)
    _w = jnp.asarray

    def _rec_inputs():
        import jax
        import jax.numpy as jnp
        _gk = jax.random.key(seed)
        x = -8.776e-05 + 1 * jax.random.normal(jax.random.fold_in(_gk, 1), (2500, 256), jnp.float32)
        _s = jax.random.randint(jax.random.fold_in(_gk, 2), (40000,), 0, 2500, jnp.int32)
        _d = jax.random.randint(jax.random.fold_in(_gk, 3), (40000,), 0, 2500, jnp.int32)
        _loop = jnp.arange(2500, dtype=jnp.int32)
        src = jnp.concatenate([_s, _d, _loop])
        dst = jnp.concatenate([_d, _s, _loop])
        _o = jnp.argsort(dst, stable=True)
        src = src[_o]
        dst = dst[_o]
        edge_type_2 = jax.random.randint(jax.random.fold_in(_gk, 13), (82500,), 0, 2, jnp.int32)
        edge_type_8 = jax.random.randint(jax.random.fold_in(_gk, 14), (82500,), 0, 8, jnp.int32)
        return (x, src, dst, edge_type_2, edge_type_8)
    x, src, dst, edge_type_2, edge_type_8 = _rec_inputs()

    def _L0_gnn_setup():
        import jax, jax.numpy as jnp
        import numpy as np
        N_NODES = 2500
        N_EDGES = 40000
        D = 256
        R = 8

        def _xavier(key, shape):
            fan_in, fan_out = (shape[-2], shape[-1])
            bound = float(np.sqrt(6.0 / (fan_in + fan_out)))
            return jax.random.uniform(key, shape, jnp.float32, -bound, bound)

        def _rgcn_layer(x, W, self_w, b, src, dst, edge_type, num_nodes):
            xW = jnp.einsum('ni,rio->rno', x, W)
            msg = xW[edge_type, src]
            agg = jax.ops.segment_sum(msg, dst, num_segments=num_nodes)
            return agg + x @ self_w + b
        key = jax.random.key(seed)
        ks = jax.random.split(key, 10)
        x = jax.random.normal(ks[0], (N_NODES, D), jnp.float32)
        edge_index = jax.random.randint(ks[1], (2, N_EDGES), 0, N_NODES)
        edge_type = jax.random.randint(ks[2], (N_EDGES,), 0, R)
        W1 = _xavier(ks[3], (R, D, D))
        self_w1 = _xavier(ks[4], (D, D))
        b1 = jnp.zeros((D,), jnp.float32)
        W2 = _xavier(ks[5], (R, D, D))
        self_w2 = _xavier(ks[6], (D, D))
        b2 = jnp.zeros((D,), jnp.float32)
        return {'x': x, 'W1': W1, 'self_w1': self_w1, 'b1': b1, 'W2': W2, 'self_w2': self_w2, 'b2': b2, 'edge_index': edge_index, 'edge_type': edge_type}
    _L0_gnn_all = _L0_gnn_setup()
    _L0_gnn_in = {k: v for k, v in _L0_gnn_all.items() if k in ('W1', 'self_w1', 'b1', 'W2', 'self_w2', 'b2')}
    del _L0_gnn_all

    def _L1_gnn_setup():
        import jax, jax.numpy as jnp
        import numpy as np
        N, E = (2500, 40000)
        IN_DIM, H, D = (256, 32, 8)
        NUM_ETYPES, L = (2, 2)

        def _hgt_layer(x, Wk, Wq, Wv, Wa, Watt, Wmsg, pri, skip, src, dst, etype):
            n = x.shape[0]
            k = (x @ Wk).reshape(n, H, D)
            q = (x @ Wq).reshape(n, H, D)
            v = (x @ Wv).reshape(n, H, D)
            k_e, q_e, v_e = (k[src], q[dst], v[src])
            is0 = (etype == 0)[:, None, None]
            kw = jnp.where(is0, jnp.einsum('ehd,hdf->ehf', k_e, Watt[:, 0]), jnp.einsum('ehd,hdf->ehf', k_e, Watt[:, 1]))
            m = jnp.where(is0, jnp.einsum('ehd,hdf->ehf', v_e, Wmsg[:, 0]), jnp.einsum('ehd,hdf->ehf', v_e, Wmsg[:, 1]))
            a = (kw * q_e).sum(-1) * pri[:, etype].T / np.float32(np.sqrt(D))
            amax = jax.ops.segment_max(a, dst, num_segments=n)
            ea = jnp.exp(a - amax[dst])
            att = ea / jax.ops.segment_sum(ea, dst, num_segments=n)[dst]
            h = jax.ops.segment_sum(m * att[:, :, None], dst, num_segments=n).reshape(n, H * D)
            h = h @ Wa
            alpha = jax.nn.sigmoid(skip)
            return h * alpha + x * (1.0 - alpha)
        key = jax.random.key(seed)
        ks = jax.random.split(key, 12)
        HD = H * D
        s = 0.02
        return {'x': jax.random.normal(ks[0], (N, IN_DIM), jnp.float32), 'Wk': jax.random.normal(ks[1], (L, IN_DIM, HD), jnp.float32) * s, 'Wq': jax.random.normal(ks[2], (L, IN_DIM, HD), jnp.float32) * s, 'Wv': jax.random.normal(ks[3], (L, IN_DIM, HD), jnp.float32) * s, 'Wa': jax.random.normal(ks[4], (L, HD, HD), jnp.float32) * s, 'Watt': jax.random.normal(ks[5], (L, H, NUM_ETYPES, D, D), jnp.float32) * s, 'Wmsg': jax.random.normal(ks[6], (L, H, NUM_ETYPES, D, D), jnp.float32) * s, 'pri': jnp.ones((L, H, NUM_ETYPES), jnp.float32), 'skip': jnp.ones((L,), jnp.float32), 'src': jax.random.randint(ks[7], (E,), 0, N), 'dst': jax.random.randint(ks[8], (E,), 0, N), 'etype': jax.random.randint(ks[9], (E,), 0, NUM_ETYPES)}
    _L1_gnn_all = _L1_gnn_setup()
    _L1_gnn_in = {k: v for k, v in _L1_gnn_all.items() if k in ('Wk', 'Wq', 'Wv', 'Wa', 'Watt', 'Wmsg', 'pri', 'skip')}
    del _L1_gnn_all
    return {'x': x, 'src': src, 'dst': dst, 'edge_type_2': edge_type_2, 'edge_type_8': edge_type_8, 'L0_gnn_W1': _L0_gnn_in['W1'], 'L0_gnn_self_w1': _L0_gnn_in['self_w1'], 'L0_gnn_b1': _L0_gnn_in['b1'], 'L0_gnn_W2': _L0_gnn_in['W2'], 'L0_gnn_self_w2': _L0_gnn_in['self_w2'], 'L0_gnn_b2': _L0_gnn_in['b2'], 'L1_gnn_Wk': _L1_gnn_in['Wk'], 'L1_gnn_Wq': _L1_gnn_in['Wq'], 'L1_gnn_Wv': _L1_gnn_in['Wv'], 'L1_gnn_Wa': _L1_gnn_in['Wa'], 'L1_gnn_Watt': _L1_gnn_in['Watt'], 'L1_gnn_Wmsg': _L1_gnn_in['Wmsg'], 'L1_gnn_pri': _L1_gnn_in['pri'], 'L1_gnn_skip': _L1_gnn_in['skip']}

def reference(x, src, dst, edge_type_2, edge_type_8, L0_gnn_W1, L0_gnn_self_w1, L0_gnn_b1, L0_gnn_W2, L0_gnn_self_w2, L0_gnn_b2, L1_gnn_Wk, L1_gnn_Wq, L1_gnn_Wv, L1_gnn_Wa, L1_gnn_Watt, L1_gnn_Wmsg, L1_gnn_pri, L1_gnn_skip):
    import jax
    import jax.numpy as jnp

    def _L0_gnn_ref(x, W1, self_w1, b1, W2, self_w2, b2, edge_index, edge_type):
        import jax, jax.numpy as jnp
        import numpy as np
        N_NODES = 2500
        N_EDGES = 40000
        D = 256
        R = 8

        def _xavier(key, shape):
            fan_in, fan_out = (shape[-2], shape[-1])
            bound = float(np.sqrt(6.0 / (fan_in + fan_out)))
            return jax.random.uniform(key, shape, jnp.float32, -bound, bound)

        def _rgcn_layer(x, W, self_w, b, src, dst, edge_type, num_nodes):
            xW = jnp.einsum('ni,rio->rno', x, W)
            msg = xW[edge_type, src]
            agg = jax.ops.segment_sum(msg, dst, num_segments=num_nodes)
            return agg + x @ self_w + b
        src, dst = (edge_index[0], edge_index[1])
        h = _rgcn_layer(x, W1, self_w1, b1, src, dst, edge_type, N_NODES)
        h = jax.nn.relu(h)
        out = _rgcn_layer(h, W2, self_w2, b2, src, dst, edge_type, N_NODES)
        return out

    def _L1_gnn_ref(x, Wk, Wq, Wv, Wa, Watt, Wmsg, pri, skip, src, dst, etype):
        import jax, jax.numpy as jnp
        import numpy as np
        N, E = (2500, 40000)
        IN_DIM, H, D = (256, 32, 8)
        NUM_ETYPES, L = (2, 2)

        def _hgt_layer(x, Wk, Wq, Wv, Wa, Watt, Wmsg, pri, skip, src, dst, etype):
            n = x.shape[0]
            k = (x @ Wk).reshape(n, H, D)
            q = (x @ Wq).reshape(n, H, D)
            v = (x @ Wv).reshape(n, H, D)
            k_e, q_e, v_e = (k[src], q[dst], v[src])
            is0 = (etype == 0)[:, None, None]
            kw = jnp.where(is0, jnp.einsum('ehd,hdf->ehf', k_e, Watt[:, 0]), jnp.einsum('ehd,hdf->ehf', k_e, Watt[:, 1]))
            m = jnp.where(is0, jnp.einsum('ehd,hdf->ehf', v_e, Wmsg[:, 0]), jnp.einsum('ehd,hdf->ehf', v_e, Wmsg[:, 1]))
            a = (kw * q_e).sum(-1) * pri[:, etype].T / np.float32(np.sqrt(D))
            amax = jax.ops.segment_max(a, dst, num_segments=n)
            ea = jnp.exp(a - amax[dst])
            att = ea / jax.ops.segment_sum(ea, dst, num_segments=n)[dst]
            h = jax.ops.segment_sum(m * att[:, :, None], dst, num_segments=n).reshape(n, H * D)
            h = h @ Wa
            alpha = jax.nn.sigmoid(skip)
            return h * alpha + x * (1.0 - alpha)
        h = x
        for l in range(L):
            h = _hgt_layer(h, Wk[l], Wq[l], Wv[l], Wa[l], Watt[l], Wmsg[l], pri[l], skip[l], src, dst, etype)
        return h
    edge_index = jnp.stack([src, dst])
    x = _layernorm(x + _L0_gnn_ref(x, L0_gnn_W1, L0_gnn_self_w1, L0_gnn_b1, L0_gnn_W2, L0_gnn_self_w2, L0_gnn_b2, edge_index, edge_type_8), axis=-1)
    x = _layernorm(x + _L1_gnn_ref(x, L1_gnn_Wk, L1_gnn_Wq, L1_gnn_Wv, L1_gnn_Wa, L1_gnn_Watt, L1_gnn_Wmsg, L1_gnn_pri, L1_gnn_skip, src, dst, edge_type_2), axis=-1)
    return x

_drawn_inputs = setup_inputs


def setup_inputs(seed=0):
    import zlib

    import numpy as np

    out = dict(_drawn_inputs(seed))
    spreads = {'L0_gnn_b1': (0.0, 0.394),
     'L0_gnn_b2': (0.0, 0.8),
     'L1_gnn_pri': (1.0, 0.6),
     'L1_gnn_skip': (1.0, 0.6)}
    factors = {'L1_gnn_Wk': 8.0,
     'L1_gnn_Wq': 8.0,
     'L1_gnn_Wv': 8.0,
     'L1_gnn_Wa': 8.0,
     'L1_gnn_Watt': 8.0,
     'L1_gnn_Wmsg': 8.0}
    for name, (base, spread) in spreads.items():
        noise = np.random.default_rng([zlib.crc32(name.encode()), seed]).standard_normal(out[name].shape)
        drawn = base * np.exp(spread * noise) if base else spread * noise
        out[name] = jnp.asarray(drawn.astype(out[name].dtype))
    for name, factor in factors.items():
        out[name] = (out[name] * factor).astype(out[name].dtype)
    return out
```

```python
from contextlib import ExitStack, contextmanager

import numpy as np
import concourse.bass as bass
from concourse import mybir

ALU = mybir.AluOpType
ACT = mybir.ActivationFunctionType
AX = mybir.AxisListType
F32 = mybir.dt.float32
I32 = mybir.dt.int32
RING = 4
STEPS = 4
BIG = 1e38
MAGIC = 1.5 * 2 ** 23
NO_NODE = 1 << 20


def ceil_div(a, b):
    return -(-a // b)


def need(eng, sem, value):
    if not isinstance(value, int) or value > 0:
        eng.wait_ge(sem, value)


def build(nc, x, src, dst, edge_type_2, edge_type_8, W1, self_w1, b1, W2, self_w2, b2,
          Wk, Wq, Wv, Wa, Watt, Wmsg, pri, skip, out):
    P = 128
    N, D = x.shape
    E = src.shape[0]
    R8 = W1.shape[0]
    H, R2, DH = Watt.shape[1], Watt.shape[2], Watt.shape[3]
    HW = DH + 1
    NT = ceil_div(N, P)
    LAST = N - (NT - 1) * P
    ET = ceil_div(E, P)
    NG = ceil_div((ET + NT - 1 + NT * (STEPS - 1)) // STEPS, RING) * RING
    NS = NG * STEPS
    KB = ceil_div(max(NS, ET + 1), P)
    ROUNDS = NG // RING
    KH = D // P
    T8, T2 = R8 * D, R2 * 2 * D
    FULL = E // (P * P)
    EPS = 1e-5

    edge_rows = nc.dram_tensor("edge_rows", (KB * P, 3 * P), F32).ap()
    step_nodes = nc.dram_tensor("step_nodes", (1 + KB * P, P), F32).ap()
    step_resets = nc.dram_tensor("step_resets", (1 + KB * P, P), F32).ap()
    step_tiles = nc.dram_tensor("step_tiles", (1, KB * P), I32).ap()
    table8 = nc.dram_tensor("table8", (NT * P * R8, D), F32).ap()
    table2 = nc.dram_tensor("table2", (NT * P * R2, 2 * D), F32).ap()

    top = ExitStack()

    def sb(name, shape, dt=F32, scope=top):
        return scope.enter_context(nc.sbuf_tensor(name, shape, dt))

    def sem(name):
        return nc.alloc_semaphore(name)

    @contextmanager
    def phase():
        earlier = nc.snapshot_sems()
        with ExitStack() as ph:
            yield ph
        nc.clear_and_free_semaphores(nc.allocated_since(earlier))
        nc.all_engine_barrier()

    with top:
        bank = [top.enter_context(nc.psum_tensor(f"bank{i}", [P, 512], F32)) for i in range(8)]
        X = sb("X", [P, NT, D])
        Hs = sb("Hs", [P, NT, D])
        OWN = sb("OWN", [P, NT, D])
        ident = sb("ident", [P, P])
        ones = sb("ones", [P, P])
        iota_free = sb("iota_free", [P, P])
        blockmask = sb("blockmask", [P, R2, DH])
        local = sb("local", [P, NS])
        index8 = sb("index8", [P, NS], I32)
        index2 = sb("index2", [P, NS], I32)
        first_local = sb("first_local", [32, NG])
        tile_of = sb("tile_of", [1, KB * P], I32)

        def prepare():
            with phase() as ph:
                def s(name):
                    return sem("p_" + name)

                def t(name, shape, dt=F32):
                    return sb("p_" + name, shape, dt, ph)

                raw = t("raw", [P, 4, KB, P], I32)
                rows = t("rows", [P, KB, 3, P])
                below = t("below", [P, NT + 1])
                junk = t("junk", [P, KB, P])
                total = t("total", [P, NT + 1])
                wk = t("wk", [P, 12, NT])
                one20 = t("one20", [P, NT])
                step_no = t("step_no", [P, KB])
                group_no = t("group_no", [P, KB])
                past = t("past", [P, KB, NT - 1])
                moved = t("moved", [P, KB, NT - 1])
                tile_f = t("tile_f", [P, KB])
                row_f = t("row_f", [P, KB])
                row_i = t("row_i", [P, KB], I32)
                tile_i = t("tile_i", [P, KB], I32)
                srow = t("srow", [P, KB, 3, P])
                inside = t("inside", [P, KB, P])
                inside2 = t("inside2", [P, KB, P])
                node = t("node", [P, KB, P])
                before = t("before", [P, KB, P])
                reset = t("reset", [P, KB, P])
                minus1 = t("minus1", [1, P])
                firstsel = t("firstsel", [P, 32])
                blk = t("blk", [P, P])

                loaded, x_loaded, padded, made = s("loaded"), s("x_loaded"), s("padded"), s("made")
                chain, consts, counted = s("chain"), s("consts"), s("counted")
                rows_ready, rows_out, picked = s("rows_ready"), s("rows_out"), s("picked")
                got = [s(f"got{b}") for b in range(KB)]
                nodes_ready, nodes_out, shifted = s("nodes_ready"), s("nodes_out"), s("shifted")
                resets_ready, tiles_in = s("resets_ready"), s("tiles_in")
                turned, taken, first_made = s("turned"), s("taken"), s("first_made")
                tail_out = s("tail_out")
                tailed = s("tailed")
                blkdone = s("blkdone")
                block = ph.enter_context(nc.Block())

                lists = (dst, src, edge_type_8, edge_type_2)
                tail_rows = E // P - FULL * P
                rest = E % P
                n_loads = 4 * (2 + (rest > 0))
                flat_nodes = step_nodes.rearrange("k e -> (k e)")

                @block.sync
                def _(sp):
                    sp.wait_ge(padded, 2)
                    for i, a in enumerate(lists):
                        whole = FULL * P * P
                        sp.dma_start(raw[:, i, 0:FULL, :],
                                     a[0:whole].rearrange("(b p e) -> p b e", p=P, e=P)).then_inc(loaded, 16)
                        sp.dma_start(raw[0:tail_rows, i, FULL, :],
                                     a[whole:whole + tail_rows * P].rearrange("(p e) -> p e", e=P)).then_inc(loaded, 16)
                        if rest:
                            sp.dma_start(raw[tail_rows:tail_rows + 1, i, FULL, 0:rest],
                                         a[E - rest:E].rearrange("(p e) -> p e", p=1)).then_inc(loaded, 16)
                    sp.dma_start(X[:, 0:NT - 1, :],
                                 x[0:(NT - 1) * P, :].rearrange("(j p) c -> p j c", p=P)).then_inc(x_loaded, 16)
                    sp.dma_start(X[0:LAST, NT - 1, :], x[(NT - 1) * P:N, :]).then_inc(x_loaded, 16)
                    sp.wait_ge(rows_ready, 1)
                    sp.dma_start(edge_rows.rearrange("(b p) c -> p b c", p=P),
                                 rows[:].rearrange("p b i e -> p b (i e)")).then_inc(rows_out, 16)
                    sp.wait_ge(nodes_ready, 1)
                    sp.dma_start(step_nodes[0:1, :], minus1[:, :]).then_inc(nodes_out, 16)
                    sp.dma_start(step_nodes[1:1 + KB * P, :].rearrange("(b p) e -> p b e", p=P),
                                 node[:]).then_inc(nodes_out, 16)
                    sp.wait_ge(nodes_out, 32)
                    sp.dma_start(before[:], flat_nodes[P - 1:P - 1 + KB * P * P].rearrange(
                        "(b p e) -> p b e", p=P, e=P)).then_inc(shifted, 16)
                    sp.dma_start(step_tiles[0, :].rearrange("(b p) -> p b", p=P), tile_i[:, :],
                                 allow_slow_non_contiguous=True).then_inc(tiles_in, 16)
                    sp.wait_ge(tiles_in, 16)
                    sp.dma_start(tile_of[:, :], step_tiles).then_inc(tiles_in, 16)
                    sp.wait_ge(resets_ready, 1)
                    sp.dma_start(step_resets[0:KB * P, :].rearrange("(b p) e -> p b e", p=P),
                                 reset[:]).then_inc(tail_out, 16)
                    sp.dma_start(step_resets[KB * P:KB * P + 1, :], minus1[:, :]).then_inc(tail_out, 16)
                    sp.wait_ge(tail_out, 32)
                    sp.wait_ge(tiles_in, 32)
                    sp.wait_ge(x_loaded, 32)

                @block.gpsimd
                def _(pool):
                    nc.gpsimd.iota(iota_free[:, :], pattern=[[1, P]], base=0, channel_multiplier=0,
                                   allow_small_or_imprecise_dtypes=True).then_inc(consts, 1)
                    nc.gpsimd.iota(step_no[:, :], pattern=[[P, KB]], base=0, channel_multiplier=1,
                                   allow_small_or_imprecise_dtypes=True).then_inc(consts, 1)
                    nc.gpsimd.memset(ident[:, :], 0.0).then_inc(made, 1)
                    nc.gpsimd.memset(firstsel[:, :], 0.0).then_inc(made, 1)
                    nc.gpsimd.iota(blk[:, 0:R2 * DH].rearrange("p (t h) -> p t h", t=R2),
                                   pattern=[[-DH, R2], [-DH * R2, DH]], base=0, channel_multiplier=1,
                                   allow_small_or_imprecise_dtypes=True).then_inc(consts, 1)
                    pool.wait_ge(made, 2)
                    nc.gpsimd.affine_select(out=ident[:, :], in_=ident[:, :], compare_op=ALU.not_equal, fill=1.0,
                                            base=0, pattern=[[-1, P]], channel_multiplier=1).then_inc(consts, 1)
                    nc.gpsimd.affine_select(out=firstsel[:, :], in_=firstsel[:, :], compare_op=ALU.not_equal,
                                            fill=1.0, base=0, pattern=[[0, 32]],
                                            channel_multiplier=1).then_inc(consts, 1)
                    pool.wait_ge(rows_out, 16)
                    pool.wait_ge(picked, 1)
                    for b in range(KB):
                        nc.gpsimd.indirect_dma_start(
                            out=srow[:, b].rearrange("p i e -> p (i e)"), out_offset=None, in_=edge_rows,
                            in_offset=bass.IndirectOffsetOnAxis(ap=row_i[:, b:b + 1], axis=0)).then_inc(got[b], 16)

                @block.tensor
                def _(pe):
                    pe.wait_ge(counted, 1)
                    nc.tensor.matmul(bank[0][:, 0:NT + 1], ones[:, :], below[:, :], start=True,
                                     stop=True).then_inc(turned, 1)
                    pe.wait_ge(consts, 5)
                    pe.wait_ge(nodes_ready, 1)
                    for i in range(3):
                        for b in range(KB):
                            n = i * KB + b
                            if n >= 4:
                                pe.wait_ge(taken, n - 3)
                            nc.tensor.transpose(bank[1 + n % 4][:, 0:P], srow[:, b, i, :], ident[:, :]).then_inc(turned, 1)
                    pe.wait_ge(taken, KB)
                    nc.tensor.matmul(bank[5][0:32, 0:NG], firstsel[:, :],
                                     local[:, 0:NS].rearrange("p (g u) -> p g u", u=STEPS)[:, :, 0],
                                     start=True, stop=True).then_inc(first_made, 1)

                @block.vector
                def _(dve):
                    v = nc.vector
                    n = [0]

                    def link(ins):
                        n[0] += 1
                        ins.then_inc(chain, 1)
                        dve.wait_ge(chain, n[0])

                    v.memset(raw[:, :, FULL:KB, :], 0)
                    link(v.memset(X[:, NT - 1, :], 0.0))
                    v.memset(raw[:, 0, FULL:KB, :], NO_NODE).then_inc(padded, 1)
                    v.memset(ones[:, :], 1.0)
                    v.memset(below[:, 0:1], 0.0)
                    v.memset(minus1[:, :], -1.0)
                    v.memset(one20[:, :], 1.0).then_inc(padded, 1)
                    dve.wait_ge(padded, 2)
                    dve.wait_ge(loaded, 16 * n_loads)
                    v.tensor_copy(rows[:, :, 0, :], raw[:, 0])
                    v.scalar_tensor_tensor(rows[:, :, 1, :], raw[:, 1], float(R8), raw[:, 2], ALU.mult, ALU.add)
                    link(v.scalar_tensor_tensor(rows[:, :, 2, :], raw[:, 1], float(R2), raw[:, 3], ALU.mult, ALU.add))
                    v.sem_inc(rows_ready, 1)
                    for j in range(1, NT + 1):
                        link(v.tensor_scalar(junk[:], rows[:, :, 0, :], float(min(j * P, N)), 0.0, ALU.is_lt, ALU.add,
                                             accum_out=below[:, j:j + 1]))
                    v.sem_inc(counted, 1)
                    dve.wait_ge(turned, 1)
                    link(v.tensor_copy(total[:, :], bank[0][:, 0:NT + 1]))
                    lo, hi = total[:, 0:NT], total[:, 1:NT + 1]

                    def whole(o, i, step, shift):
                        link(v.tensor_scalar(o, i, 1.0 / step, (shift - (step - 1) / 2) / step, ALU.mult, ALU.add))
                        link(v.tensor_scalar(o, o, MAGIC, None, ALU.add))
                        link(v.tensor_scalar(o, o, -MAGIC, None, ALU.add))

                    first_row, last_row, some, count, groups, upto, offset = (wk[:, i, :] for i in range(7))
                    whole(first_row, lo, P, 0)
                    whole(last_row, hi, P, -1)
                    link(v.tensor_tensor(some, hi, lo, ALU.is_gt))
                    link(v.tensor_tensor(count, last_row, first_row, ALU.subtract))
                    link(v.scalar_tensor_tensor(count, count, 1.0, some, ALU.add, ALU.mult))
                    whole(groups, count, STEPS, STEPS - 1)
                    link(v.tensor_tensor_scan(upto, one20[:, :], groups, 0.0, ALU.mult, ALU.add))
                    link(v.tensor_tensor(offset, upto, groups, ALU.subtract))
                    link(v.scalar_tensor_tensor(offset, offset, -float(STEPS), first_row, ALU.mult, ALU.add))
                    link(v.tensor_tensor(wk[:, 7, 0:NT - 1], offset[:, 1:NT], offset[:, 0:NT - 1], ALU.subtract))
                    dve.wait_ge(consts, 5)
                    whole(group_no[:, :], step_no[:, :], STEPS, 0)
                    shape = [P, KB, NT - 1]
                    link(v.tensor_tensor(past[:], group_no[:, :, None].to_broadcast(shape),
                                         upto[:, None, 0:NT - 1].to_broadcast(shape), ALU.is_ge))
                    link(v.tensor_tensor(moved[:], past[:], wk[:, 7, None, 0:NT - 1].to_broadcast(shape), ALU.mult))
                    v.tensor_reduce(tile_f[:, :], past[:], AX.X, ALU.add)
                    link(v.tensor_reduce(row_f[:, :], moved[:], AX.X, ALU.add))
                    link(v.tensor_tensor(row_f[:, :], row_f[:, :], step_no[:, :], ALU.add))
                    link(v.tensor_scalar(row_f[:, :], row_f[:, :], offset[:, 0:1], float(ET), ALU.add, ALU.min))
                    v.tensor_copy(tile_i[:, :], tile_f[:, :])
                    v.tensor_copy(row_i[:, :], row_f[:, :]).then_inc(picked, 1)
                    bm = blk[:, 0:R2 * DH].rearrange("p (t h) -> p t h", t=R2)
                    link(v.tensor_scalar(blockmask[:], bm, -0.5, None, ALU.is_gt))
                    link(v.tensor_scalar(bm, bm, DH - 0.5, None, ALU.is_lt))
                    link(v.tensor_tensor(blockmask[:], blockmask[:], bm, ALU.mult))
                    for b in range(KB):
                        dve.wait_ge(got[b], 16)
                    link(v.tensor_scalar(tile_f[:, :], tile_f[:, :], float(P), None, ALU.mult))
                    for b in range(KB):
                        v.tensor_scalar(inside[:, b], srow[:, b, 0, :], tile_f[:, b:b + 1], None, ALU.subtract)
                    link(v.tensor_scalar(node[:], srow[:, :, 0, :], 1.0, None, ALU.add))
                    link(v.tensor_scalar(inside2[:], inside[:], float(P), None, ALU.is_lt))
                    link(v.scalar_tensor_tensor(inside2[:], inside[:], 0.0, inside2[:], ALU.is_ge, ALU.mult))
                    link(v.tensor_tensor(node[:], node[:], inside2[:], ALU.mult))
                    link(v.tensor_scalar(node[:], node[:], -1.0, None, ALU.add))
                    link(v.tensor_copy(srow[:, :, 0, :], inside[:]))
                    v.sem_inc(nodes_ready, 1)
                    dve.wait_ge(shifted, 16)
                    link(v.tensor_tensor(reset[:], node[:], before[:], ALU.not_equal))
                    v.tensor_scalar(reset[:], reset[:], -BIG, None, ALU.mult).then_inc(resets_ready, 1)
                    for i in range(3):
                        for b in range(KB):
                            k = i * KB + b
                            w = min(P, NS - b * P)
                            dve.wait_ge(turned, 2 + k)
                            dest = (local, index8, index2)[i]
                            v.tensor_copy(dest[:, b * P:b * P + w], bank[1 + k % 4][:, 0:w]).then_inc(taken, 1)
                    dve.wait_ge(first_made, 1)
                    v.tensor_copy(first_local[:, :], bank[5][0:32, 0:NG])

        def dense(tag, xin, weights, n_table, table, bias):
            with phase() as ph:
                def s(name):
                    return sem(f"{tag}_{name}")

                xs = sb(f"{tag}_xs", [P, 2, D], F32, ph)
                xt = sb(f"{tag}_xt", [P, 2, KH, P], F32, ph)
                stage = sb(f"{tag}_stage", [P, 2, n_table], F32, ph)
                copied, turned, kept = s("copied"), s("turned"), s("kept")
                multiplied, act_took, dve_took = s("multiplied"), s("act_took"), s("dve_took")
                stored = [s("stored0"), s("stored1")]
                NCH = n_table // 512
                act_chunks = [c for c in range(NCH) if c % 2 == 0]
                dve_chunks = [c for c in range(NCH) if c % 2 == 1]
                rows_out = table.rearrange("(j p r) c -> p j (r c)", p=P, r=n_table // table.shape[1])
                block = ph.enter_context(nc.Block())

                def tiles(eng, step):
                    step(0, 0)
                    step(1, 1)
                    with eng.Fori(1, NT // 2) as i:
                        step(i * 2, 0)
                        step(i * 2 + 1, 1)

                def at(j):
                    return slice(j, j + 1) if isinstance(j, int) else bass.ds(j, 1)

                @block.vector
                def _(dve):
                    def step(j, r):
                        need(dve, turned, j - 1)
                        nc.vector.tensor_copy(xs[:, r, :], xin[:, at(j), :].rearrange("p a c -> p (a c)")).then_inc(copied, 1)
                        for k, c in enumerate(dve_chunks):
                            dve.wait_ge(multiplied, j * (NCH + 1) + c + 1)
                            if k == 0 and (not isinstance(j, int) or j >= 2):
                                dve.wait_ge(stored[r], (j - r) * 8)
                            nc.vector.tensor_copy(stage[:, r, c * 512:c * 512 + 512], bank[c][:, :]).then_inc(dve_took, 1)
                        dve.wait_ge(multiplied, j * (NCH + 1) + NCH + 1)
                        own = OWN[:, at(j), :].rearrange("p a c -> p (a c)")
                        if bias is None:
                            nc.vector.tensor_copy(own, bank[NCH][:, 0:D]).then_inc(dve_took, 1)
                        else:
                            nc.vector.tensor_tensor(own, bank[NCH][:, 0:D], bias[:, :], ALU.add).then_inc(dve_took, 1)
                    tiles(dve, step)

                @block.tensor
                def _(pe):
                    def step(j, r):
                        pe.wait_ge(copied, j + 1)
                        need(pe, kept, j - 1)
                        for h in range(KH):
                            last = nc.tensor.transpose(bank[6 + r][:, h * P:h * P + P],
                                                       xs[:, r, h * P:h * P + P], ident[:, :])
                        last.then_inc(turned, 1)
                        pe.wait_ge(kept, j + 1)
                        for c in range(NCH + 1):
                            w = 512 if c < NCH else D
                            if c in act_chunks:
                                need(pe, act_took, (j - 1) * len(act_chunks) + c // 2 + 1)
                            else:
                                need(pe, dve_took, (j - 1) * (len(dve_chunks) + 1)
                                     + (c // 2 if c < NCH else len(dve_chunks)) + 1)
                            for h in range(KH):
                                last = nc.tensor.matmul(bank[c][:, 0:w], xt[:, r, h, :],
                                                        weights[:, h, c * 512:c * 512 + w],
                                                        start=(h == 0), stop=(h == KH - 1))
                            last.then_inc(multiplied, 1)
                    tiles(pe, step)

                @block.scalar
                def _(act):
                    def step(j, r):
                        act.wait_ge(turned, j + 1)
                        need(act, multiplied, (j - 1) * (NCH + 1))
                        nc.scalar.copy(xt[:, r].rearrange("p h n -> p (h n)"), bank[6 + r][:, 0:D]).then_inc(kept, 1)
                        for k, c in enumerate(act_chunks):
                            act.wait_ge(multiplied, j * (NCH + 1) + c + 1)
                            if k == 0 and (not isinstance(j, int) or j >= 2):
                                act.wait_ge(stored[r], (j - r) * 8)
                            nc.scalar.copy(stage[:, r, c * 512:c * 512 + 512], bank[c][:, :]).then_inc(act_took, 1)
                    tiles(act, step)

                @block.sync
                def _(sp):
                    def step(j, r):
                        sp.wait_ge(act_took, (j + 1) * len(act_chunks))
                        sp.wait_ge(dve_took, j * (len(dve_chunks) + 1) + len(dve_chunks))
                        sp.dma_start(rows_out[:, at(j), :], stage[:, r:r + 1, :]).then_inc(stored[r], 16)
                    tiles(sp, step)
                    sp.wait_ge(stored[0], 16 * (NT // 2))
                    sp.wait_ge(stored[1], 16 * (NT // 2))

        def over_groups(eng, step, early=0, late=0):
            for g in range(-early, RING):
                step(g, g % RING)
            with eng.Fori(1, ROUNDS - 1) as i:
                for r in range(RING):
                    step(i * RING + r, r)
            for g in range(NG - RING, NG + late):
                step(g, g % RING)

        def exists(g):
            return not isinstance(g, int) or 0 <= g < NG

        def ring(r, lag):
            return (r + lag) % RING

        def span(g, width):
            return slice(g * width, (g + 1) * width) if isinstance(g, int) else bass.ds(g * width, width)

        def tile_at(eng, g):
            first = slice(g * STEPS, g * STEPS + 1) if isinstance(g, int) else bass.ds(g * STEPS, 1)
            return bass.ds(eng.value_load(tile_of[0:1, first], min_val=0, max_val=NT - 1), 1)

        def gather_groups(pool, pace, index, index_now, index_ready, table, rows, width, arrived, freed):
            def step(g, r):
                if not isinstance(g, int) or g >= RING:
                    pool.wait_ge(freed, g - RING + 1)
                    nc.gpsimd.sem_inc(pace, 1)
                nc.gpsimd.tensor_copy(index_now[:, r, :], index[:, span(g, STEPS)]).then_inc(index_ready, 1)
                pool.wait_ge(index_ready, g + 1)
                nc.gpsimd.sem_inc(pace, 1)
                for u in range(STEPS):
                    nc.gpsimd.indirect_dma_start(
                        out=rows[:, r, u, 0:width], out_offset=None, in_=table,
                        in_offset=bass.IndirectOffsetOnAxis(ap=index_now[:, r, u:u + 1], axis=0)
                    ).then_inc(arrived[r][u], 16)
            over_groups(pool, step)

        def uses(g, r):
            return g // RING + 1 if isinstance(g, int) else (g - r) // RING + 1

        def write_onehot(dve, onehot, r, g, ready):
            shape = [P, STEPS, P]
            nc.vector.tensor_tensor(onehot[:, r], iota_free[:, None, :].to_broadcast(shape),
                                    local[:, span(g, STEPS)][:, :, None].to_broadcast(shape),
                                    ALU.is_equal).then_inc(ready, 1)

        def convolve(tag):
            with phase() as ph:
                def s(name):
                    return sem(f"{tag}_{name}")

                rows = sb(f"{tag}_rows", [P, RING, STEPS, D], F32, ph)
                onehot = sb(f"{tag}_onehot", [P, RING, STEPS, P], F32, ph)
                index_now = sb(f"{tag}_index", [P, RING, STEPS], I32, ph)
                pace, index_ready = s("pace"), s("index_ready")
                arrived = [[s(f"arrived{r}_{u}") for u in range(STEPS)] for r in range(RING)]
                onehot_ready, summed, added = s("onehot_ready"), s("summed"), s("added")
                block = ph.enter_context(nc.Block())

                @block.gpsimd
                def _(pool):
                    gather_groups(pool, pace, index8, index_now, index_ready, table8, rows, D, arrived, summed)

                @block.vector
                def _(dve):
                    def step(g, r):
                        if exists(g + 1):
                            need(dve, summed, g + 2 - RING)
                            write_onehot(dve, onehot, ring(r, 1), g + 1, onehot_ready)
                        if exists(g):
                            own = OWN[:, tile_at(dve, g), :].rearrange("p a c -> p (a c)")
                            dve.wait_ge(summed, g + 1)
                            need(dve, added, g)
                            nc.vector.tensor_tensor(own, own, bank[r % 2][:, 0:D], ALU.add).then_inc(added, 1)
                    over_groups(dve, step, early=1)

                @block.tensor
                def _(pe):
                    def step(g, r):
                        pe.wait_ge(onehot_ready, g + 1)
                        need(pe, added, g - 1)
                        for u in range(STEPS):
                            pe.wait_ge(arrived[r][u], uses(g, r) * 16)
                            last = nc.tensor.matmul(bank[r % 2][:, 0:D], onehot[:, r, u, :], rows[:, r, u, :],
                                                    start=(u == 0), stop=(u == STEPS - 1))
                        last.then_inc(summed, 1)
                    over_groups(pe, step)

        def attend(tag, AGG):
            with phase() as ph:
                def s(name):
                    return sem(f"{tag}_{name}")

                def t(name, shape, dt=F32):
                    return sb(f"{tag}_{name}", shape, dt, ph)

                rows = t("rows", [P, RING, STEPS, 2 * D])
                onehot = t("onehot", [P, RING, STEPS, P])
                turned_onehot = t("turned_onehot", [P, 2, STEPS, P])
                index_now = t("index", [P, RING, STEPS], I32)
                resets = t("resets", [H, RING, STEPS * P + 1])
                scores = t("scores", [P, 2, STEPS, H])
                shifted = t("shifted", [P, 2, STEPS, H])
                forth = t("forth", [H, 2, STEPS * P])
                guard = t("guard", [H, 2, STEPS * P])
                change = t("change", [H, 2])
                factor = t("factor", [H, 2])
                pick = t("pick", [H, 2, P])
                spread = t("spread", [H, 2, H])
                weighted = t("weighted", [P, 2, STEPS, H, HW])
                pace, index_ready = s("pace"), s("index_ready")
                arrived = [[s(f"arrived{r}_{u}") for u in range(STEPS)] for r in range(RING)]
                resets_in = [s(f"resets_in{r}") for r in range(RING)]
                onehot_ready, onehot_turned, onehot_kept = s("onehot_ready"), s("onehot_turned"), s("onehot_kept")
                queried, multiplied, scored = s("queried"), s("multiplied"), s("scored")
                scores_turned, forth_ready, guard_ready = s("scores_turned"), s("forth_ready"), s("guard_ready")
                guard_turned, shifted_ready, weights_ready = s("guard_turned"), s("shifted_ready"), s("weights_ready")
                change_ready, factor_ready, pick_ready, factor_spread = (
                    s("change_ready"), s("factor_ready"), s("pick_ready"), s("factor_spread"))
                messages_ready, summed, scaled, added = s("messages_ready"), s("summed"), s("scaled"), s("added")
                cleared = s("cleared")
                block = ph.enter_context(nc.Block())

                q_bank = (bank[0], bank[1])
                onehot_bank, score_bank, guard_bank, sum_bank = bank[2], bank[3], bank[4], (bank[5], bank[6])
                factor_bank = bank[7]
                flat_resets = step_resets.rearrange("k e -> (k e)").rearrange("(o n) -> o n", o=1)

                @block.sync
                def _(sp):
                    def step(g, r):
                        need(sp, guard_ready, g - RING + 1)
                        w = STEPS * P
                        part = (slice(g * w, g * w + w + 1) if isinstance(g, int) else bass.ds(g * w, w + 1))
                        sp.dma_start(resets[:, r, :], flat_resets[:, part].to_broadcast([H, w + 1])).then_inc(resets_in[r], 16)
                    over_groups(sp, step)

                @block.gpsimd
                def _(pool):
                    gather_groups(pool, pace, index2, index_now, index_ready, table2, rows, 2 * D,
                                  arrived, messages_ready)

                @block.vector
                def _(dve):
                    v = nc.vector
                    v.memset(forth[:, 1, :], 0.0)
                    v.memset(guard[:, 1, :], 0.0)
                    v.memset(AGG[:], 0.0).then_inc(cleared, 1)
                    dve.wait_ge(cleared, 1)

                    def step(g, r):
                        e, o = r % 2, (r + 1) % 2
                        if exists(g + 1):
                            need(dve, summed, g + 2 - RING)
                            write_onehot(dve, onehot, ring(r, 1), g + 1, onehot_ready)
                        if exists(g - 1):
                            dve.wait_ge(factor_ready, g)
                            need(dve, factor_spread, g - 2)
                            v.scalar_tensor_tensor(spread[:, o, :], ident[0:H, 0:H], factor[:, o:o + 1],
                                                   ident[0:H, 0:H], ALU.mult, ALU.subtract)
                            firsts = first_local[:, slice(g - 1, g) if isinstance(g, int) else bass.ds(g - 1, 1)]
                            v.tensor_tensor(pick[:, o, :], iota_free[0:H, :], firsts.to_broadcast([H, P]),
                                            ALU.is_equal).then_inc(pick_ready, 1)
                        if exists(g - 2):
                            agg = AGG[:, tile_at(dve, g - 2)].rearrange("p a h w -> p (a h) w")
                            dve.wait_ge(factor_spread, g - 1)
                            need(dve, added, g - 2)
                            fac = factor_bank[:, 0:H]
                            v.scalar_tensor_tensor(agg, fac[:, :, None].to_broadcast([P, H, HW]), 1.0, agg,
                                                   ALU.add, ALU.mult).then_inc(scaled, 1)
                            dve.wait_ge(scaled, g - 1)
                            dve.wait_ge(summed, g - 1)
                            v.tensor_tensor(agg, agg, sum_bank[e][:, 0:H * HW].rearrange("p (h w) -> p h w", h=H),
                                            ALU.add).then_inc(added, 1)
                        if exists(g):
                            for half in range(2):
                                us = slice(half * 2, half * 2 + 2)
                                dve.wait_ge(queried, g * 2 + half + 1)
                                for u in range(half * 2, half * 2 + 2):
                                    dve.wait_ge(arrived[r][u], uses(g, r) * 16)
                                v.tensor_tensor(rows[:, r, us, 0:D], rows[:, r, us, 0:D],
                                                q_bank[half][:, :].rearrange("p (u c) -> p u c", u=2),
                                                ALU.mult).then_inc(multiplied, 1)
                            dve.wait_ge(multiplied, g * 2 + 2)
                            need(dve, weights_ready, g - 1)
                            need(dve, scores_turned, g - 1)
                            v.tensor_reduce(scores[:, e], rows[:, r, :, 0:D].rearrange("p u (h d) -> p u h d", h=H),
                                            AX.X, ALU.add).then_inc(scored, 1)
                        if exists(g - 1):
                            q = ring(r, -1)
                            dve.wait_ge(weights_ready, g)
                            v.tensor_tensor(weighted[:, o, :, :, 0:DH],
                                            rows[:, q, :, D:2 * D].rearrange("p u (h d) -> p u h d", h=H),
                                            weighted[:, o, :, :, DH:HW].to_broadcast([P, STEPS, H, DH]),
                                            ALU.mult).then_inc(messages_ready, 1)
                        if exists(g):
                            dve.wait_ge(resets_in[r], uses(g, r) * 16)
                            dve.wait_ge(scores_turned, g + 1)
                            need(dve, forth_ready, g)
                            need(dve, guard_ready, g)
                            v.tensor_tensor_scan(forth[:, e, :], resets[:, r, 0:STEPS * P], score_bank[0:H, :],
                                                 forth[:, o, STEPS * P - 1:STEPS * P], ALU.add,
                                                 ALU.max).then_inc(forth_ready, 1)
                            dve.wait_ge(forth_ready, g + 1)
                            need(dve, guard_turned, g - 1)
                            v.tensor_tensor_scan(guard[:, e, ::-1], resets[:, r, STEPS * P:0:-1], forth[:, e, ::-1],
                                                 -BIG, ALU.add, ALU.max).then_inc(guard_ready, 1)
                            dve.wait_ge(guard_ready, g + 1)
                            need(dve, factor_ready, g - 1)
                            v.tensor_scalar(change[:, e:e + 1], guard[:, o, STEPS * P - 1:STEPS * P],
                                            guard[:, e, 0:1], 0.0, ALU.subtract, ALU.min).then_inc(change_ready, 1)
                            dve.wait_ge(guard_turned, g + 1)
                            v.tensor_tensor(shifted[:, e], scores[:, e],
                                            guard_bank[:, 0:P].rearrange("p (u h) -> p u h", u=STEPS),
                                            ALU.subtract).then_inc(shifted_ready, 1)
                    over_groups(dve, step, early=1, late=2)

                @block.tensor
                def _(pe):
                    def step(g, r):
                        e, o = r % 2, (r + 1) % 2
                        n = ring(r, 1)
                        if exists(g + 1):
                            pe.wait_ge(onehot_ready, g + 2)
                            need(pe, onehot_kept, g + 1)
                            for u in range(STEPS):
                                last = nc.tensor.transpose(onehot_bank[:, u * P:u * P + P], onehot[:, n, u, :], ident[:, :])
                            last.then_inc(onehot_turned, 1)
                        if exists(g - 1):
                            pe.wait_ge(pick_ready, g)
                            need(pe, scaled, g - 1)
                            nc.tensor.matmul(factor_bank[:, 0:H], pick[:, o, :], spread[:, o, :],
                                             start=True, stop=True).then_inc(factor_spread, 1)
                        if exists(g):
                            pe.wait_ge(scored, g + 1)
                            need(pe, forth_ready, g)
                            for u in range(STEPS):
                                last = nc.tensor.matmul(score_bank[0:H, u * P:u * P + P], scores[:, e, u, :],
                                                        ident[:, :], start=True, stop=True)
                            last.then_inc(scores_turned, 1)
                        if exists(g + 1):
                            query = OWN[:, tile_at(pe, g + 1), :].rearrange("p a c -> p (a c)")
                            pe.wait_ge(onehot_kept, g + 2)
                            for half in range(2):
                                need(pe, multiplied, g * 2 + half + 1)
                                for u in range(2):
                                    last = nc.tensor.matmul(q_bank[half][:, u * D:u * D + D],
                                                            turned_onehot[:, o, half * 2 + u, :], query,
                                                            start=True, stop=True)
                                last.then_inc(queried, 1)
                        if exists(g - 1):
                            q = ring(r, -1)
                            pe.wait_ge(messages_ready, g)
                            need(pe, added, g - 2)
                            for u in range(STEPS):
                                last = nc.tensor.matmul(sum_bank[o][:, 0:H * HW], onehot[:, q, u, :],
                                                        weighted[:, o, u].rearrange("p h w -> p (h w)"),
                                                        start=(u == 0), stop=(u == STEPS - 1))
                            last.then_inc(summed, 1)
                        if exists(g):
                            pe.wait_ge(guard_ready, g + 1)
                            need(pe, shifted_ready, g)
                            for u in range(STEPS):
                                last = nc.tensor.matmul(guard_bank[:, u * H:u * H + H],
                                                        guard[:, e, u * P:u * P + P], ident[0:H, 0:H],
                                                        start=True, stop=True)
                            last.then_inc(guard_turned, 1)
                    over_groups(pe, step, early=1, late=1)

                @block.scalar
                def _(act):
                    def step(g, r):
                        e, o = r % 2, (r + 1) % 2
                        if exists(g + 1):
                            act.wait_ge(onehot_turned, g + 2)
                            need(act, queried, g * 2)
                            nc.scalar.copy(turned_onehot[:, o].rearrange("p u n -> p (u n)"),
                                           onehot_bank[:, :]).then_inc(onehot_kept, 1)
                        if exists(g):
                            act.wait_ge(change_ready, g + 1)
                            need(act, pick_ready, g - 1)
                            nc.scalar.activation(factor[:, e:e + 1], change[:, e:e + 1], ACT.Exp).then_inc(factor_ready, 1)
                            act.wait_ge(shifted_ready, g + 1)
                            need(act, summed, g - 1)
                            nc.scalar.activation(weighted[:, e, :, :, DH],
                                                 shifted[:, e], ACT.Exp).then_inc(weights_ready, 1)
                    over_groups(act, step, early=1)

        def norm(tag, A, B, store):
            with phase() as ph:
                stats = sb(f"{tag}_stats", [P, NT, 6], F32, ph)
                mv = sb(f"{tag}_mv", [P, NT, 2], F32, ph)
                rstd = sb(f"{tag}_rstd", [P, NT], F32, ph)
                eps = sb(f"{tag}_eps", [P, 1], F32, ph)
                chain, var_ready, rooted, done, stored = (
                    sem(f"{tag}_{k}") for k in ("chain", "var_ready", "rooted", "done", "stored"))
                block = ph.enter_context(nc.Block())

                @block.vector
                def _(dve):
                    v = nc.vector
                    v.memset(eps[:, :], EPS)
                    v.tensor_tensor(A[:], A[:], B[:], ALU.add).then_inc(chain, 1)
                    dve.wait_ge(chain, 1)
                    with dve.Fori(0, NT) as j:
                        v.bn_stats(stats[:, bass.ds(j, 1), :].rearrange("p a c -> p (a c)"),
                                   A[:, bass.ds(j, 1), :].rearrange("p a c -> p (a c)")).then_inc(chain, 1)
                    dve.wait_ge(chain, 1 + NT)
                    for j in range(NT):
                        v.bn_aggr(mv[:, j, :], stats[:, j, :]).then_inc(var_ready, 1)
                    dve.wait_ge(rooted, 1)
                    v.reciprocal(rstd[:, :], rstd[:, :])
                    shape = [P, NT, D]
                    v.tensor_tensor(A[:], A[:], mv[:, :, 0:1].to_broadcast(shape), ALU.subtract).then_inc(chain, 1)
                    dve.wait_ge(chain, 2 + NT)
                    v.tensor_tensor(A[:], A[:], rstd[:, :, None].to_broadcast(shape), ALU.mult).then_inc(done, 1)

                @block.scalar
                def _(act):
                    act.wait_ge(var_ready, NT)
                    nc.scalar.activation(rstd[:, :], mv[:, :, 1], ACT.Sqrt, bias=eps[:, 0:1]).then_inc(rooted, 1)

                if store:
                    @block.sync
                    def _(sp):
                        sp.wait_ge(done, 1)
                        sp.dma_start(out[0:(NT - 1) * P, :].rearrange("(j p) c -> p j c", p=P),
                                     A[:, 0:NT - 1, :]).then_inc(stored, 16)
                        sp.dma_start(out[(NT - 1) * P:N, :], A[0:LAST, NT - 1, :]).then_inc(stored, 16)
                        sp.wait_ge(stored, 32)

        def conv_layer(tag, xin, W, self_w, b):
            with phase() as ph:
                weights = sb(f"{tag}_weights", [P, KH, T8 + D], F32, ph)
                bias = sb(f"{tag}_bias", [P, D], F32, ph)
                loaded = sem(f"{tag}_loaded")
                with nc.Block() as block:
                    @block.sync
                    def _(sp):
                        for r in range(R8):
                            sp.dma_start(weights[:, :, r * D:(r + 1) * D],
                                         W[r].rearrange("(h p) c -> p h c", p=P)).then_inc(loaded, 16)
                        sp.dma_start(weights[:, :, T8:], self_w.rearrange("(h p) c -> p h c", p=P)).then_inc(loaded, 16)
                        sp.dma_start(bias[:, :], b.rearrange("(o c) -> o c", o=1).to_broadcast([P, D])).then_inc(loaded, 16)
                        sp.wait_ge(loaded, 16 * (R8 + 2))
                dense(tag + "_d", xin, weights, T8, table8, bias)
            convolve(tag + "_c")

        def relu_layer():
            with nc.Block() as block:
                @block.vector
                def _(dve):
                    nc.vector.tensor_scalar(Hs[:], OWN[:], 0.0, None, ALU.max)

        def head_weights(tag, layer, weights):
            with phase() as ph:
                def t(name, shape, dt=F32):
                    return sb(f"{tag}_{name}", shape, dt, ph)

                def s(name):
                    return sem(f"{tag}_{name}")

                NB = H // DH
                plain = t("plain", [P, 2, KH, D])
                wide = t("wide", [P, 2, KH, NB, P])
                turned = t("turned", [P, 2, KH, NB, P])
                small = t("small", [P, 2, NB, DH])
                prior = t("prior", [P, NB])
                blocks = t("blocks", [P, 2, NB, R2, DH, DH])
                loaded, ready, made, moved, kept, multiplied, taken = (
                    s(k) for k in ("loaded", "ready", "made", "moved", "kept", "multiplied", "taken"))
                block = ph.enter_context(nc.Block())
                pri_flat = pri[layer].rearrange("h t -> (h t)")
                PB = DH * R2

                @block.sync
                def _(sp):
                    sp.dma_start(plain[:, 0], Wk[layer].rearrange("(h p) c -> p h c", p=P)).then_inc(loaded, 16)
                    sp.dma_start(plain[:, 1], Wv[layer].rearrange("(h p) c -> p h c", p=P)).then_inc(loaded, 16)
                    sp.dma_start(weights[:, :, T2:], Wq[layer].rearrange("(h p) c -> p h c", p=P)).then_inc(loaded, 16)
                    for i, a in enumerate((Watt, Wmsg)):
                        sp.dma_start(small[:, i], a[layer].rearrange("h t d f -> (h t d) f")
                                     .rearrange("(b p) f -> p b f", p=P)).then_inc(loaded, 16)
                    for b in range(NB):
                        sp.dma_start(prior[:, b:b + 1], pri_flat[b * PB:(b + 1) * PB].rearrange("(k o) -> k o", o=1)
                                     .to_broadcast([PB, DH])).then_inc(loaded, 16)
                    sp.wait_ge(loaded, 16 * (5 + NB))

                @block.vector
                def _(dve):
                    v = nc.vector
                    dve.wait_ge(loaded, 16 * (5 + NB))
                    for i in range(2):
                        for h in range(KH):
                            v.tensor_copy(wide[:, i, h].rearrange("p b (h t d) -> p (b h) t d", h=DH, t=R2),
                                          plain[:, i, h].rearrange("p (h d) -> p h d", h=H)[:, :, None, :]
                                          .to_broadcast([P, H, R2, DH])).then_inc(ready, 1)
                    v.tensor_tensor(small[:, 0], small[:, 0], prior[:, :, None].to_broadcast([P, NB, DH]),
                                    ALU.mult).then_inc(made, 1)
                    dve.wait_ge(made, 1)
                    v.tensor_scalar(small[:, 0], small[:, 0], float(np.float32(1) / np.sqrt(np.float32(DH))), None,
                                    ALU.mult).then_inc(made, 1)
                    dve.wait_ge(made, 2)
                    for i in range(2):
                        for b in range(NB):
                            v.tensor_tensor(blocks[:, i, b].rearrange("p t h f -> p (t h) f"),
                                            blockmask[:].rearrange("p t h -> p (t h)")[:, :, None].to_broadcast([P, PB, DH]),
                                            small[:, i, b, None, :].to_broadcast([P, PB, DH]), ALU.mult).then_inc(made, 1)
                    for n in range(2 * KH):
                        dve.wait_ge(moved, n + 1)
                        v.tensor_copy(turned[:, n // KH, n % KH].rearrange("p b c -> p (b c)"),
                                      bank[n][:, :]).then_inc(kept, 1)
                    for n in range(2 * KH):
                        i, h = n // KH, n % KH
                        dve.wait_ge(multiplied, n + 1)
                        dest = weights[:, h, 0:T2].rearrange("p (t i h f) -> p t i h f", t=R2, i=2, h=H)[:, :, i]
                        for b in range(NB):
                            v.tensor_copy(dest[:, :, b * DH:(b + 1) * DH, :].rearrange("p t h f -> p t (h f)"),
                                          bank[n][:, b * P:(b + 1) * P].rearrange("p (t c) -> p t c", t=R2))

                @block.tensor
                def _(pe):
                    for n in range(2 * KH):
                        i, h = n // KH, n % KH
                        pe.wait_ge(ready, n + 1)
                        for b in range(NB):
                            last = nc.tensor.transpose(bank[n][:, b * P:(b + 1) * P], wide[:, i, h, b, :], ident[:, :])
                        last.then_inc(moved, 1)
                    pe.wait_ge(made, 2 + 2 * NB)
                    for n in range(2 * KH):
                        i, h = n // KH, n % KH
                        pe.wait_ge(kept, n + 1)
                        for b in range(NB):
                            last = nc.tensor.matmul(bank[n][:, b * P:(b + 1) * P], turned[:, i, h, b, :],
                                                    blocks[:, i, b].rearrange("p t h f -> p (t h f)"),
                                                    start=True, stop=True)
                        last.then_inc(multiplied, 1)

        def mix_layer(tag, layer, xin, AGG):
            with phase() as ph:
                def t(name, shape, dt=F32):
                    return sb(f"{tag}_{name}", shape, dt, ph)

                def s(name):
                    return sem(f"{tag}_{name}")

                wa = t("wa", [P, KH, D])
                gate = t("gate", [P, 4])
                attended = t("attended", [P, 2, D])
                below = t("below", [P, 2, H])
                xt = t("xt", [P, 2, KH, P])
                rest = t("rest", [P, 2, D])
                loaded, chain, opened, exped = s("loaded"), s("chain"), s("opened"), s("exped")
                bounded, inverted, divided = s("bounded"), s("inverted"), s("divided")
                turned, kept, multiplied, mixed, scaled = (
                    s("turned"), s("kept"), s("multiplied"), s("mixed"), s("scaled"))
                block = ph.enter_context(nc.Block())

                def tiles(eng, step):
                    for j in range(2):
                        step(j, j)
                    with eng.Fori(1, NT // 2) as i:
                        step(i * 2, 0)
                        step(i * 2 + 1, 1)

                def at(j):
                    return slice(j, j + 1) if isinstance(j, int) else bass.ds(j, 1)

                @block.sync
                def _(sp):
                    sp.dma_start(wa[:], Wa[layer].rearrange("(h p) c -> p h c", p=P)).then_inc(loaded, 16)
                    sp.dma_start(gate[:, 0:1], skip[layer:layer + 1].rearrange("(o c) -> o c", o=1)
                                 .to_broadcast([P, 1])).then_inc(loaded, 16)
                    sp.wait_ge(loaded, 32)

                @block.scalar
                def _(act):
                    act.wait_ge(loaded, 32)
                    nc.scalar.activation(gate[:, 1:2], gate[:, 0:1], ACT.Exp, scale=-1.0).then_inc(exped, 1)

                    def step(j, r):
                        act.wait_ge(turned, j + 1)
                        need(act, multiplied, j - 1)
                        nc.scalar.copy(xt[:, r].rearrange("p h n -> p (h n)"), bank[r][:, 0:D]).then_inc(kept, 1)
                    tiles(act, step)

                @block.vector
                def _(dve):
                    v = nc.vector
                    dve.wait_ge(exped, 1)
                    v.tensor_scalar(gate[:, 1:2], gate[:, 1:2], 1.0, None, ALU.add).then_inc(chain, 1)
                    dve.wait_ge(chain, 1)
                    v.reciprocal(gate[:, 2:3], gate[:, 1:2]).then_inc(chain, 1)
                    dve.wait_ge(chain, 2)
                    v.tensor_scalar(gate[:, 3:4], gate[:, 2:3], -1.0, 1.0, ALU.mult, ALU.add).then_inc(chain, 1)
                    dve.wait_ge(chain, 3)

                    def step(j, r):
                        v.tensor_scalar(below[:, r], AGG[:, at(j), :, DH].rearrange("p a h -> p (a h)"),
                                        1e-30, None, ALU.max).then_inc(bounded, 1)
                        dve.wait_ge(bounded, j + 1)
                        v.reciprocal(below[:, r], below[:, r]).then_inc(inverted, 1)
                        dve.wait_ge(inverted, j + 1)
                        need(dve, turned, j - 1)
                        v.tensor_tensor(attended[:, r].rearrange("p (h d) -> p h d", h=H),
                                        AGG[:, at(j), :, 0:DH].rearrange("p a h d -> p (a h) d"),
                                        below[:, r, :, None].to_broadcast([P, H, DH]), ALU.mult).then_inc(divided, 1)
                        v.tensor_scalar(rest[:, r], xin[:, at(j), :].rearrange("p a c -> p (a c)"),
                                        gate[:, 3:4], None, ALU.mult).then_inc(scaled, 1)
                        dve.wait_ge(multiplied, j + 1)
                        dve.wait_ge(scaled, j + 1)
                        v.scalar_tensor_tensor(Hs[:, at(j), :].rearrange("p a c -> p (a c)"), bank[2 + r][:, 0:D],
                                               gate[:, 2:3], rest[:, r], ALU.mult, ALU.add).then_inc(mixed, 1)
                        dve.wait_ge(mixed, j + 1)
                    tiles(dve, step)

                @block.tensor
                def _(pe):
                    pe.wait_ge(loaded, 32)

                    def step(j, r):
                        pe.wait_ge(divided, j + 1)
                        need(pe, kept, j - 1)
                        for h in range(KH):
                            last = nc.tensor.transpose(bank[r][:, h * P:h * P + P], attended[:, r, h * P:h * P + P],
                                                       ident[:, :])
                        last.then_inc(turned, 1)
                        pe.wait_ge(kept, j + 1)
                        need(pe, mixed, j - 1)
                        for h in range(KH):
                            last = nc.tensor.matmul(bank[2 + r][:, 0:D], xt[:, r, h, :], wa[:, h, :],
                                                    start=(h == 0), stop=(h == KH - 1))
                        last.then_inc(multiplied, 1)
                    tiles(pe, step)

        def attention_layer(layer, xin):
            with phase() as ph:
                weights = sb(f"t{layer}_weights", [P, KH, T2 + D], F32, ph)
                head_weights(f"t{layer}w", layer, weights)
                dense(f"t{layer}d", xin, weights, T2, table2, None)
            with phase() as ph:
                AGG = sb(f"t{layer}_AGG", [P, NT, H, HW], F32, ph)
                attend(f"t{layer}a", AGG)
                mix_layer(f"t{layer}m", layer, xin, AGG)

        prepare()
        conv_layer("c1", X, W1, self_w1, b1)
        relu_layer()
        conv_layer("c2", Hs, W2, self_w2, b2)
        norm("n1", X, OWN, False)
        attention_layer(0, X)
        attention_layer(1, Hs)
        norm("n2", X, Hs, True)


_INS = ['x', 'src', 'dst', 'edge_type_2', 'edge_type_8', 'L0_gnn_W1', 'L0_gnn_self_w1', 'L0_gnn_b1', 'L0_gnn_W2',
        'L0_gnn_self_w2', 'L0_gnn_b2', 'L1_gnn_Wk', 'L1_gnn_Wq', 'L1_gnn_Wv', 'L1_gnn_Wa', 'L1_gnn_Watt',
        'L1_gnn_Wmsg', 'L1_gnn_pri', 'L1_gnn_skip']


def kernel(**inputs):
    import numpy as _np
    import concourse.bacc as _bacc
    from concourse import mybir as _mybir
    from concourse.bass_utils import run_bass_kernel_spmd as _run

    nc = _bacc.Bacc("TRN2", target_bir_lowering=False, num_devices=1)
    arrays, args = {}, []
    for name in _INS:
        a = _np.ascontiguousarray(inputs[name])
        arrays[f"in_{name}_dram"] = a
        args.append(nc.dram_tensor(f"in_{name}_dram", a.shape, _mybir.dt.from_np(a.dtype), kind="ExternalInput").ap())
    shape = inputs["x"].shape
    args.append(nc.dram_tensor("out_0_dram", shape, _mybir.dt.float32, kind="ExternalOutput").ap())
    build(nc, *args)
    r = _run(nc, [arrays], core_ids=[0])
    return r.results[0]["out_0_dram"]
```

```python
from contextlib import ExitStack, contextmanager

import numpy as np
import concourse.bass as bass
from concourse import mybir

ALU = mybir.AluOpType
ACT = mybir.ActivationFunctionType
AX = mybir.AxisListType
F32 = mybir.dt.float32
I32 = mybir.dt.int32
STEPS = 2
STRANDS = 4
RING = 2 * STRANDS
BIG = 1e38
MAGIC = 1.5 * 2 ** 23
NO_NODE = 1 << 20


def ceil_div(a, b):
    return -(-a // b)


def need(eng, sem, value):
    if not isinstance(value, int) or value > 0:
        eng.wait_ge(sem, value)


def build(nc, x, src, dst, edge_type_2, edge_type_8, W1, self_w1, b1, W2, self_w2, b2,
          Wk, Wq, Wv, Wa, Watt, Wmsg, pri, skip, out):
    P = 128
    N, D = x.shape
    E = src.shape[0]
    R8 = W1.shape[0]
    H, R2, DH = Watt.shape[1], Watt.shape[2], Watt.shape[3]
    HW = DH + 1
    NT = ceil_div(N, P)
    LAST = N - (NT - 1) * P
    ET = ceil_div(E, P)
    NG = ceil_div((ET + NT - 1 + NT * (STEPS - 1)) // STEPS, RING) * RING
    NS = NG * STEPS
    KB = ceil_div(max(NS, ET + 1), P)
    ROUNDS = NG // RING
    LEN = NG // STRANDS
    ENDS = 2 * STRANDS
    KH = D // P
    T8, T2 = R8 * D, R2 * 2 * D
    FULL = E // (P * P)
    EPS = 1e-5

    edge_rows = nc.dram_tensor("edge_rows", (KB * P, 3 * P), F32).ap()
    step_nodes = nc.dram_tensor("step_nodes", (1 + KB * P, P), F32).ap()
    step_resets = nc.dram_tensor("step_resets", (1 + KB * P, P), F32).ap()
    step_tiles = nc.dram_tensor("step_tiles", (1, KB * P), I32).ap()
    table8 = nc.dram_tensor("table8", (NT * P * R8, D), F32).ap()
    table2 = nc.dram_tensor("table2", (NT * P * R2, 2 * D), F32).ap()

    top = ExitStack()

    def sb(name, shape, dt=F32, scope=top):
        return scope.enter_context(nc.sbuf_tensor(name, shape, dt))

    def sem(name):
        return nc.alloc_semaphore(name)

    @contextmanager
    def phase():
        earlier = nc.snapshot_sems()
        with ExitStack() as ph:
            yield ph
        nc.clear_and_free_semaphores(nc.allocated_since(earlier))
        nc.all_engine_barrier()

    with top:
        bank = [top.enter_context(nc.psum_tensor(f"bank{i}", [P, 512], F32)) for i in range(8)]
        X = sb("X", [P, NT, D])
        Hs = sb("Hs", [P, NT, D])
        OWN = sb("OWN", [P, NT, D])
        ident = sb("ident", [P, P])
        ones = sb("ones", [P, P])
        iota_free = sb("iota_free", [P, P])
        blockmask = sb("blockmask", [P, R2, DH])
        local = sb("local", [P, NS])
        index8 = sb("index8", [P, NS], I32)
        index2 = sb("index2", [P, NS], I32)
        group_tile = sb("group_tile", [P, STRANDS, LEN], I32)
        group_slot = sb("group_slot", [P, STRANDS, LEN], I32)
        first_local = sb("first_local", [P, LEN])
        still_first = sb("still_first", [P, LEN])
        end_node = sb("end_node", [P, 2, STRANDS])
        at_end = sb("at_end", [P, 2, STRANDS])

        def prepare():
            with phase() as ph:
                def s(name):
                    return sem("p_" + name)

                def t(name, shape, dt=F32):
                    return sb("p_" + name, shape, dt, ph)

                raw = t("raw", [P, 4, KB, P], I32)
                rows = t("rows", [P, KB, 3, P])
                below = t("below", [P, NT + 1])
                junk = t("junk", [P, KB, P])
                tiles_all = t("tiles_all", [P, NS], I32)
                tile_g = t("tile_g", [P, STRANDS, LEN])
                slot_g = t("slot_g", [P, STRANDS, LEN])
                first_tile = t("first_tile", [P, LEN])
                node_ok = t("node_ok", [P, LEN])
                end_tile = t("end_tile", [P, 2, STRANDS])
                total = t("total", [P, NT + 1])
                wk = t("wk", [P, 12, NT])
                one20 = t("one20", [P, NT])
                step_no = t("step_no", [P, KB])
                group_no = t("group_no", [P, KB])
                past = t("past", [P, KB, NT - 1])
                moved = t("moved", [P, KB, NT - 1])
                tile_f = t("tile_f", [P, KB])
                row_f = t("row_f", [P, KB])
                row_i = t("row_i", [P, KB], I32)
                tile_i = t("tile_i", [P, KB], I32)
                srow = t("srow", [P, KB, 3, P])
                inside = t("inside", [P, KB, P])
                inside2 = t("inside2", [P, KB, P])
                node = t("node", [P, KB, P])
                before = t("before", [P, KB, P])
                reset = t("reset", [P, KB, P])
                minus1 = t("minus1", [1, P])
                firstsel = t("firstsel", [P, P])
                blk = t("blk", [P, P])

                loaded, x_loaded, padded, made = s("loaded"), s("x_loaded"), s("padded"), s("made")
                chain, consts, counted = s("chain"), s("consts"), s("counted")
                rows_ready, rows_out, picked = s("rows_ready"), s("rows_out"), s("picked")
                got = [s(f"got{b}") for b in range(KB)]
                nodes_ready, nodes_out, shifted = s("nodes_ready"), s("nodes_out"), s("shifted")
                resets_ready, tiles_in = s("resets_ready"), s("tiles_in")
                turned, taken, first_made = s("turned"), s("taken"), s("first_made")
                tail_out, ends_in = s("tail_out"), s("ends_in")
                block = ph.enter_context(nc.Block())

                lists = (dst, src, edge_type_8, edge_type_2)
                tail_rows = E // P - FULL * P
                rest = E % P
                n_loads = 4 * (2 + (rest > 0))
                flat_nodes = step_nodes.rearrange("k e -> (k e)")

                @block.sync
                def _(sp):
                    sp.wait_ge(padded, 2)
                    for i, a in enumerate(lists):
                        whole = FULL * P * P
                        sp.dma_start(raw[:, i, 0:FULL, :],
                                     a[0:whole].rearrange("(b p e) -> p b e", p=P, e=P)).then_inc(loaded, 16)
                        sp.dma_start(raw[0:tail_rows, i, FULL, :],
                                     a[whole:whole + tail_rows * P].rearrange("(p e) -> p e", e=P)).then_inc(loaded, 16)
                        if rest:
                            sp.dma_start(raw[tail_rows:tail_rows + 1, i, FULL, 0:rest],
                                         a[E - rest:E].rearrange("(p e) -> p e", p=1)).then_inc(loaded, 16)
                    sp.dma_start(X[:, 0:NT - 1, :],
                                 x[0:(NT - 1) * P, :].rearrange("(j p) c -> p j c", p=P)).then_inc(x_loaded, 16)
                    sp.dma_start(X[0:LAST, NT - 1, :], x[(NT - 1) * P:N, :]).then_inc(x_loaded, 16)
                    sp.wait_ge(rows_ready, 1)
                    sp.dma_start(edge_rows.rearrange("(b p) c -> p b c", p=P),
                                 rows[:].rearrange("p b i e -> p b (i e)")).then_inc(rows_out, 16)
                    sp.wait_ge(nodes_ready, 1)
                    sp.dma_start(step_nodes[0:1, :], minus1[:, :]).then_inc(nodes_out, 16)
                    sp.dma_start(step_nodes[1:1 + KB * P, :].rearrange("(b p) e -> p b e", p=P),
                                 node[:]).then_inc(nodes_out, 16)
                    sp.wait_ge(nodes_out, 32)
                    sp.dma_start(before[:], flat_nodes[P - 1:P - 1 + KB * P * P].rearrange(
                        "(b p e) -> p b e", p=P, e=P)).then_inc(shifted, 16)
                    sp.dma_start(step_tiles[0, :].rearrange("(b p) -> p b", p=P), tile_i[:, :],
                                 allow_slow_non_contiguous=True).then_inc(tiles_in, 16)
                    sp.wait_ge(tiles_in, 16)
                    sp.dma_start(tiles_all[:, :], step_tiles[:, 0:NS].to_broadcast([P, NS])).then_inc(tiles_in, 16)
                    of_strands = flat_nodes[P:P + NS * P].rearrange("(c f) -> c f", c=STRANDS)
                    for k, edge in enumerate((0, NS * P // STRANDS - 1)):
                        sp.dma_start(end_node[:, k, :], of_strands[:, edge:edge + 1].rearrange("c o -> o c")
                                     .to_broadcast([P, STRANDS]), allow_slow_non_contiguous=True).then_inc(ends_in, 16)
                    sp.wait_ge(resets_ready, 1)
                    sp.dma_start(step_resets[0:KB * P, :].rearrange("(b p) e -> p b e", p=P),
                                 reset[:]).then_inc(tail_out, 16)
                    sp.dma_start(step_resets[KB * P:KB * P + 1, :], minus1[:, :]).then_inc(tail_out, 16)
                    sp.wait_ge(tail_out, 32)
                    sp.wait_ge(x_loaded, 32)

                @block.gpsimd
                def _(pool):
                    nc.gpsimd.iota(iota_free[:, :], pattern=[[1, P]], base=0, channel_multiplier=0,
                                   allow_small_or_imprecise_dtypes=True).then_inc(consts, 1)
                    nc.gpsimd.iota(step_no[:, :], pattern=[[P, KB]], base=0, channel_multiplier=1,
                                   allow_small_or_imprecise_dtypes=True).then_inc(consts, 1)
                    nc.gpsimd.memset(ident[:, :], 0.0).then_inc(made, 1)
                    nc.gpsimd.memset(firstsel[:, :], 0.0).then_inc(made, 1)
                    nc.gpsimd.iota(blk[:, 0:R2 * DH].rearrange("p (t h) -> p t h", t=R2),
                                   pattern=[[-DH, R2], [-DH * R2, DH]], base=0, channel_multiplier=1,
                                   allow_small_or_imprecise_dtypes=True).then_inc(consts, 1)
                    pool.wait_ge(made, 2)
                    nc.gpsimd.affine_select(out=ident[:, :], in_=ident[:, :], compare_op=ALU.not_equal, fill=1.0,
                                            base=0, pattern=[[-1, P]], channel_multiplier=1).then_inc(consts, 1)
                    nc.gpsimd.affine_select(out=firstsel[:, :], in_=firstsel[:, :], compare_op=ALU.not_equal,
                                            fill=1.0, base=0, pattern=[[0, P]],
                                            channel_multiplier=1).then_inc(consts, 1)
                    pool.wait_ge(rows_out, 16)
                    pool.wait_ge(picked, 1)
                    for b in range(KB):
                        nc.gpsimd.indirect_dma_start(
                            out=srow[:, b].rearrange("p i e -> p (i e)"), out_offset=None, in_=edge_rows,
                            in_offset=bass.IndirectOffsetOnAxis(ap=row_i[:, b:b + 1], axis=0)).then_inc(got[b], 16)

                @block.tensor
                def _(pe):
                    pe.wait_ge(counted, 1)
                    nc.tensor.matmul(bank[0][:, 0:NT + 1], ones[:, :], below[:, :], start=True,
                                     stop=True).then_inc(turned, 1)
                    pe.wait_ge(consts, 5)
                    pe.wait_ge(nodes_ready, 1)
                    for i in range(3):
                        for b in range(KB):
                            n = i * KB + b
                            if n >= 4:
                                pe.wait_ge(taken, n - 3)
                            nc.tensor.transpose(bank[1 + n % 4][:, 0:P], srow[:, b, i, :], ident[:, :]).then_inc(turned, 1)
                    pe.wait_ge(taken, KB)
                    nc.tensor.matmul(bank[5][:, 0:NG], firstsel[:, :],
                                     local[:, 0:NS].rearrange("p (g u) -> p g u", u=STEPS)[:, :, 0],
                                     start=True, stop=True).then_inc(first_made, 1)

                @block.vector
                def _(dve):
                    v = nc.vector
                    n = [0]

                    def link(ins):
                        n[0] += 1
                        ins.then_inc(chain, 1)
                        dve.wait_ge(chain, n[0])

                    v.memset(raw[:, :, FULL:KB, :], 0)
                    link(v.memset(X[:, NT - 1, :], 0.0))
                    v.memset(raw[:, 0, FULL:KB, :], NO_NODE).then_inc(padded, 1)
                    v.memset(ones[:, :], 1.0)
                    v.memset(below[:, 0:1], 0.0)
                    v.memset(minus1[:, :], -1.0)
                    v.memset(one20[:, :], 1.0).then_inc(padded, 1)
                    dve.wait_ge(padded, 2)
                    dve.wait_ge(loaded, 16 * n_loads)
                    v.tensor_copy(rows[:, :, 0, :], raw[:, 0])
                    v.scalar_tensor_tensor(rows[:, :, 1, :], raw[:, 1], float(R8), raw[:, 2], ALU.mult, ALU.add)
                    link(v.scalar_tensor_tensor(rows[:, :, 2, :], raw[:, 1], float(R2), raw[:, 3], ALU.mult, ALU.add))
                    v.sem_inc(rows_ready, 1)
                    for j in range(1, NT + 1):
                        link(v.tensor_scalar(junk[:], rows[:, :, 0, :], float(min(j * P, N)), 0.0, ALU.is_lt, ALU.add,
                                             accum_out=below[:, j:j + 1]))
                    v.sem_inc(counted, 1)
                    dve.wait_ge(turned, 1)
                    link(v.tensor_copy(total[:, :], bank[0][:, 0:NT + 1]))
                    lo, hi = total[:, 0:NT], total[:, 1:NT + 1]

                    def whole(o, i, step, shift):
                        link(v.tensor_scalar(o, i, 1.0 / step, (shift - (step - 1) / 2) / step, ALU.mult, ALU.add))
                        link(v.tensor_scalar(o, o, MAGIC, None, ALU.add))
                        link(v.tensor_scalar(o, o, -MAGIC, None, ALU.add))

                    first_row, last_row, some, count, groups, upto, offset = (wk[:, i, :] for i in range(7))
                    whole(first_row, lo, P, 0)
                    whole(last_row, hi, P, -1)
                    link(v.tensor_tensor(some, hi, lo, ALU.is_gt))
                    link(v.tensor_tensor(count, last_row, first_row, ALU.subtract))
                    link(v.scalar_tensor_tensor(count, count, 1.0, some, ALU.add, ALU.mult))
                    whole(groups, count, STEPS, STEPS - 1)
                    link(v.tensor_tensor_scan(upto, one20[:, :], groups, 0.0, ALU.mult, ALU.add))
                    link(v.tensor_tensor(offset, upto, groups, ALU.subtract))
                    link(v.scalar_tensor_tensor(offset, offset, -float(STEPS), first_row, ALU.mult, ALU.add))
                    link(v.tensor_tensor(wk[:, 7, 0:NT - 1], offset[:, 1:NT], offset[:, 0:NT - 1], ALU.subtract))
                    dve.wait_ge(consts, 5)
                    whole(group_no[:, :], step_no[:, :], STEPS, 0)
                    shape = [P, KB, NT - 1]
                    link(v.tensor_tensor(past[:], group_no[:, :, None].to_broadcast(shape),
                                         upto[:, None, 0:NT - 1].to_broadcast(shape), ALU.is_ge))
                    link(v.tensor_tensor(moved[:], past[:], wk[:, 7, None, 0:NT - 1].to_broadcast(shape), ALU.mult))
                    v.tensor_reduce(tile_f[:, :], past[:], AX.X, ALU.add)
                    link(v.tensor_reduce(row_f[:, :], moved[:], AX.X, ALU.add))
                    link(v.tensor_tensor(row_f[:, :], row_f[:, :], step_no[:, :], ALU.add))
                    link(v.tensor_scalar(row_f[:, :], row_f[:, :], offset[:, 0:1], float(ET), ALU.add, ALU.min))
                    v.tensor_copy(tile_i[:, :], tile_f[:, :])
                    v.tensor_copy(row_i[:, :], row_f[:, :]).then_inc(picked, 1)
                    bm = blk[:, 0:R2 * DH].rearrange("p (t h) -> p t h", t=R2)
                    link(v.tensor_scalar(blockmask[:], bm, -0.5, None, ALU.is_gt))
                    link(v.tensor_scalar(bm, bm, DH - 0.5, None, ALU.is_lt))
                    link(v.tensor_tensor(blockmask[:], blockmask[:], bm, ALU.mult))
                    for b in range(KB):
                        dve.wait_ge(got[b], 16)
                    link(v.tensor_scalar(tile_f[:, :], tile_f[:, :], float(P), None, ALU.mult))
                    for b in range(KB):
                        v.tensor_scalar(inside[:, b], srow[:, b, 0, :], tile_f[:, b:b + 1], None, ALU.subtract)
                    link(v.tensor_scalar(node[:], srow[:, :, 0, :], 1.0, None, ALU.add))
                    link(v.tensor_scalar(inside2[:], inside[:], float(P), None, ALU.is_lt))
                    link(v.scalar_tensor_tensor(inside2[:], inside[:], 0.0, inside2[:], ALU.is_ge, ALU.mult))
                    link(v.tensor_tensor(node[:], node[:], inside2[:], ALU.mult))
                    link(v.tensor_scalar(node[:], node[:], -1.0, None, ALU.add))
                    link(v.tensor_copy(srow[:, :, 0, :], inside[:]))
                    v.sem_inc(nodes_ready, 1)
                    dve.wait_ge(shifted, 16)
                    link(v.tensor_tensor(reset[:], node[:], before[:], ALU.not_equal))
                    v.tensor_scalar(reset[:], reset[:], -BIG, None, ALU.mult).then_inc(resets_ready, 1)
                    for i in range(3):
                        for b in range(KB):
                            k = i * KB + b
                            w = min(P, NS - b * P)
                            dve.wait_ge(turned, 2 + k)
                            dest = (local, index8, index2)[i]
                            v.tensor_copy(dest[:, b * P:b * P + w], bank[1 + k % 4][:, 0:w]).then_inc(taken, 1)
                    dve.wait_ge(first_made, 1)
                    for c in range(STRANDS):
                        on = slice(c * H, (c + 1) * H)
                        v.tensor_copy(first_local[on, :], bank[5][on, c * LEN:(c + 1) * LEN]).then_inc(chain, 1)
                    n[0] += STRANDS
                    dve.wait_ge(tiles_in, 32)
                    link(v.tensor_copy(tile_g[:], tiles_all[:].rearrange("p (c g u) -> p c g u", c=STRANDS, u=STEPS)[:, :, :, 0]))
                    for c in range(STRANDS):
                        on = slice(c * H, (c + 1) * H)
                        v.tensor_copy(first_tile[on, :], tile_g[on, c, :])
                        if c:
                            v.tensor_scalar(slot_g[:, c], tile_g[:, c], tile_g[:, c, 0:1], None, ALU.is_equal)
                        else:
                            v.memset(slot_g[:, c], 0.0)
                        for k, g in enumerate((0, LEN - 1)):
                            ins = v.tensor_copy(end_tile[:, k, c:c + 1], tile_g[:, c, g:g + 1])
                    link(ins)
                    for c in range(1, STRANDS):
                        link(v.tensor_scalar(node[:, c, 0:LEN], tile_g[:, c], -1.0, float(NT - 1 + c), ALU.mult, ALU.add))
                        link(v.tensor_tensor(slot_g[:, c], slot_g[:, c], node[:, c, 0:LEN], ALU.mult))
                    link(v.tensor_tensor(slot_g[:], slot_g[:], tile_g[:], ALU.add))
                    v.tensor_copy(group_slot[:], slot_g[:])
                    v.tensor_copy(group_tile[:], tile_g[:])
                    link(v.tensor_scalar(node_ok[:, :], first_local[:, :], float(P), None, ALU.is_lt))
                    link(v.scalar_tensor_tensor(node_ok[:, :], first_local[:, :], 0.0, node_ok[:, :], ALU.is_ge, ALU.mult))
                    link(v.scalar_tensor_tensor(first_tile[:, :], first_tile[:, :], float(P), first_local[:, :],
                                                ALU.mult, ALU.add))
                    link(v.scalar_tensor_tensor(first_tile[:, :], first_tile[:, :], 1.0, node_ok[:, :], ALU.add, ALU.mult))
                    link(v.tensor_scalar(still_first[:, :], first_tile[:, :], first_tile[:, 0:1], None, ALU.is_equal))
                    link(v.tensor_scalar(still_first[:, :], still_first[:, :], -1.0, BIG, ALU.add, ALU.mult))
                    dve.wait_ge(ends_in, 32)
                    link(v.scalar_tensor_tensor(at_end[:], end_tile[:], -float(P), end_node[:], ALU.mult, ALU.add))
                    link(v.tensor_scalar(at_end[:], at_end[:], step_no[:, 0:1], None, ALU.is_equal))
                    link(v.tensor_tensor(end_tile[:, 0], end_node[:, 0], end_node[:, 1], ALU.not_equal))
                    v.tensor_tensor(at_end[:, 1], at_end[:, 1], end_tile[:, 0], ALU.mult)

        def over_tiles(eng, step, early=0):
            for j in range(-early, 2):
                step(j, j % 2)
            with eng.Fori(1, NT // 2 - 1) as i:
                step(i * 2, 0)
                step(i * 2 + 1, 1)
            for j in (NT - 2, NT - 1):
                step(j, j % 2)

        def is_tile(j):
            return not isinstance(j, int) or 0 <= j < NT

        def at(j):
            return slice(j, j + 1) if isinstance(j, int) else bass.ds(j, 1)

        def dense(tag, xin, weights, n_table, table, bias):
            with phase() as ph:
                def s(name):
                    return sem(f"{tag}_{name}")

                xs = sb(f"{tag}_xs", [P, 2, D], F32, ph)
                xt = sb(f"{tag}_xt", [P, 2, KH, P], F32, ph)
                stage = sb(f"{tag}_stage", [P, 2, n_table], F32, ph)
                copied, turned, kept = s("copied"), s("turned"), s("kept")
                multiplied, act_took, dve_took = s("multiplied"), s("act_took"), s("dve_took")
                stored = [s("stored0"), s("stored1")]
                NCH = n_table // 512
                act_chunks = [c for c in range(NCH) if c % 2 == 0]
                dve_chunks = [c for c in range(NCH) if c % 2 == 1]
                rows_out = table.rearrange("(j p r) c -> p j (r c)", p=P, r=n_table // table.shape[1])
                block = ph.enter_context(nc.Block())

                @block.vector
                def _(dve):
                    def step(j, r):
                        if is_tile(j + 2):
                            need(dve, turned, j + 1)
                            nc.vector.tensor_copy(xs[:, r, :], xin[:, at(j + 2), :].rearrange("p a c -> p (a c)")).then_inc(copied, 1)
                        if is_tile(j):
                            for k, c in enumerate(dve_chunks):
                                dve.wait_ge(multiplied, j * (NCH + 1) + c + 1)
                                if k == 0 and (not isinstance(j, int) or j >= 2):
                                    dve.wait_ge(stored[r], (j - r) * 8)
                                nc.vector.tensor_copy(stage[:, r, c * 512:c * 512 + 512], bank[c][:, :]).then_inc(dve_took, 1)
                            dve.wait_ge(multiplied, j * (NCH + 1) + NCH + 1)
                            own = OWN[:, at(j), :].rearrange("p a c -> p (a c)")
                            if bias is None:
                                nc.vector.tensor_copy(own, bank[NCH][:, 0:D]).then_inc(dve_took, 1)
                            else:
                                nc.vector.tensor_tensor(own, bank[NCH][:, 0:D], bias[:, :], ALU.add).then_inc(dve_took, 1)
                    over_tiles(dve, step, early=2)

                @block.tensor
                def _(pe):
                    def step(j, r):
                        if is_tile(j + 1):
                            pe.wait_ge(copied, j + 2)
                            need(pe, kept, j)
                            for h in range(KH):
                                last = nc.tensor.transpose(bank[7 - r][:, h * P:h * P + P],
                                                           xs[:, 1 - r, h * P:h * P + P], ident[:, :])
                            last.then_inc(turned, 1)
                        if is_tile(j):
                            pe.wait_ge(kept, j + 1)
                            for c in range(NCH + 1):
                                w = 512 if c < NCH else D
                                if c in act_chunks:
                                    need(pe, act_took, (j - 1) * len(act_chunks) + c // 2 + 1)
                                else:
                                    need(pe, dve_took, (j - 1) * (len(dve_chunks) + 1)
                                         + (c // 2 if c < NCH else len(dve_chunks)) + 1)
                                for h in range(KH):
                                    last = nc.tensor.matmul(bank[c][:, 0:w], xt[:, r, h, :],
                                                            weights[:, h, c * 512:c * 512 + w],
                                                            start=(h == 0), stop=(h == KH - 1))
                                last.then_inc(multiplied, 1)
                    over_tiles(pe, step, early=1)

                @block.scalar
                def _(act):
                    def step(j, r):
                        if is_tile(j + 1):
                            act.wait_ge(turned, j + 2)
                            need(act, multiplied, j * (NCH + 1))
                            nc.scalar.copy(xt[:, 1 - r].rearrange("p h n -> p (h n)"), bank[7 - r][:, 0:D]).then_inc(kept, 1)
                        if is_tile(j):
                            for k, c in enumerate(act_chunks):
                                act.wait_ge(multiplied, j * (NCH + 1) + c + 1)
                                if k == 0 and (not isinstance(j, int) or j >= 2):
                                    act.wait_ge(stored[r], (j - r) * 8)
                                nc.scalar.copy(stage[:, r, c * 512:c * 512 + 512], bank[c][:, :]).then_inc(act_took, 1)
                    over_tiles(act, step, early=1)

                @block.sync
                def _(sp):
                    def step(j, r):
                        sp.wait_ge(act_took, (j + 1) * len(act_chunks))
                        sp.wait_ge(dve_took, j * (len(dve_chunks) + 1) + len(dve_chunks))
                        sp.dma_start(rows_out[:, at(j), :], stage[:, r:r + 1, :]).then_inc(stored[r], 16)
                    over_tiles(sp, step)
                    sp.wait_ge(stored[0], 16 * (NT // 2))
                    sp.wait_ge(stored[1], 16 * (NT // 2))

        class Unit:

            def __init__(self, i, r):
                self.i, self.r, self.c = i, r, r % STRANDS
                self.n = i * RING + r
                self.w = i * (RING // STRANDS) + r // STRANDS
                self.slot = r % RING
                self.turn = (r // STRANDS) % 2
                self.fills = i + r // RING + 1
                self.fixed = isinstance(i, int)
                self.exists = not self.fixed or 0 <= self.n < NG

            def shift(self, lag):
                return Unit(self.i, self.r + lag)

            def steps(self, columns):
                start = self.w * STEPS
                strand = columns.rearrange("p (c s) -> p c s", c=STRANDS)[:, self.c, :]
                return strand[:, start:start + STEPS] if self.fixed else strand[:, bass.ds(start, STEPS)]

            def group(self, columns):
                return columns[:, self.w:self.w + 1] if self.fixed else columns[:, bass.ds(self.w, 1)]

            def place(self, eng, table, limit):
                entry = table[0:1, self.c, self.w:self.w + 1] if self.fixed else table[0:1, self.c, bass.ds(self.w, 1)]
                return bass.ds(eng.value_load(entry, min_val=0, max_val=limit - 1), 1)

        def over_units(eng, step, early=0, late=0):
            for r in range(-early, RING):
                step(Unit(0, r))
            with eng.Fori(1, ROUNDS - 1) as i:
                for r in range(RING):
                    step(Unit(i, r))
            for r in range(RING + late):
                step(Unit(ROUNDS - 1, r))

        def gather_rows(pool, pace, index, index_now, index_ready, table, rows, width, arrived, freed, read,
                        afterwards=None, late=0):
            def step(U):
                if U.exists:
                    gather(U)
                if afterwards:
                    afterwards(U)

            def gather(U):
                if U.c == 0:
                    if not U.fixed or U.n >= RING:
                        pool.wait_ge(read, U.n - STRANDS)
                        nc.gpsimd.sem_inc(pace, 1)
                    every = index[:, :].rearrange("p (c s) -> p c s", c=STRANDS)
                    start = U.w * STEPS
                    now = every[:, :, start:start + STEPS] if U.fixed else every[:, :, bass.ds(start, STEPS)]
                    nc.gpsimd.tensor_copy(index_now[:, U.turn], now).then_inc(index_ready, 1)
                    pool.wait_ge(index_ready, U.w + 1)
                    nc.gpsimd.sem_inc(pace, 1)
                if not U.fixed or U.n >= RING:
                    pool.wait_ge(freed, U.n - RING + 1)
                    nc.gpsimd.sem_inc(pace, 1)
                for u in range(STEPS):
                    nc.gpsimd.indirect_dma_start(
                        out=rows[:, U.slot, u, 0:width], out_offset=None, in_=table,
                        in_offset=bass.IndirectOffsetOnAxis(ap=index_now[:, U.turn, U.c, u:u + 1], axis=0)
                    ).then_inc(arrived[U.slot][u], 16)
            over_units(pool, step, late=late)

        def write_onehot(onehot, U, ready):
            shape = [P, STEPS, P]
            nc.vector.tensor_tensor(onehot[:, U.slot], iota_free[:, None, :].to_broadcast(shape),
                                    U.steps(local[:, :])[:, :, None].to_broadcast(shape),
                                    ALU.is_equal).then_inc(ready, 1)

        def convolve(tag):
            with phase() as ph:
                def s(name):
                    return sem(f"{tag}_{name}")

                rows = sb(f"{tag}_rows", [P, RING, STEPS, D], F32, ph)
                onehot = sb(f"{tag}_onehot", [P, RING, STEPS, P], F32, ph)
                index_now = sb(f"{tag}_index", [P, 2, STRANDS, STEPS], I32, ph)
                pace, index_ready = s("pace"), s("index_ready")
                arrived = [[s(f"arrived{r}_{u}") for u in range(STEPS)] for r in range(RING)]
                onehot_ready, summed, added = s("onehot_ready"), s("summed"), s("added")
                block = ph.enter_context(nc.Block())

                @block.gpsimd
                def _(pool):
                    gather_rows(pool, pace, index8, index_now, index_ready, table8, rows, D, arrived, summed, summed)

                @block.vector
                def _(dve):
                    def step(U):
                        ahead, behind = U.shift(1), U.shift(-1)
                        if ahead.exists:
                            need(dve, summed, ahead.n - RING + 1)
                            write_onehot(onehot, ahead, onehot_ready)
                        if behind.exists:
                            own = OWN[:, behind.place(dve, group_tile, NT), :].rearrange("p a c -> p (a c)")
                            dve.wait_ge(summed, U.n)
                            need(dve, added, U.n - 1)
                            nc.vector.tensor_tensor(own, own, bank[(U.slot - 1) % 2][:, 0:D], ALU.add).then_inc(added, 1)
                    over_units(dve, step, early=1, late=1)

                @block.tensor
                def _(pe):
                    def step(U):
                        pe.wait_ge(onehot_ready, U.n + 1)
                        need(pe, added, U.n - 1)
                        for u in range(STEPS):
                            pe.wait_ge(arrived[U.slot][u], U.fills * 16)
                            last = nc.tensor.matmul(bank[U.slot % 2][:, 0:D], onehot[:, U.slot, u, :],
                                                    rows[:, U.slot, u, :], start=(u == 0), stop=(u == STEPS - 1))
                        last.then_inc(summed, 1)
                    over_units(pe, step)

        def attend(tag, AGG, first_guard, last_guard):
            with phase() as ph:
                def s(name):
                    return sem(f"{tag}_{name}")

                def t(name, shape, dt=F32):
                    return sb(f"{tag}_{name}", shape, dt, ph)

                EDGES = STEPS * P
                rows = t("rows", [P, RING, STEPS, 2 * D])
                onehot = t("onehot", [P, RING, STEPS, P])
                turned_onehot = t("turned_onehot", [P, 2, STEPS, P])
                index_now = t("index", [P, 2, STRANDS, STEPS], I32)
                resets = t("resets", [P, 2, EDGES + 1])
                scores = t("scores", [P, 2, STEPS, STRANDS, H])
                forth = t("forth", [P, 2, EDGES])
                guard = t("guard", [P, 2, EDGES])
                change = t("change", [P, 2])
                factor = t("factor", [P, 2])
                minus_one = t("minus_one", [P, 1])
                minus_ident = t("minus_ident", [P, P])
                off_pick = t("off_pick", [P, 2, P])
                pick = t("pick", [P, 2, P])
                spread = t("spread", [P, 2, P])
                factors = t("factors", [P, 2, P])
                distance = t("distance", [P, STEPS, P])
                weighted = t("weighted", [P, 2, STRANDS, STEPS, H, HW])
                pace, index_ready = s("pace"), s("index_ready")
                arrived = [[s(f"arrived{r}_{u}") for u in range(STEPS)] for r in range(RING)]
                resets_in = [s(f"resets_in{r}") for r in range(2)]
                onehot_ready, onehot_turned, onehot_kept = s("onehot_ready"), s("onehot_turned"), s("onehot_kept")
                queried, multiplied, scored = s("queried"), s("multiplied"), s("scored")
                messages_ready, summed, scaled, added = s("messages_ready"), s("summed"), s("scaled"), s("added")
                vector_scaled = s("vector_scaled")
                scores_turned, forth_ready, guard_ready = s("scores_turned"), s("forth_ready"), s("guard_ready")
                scores_moved, guard_turned, weights_ready = s("scores_moved"), s("guard_turned"), s("weights_ready")
                change_ready, factor_ready, pick_ready, factor_spread, factors_kept = (
                    s("change_ready"), s("factor_ready"), s("pick_ready"), s("factor_spread"), s("factors_kept"))
                distance_ready, off_pick_ready, less_ready, spread_ready = (
                    s("distance_ready"), s("off_pick_ready"), s("less_ready"), s("spread_ready"))
                first_guarded, cleared = s("first_guarded"), s("cleared")
                block = ph.enter_context(nc.Block())

                q_bank, sum_bank = (bank[0], bank[1]), (bank[5], bank[6])
                onehot_bank, score_bank, guard_bank, factor_bank = bank[2], bank[3], bank[4], bank[7]
                flat_resets = step_resets.rearrange("k e -> (k e)").rearrange("(o n) -> o n", o=1)
                FREE = STRANDS - 1
                VECTOR_SCALES = (STRANDS - 1,)
                SCALE_LAG = RING - 1
                LAG = STRANDS

                @block.sync
                def _(sp):
                    def step(U):
                        if U.c == 0:
                            need(sp, guard_ready, U.w - 1)
                            for c in range(STRANDS):
                                start = (U.w + c * LEN) * EDGES
                                part = slice(start, start + EDGES + 1) if U.fixed else bass.ds(start, EDGES + 1)
                                sp.dma_start(resets[c * H:(c + 1) * H, U.turn, :],
                                             flat_resets[:, part].to_broadcast([H, EDGES + 1])).then_inc(resets_in[U.turn], 16)
                    over_units(sp, step)

                @block.gpsimd
                def _(pool):
                    def scale_down(U):
                        done = U.shift(-SCALE_LAG)
                        if not done.exists or done.c in VECTOR_SCALES:
                            return
                        agg = AGG[:, done.place(pool, group_slot, NT + STRANDS - 1)].rearrange("p a h w -> p (a h) w")
                        pool.wait_ge(factors_kept, done.w + 1)
                        pool.wait_ge(added, FREE + done.n - STRANDS + 1)
                        nc.gpsimd.sem_inc(pace, 1)
                        fac = factors[:, done.turn, done.c * H:(done.c + 1) * H]
                        nc.gpsimd.tensor_tensor(agg, agg, fac[:, :, None].to_broadcast([P, H, HW]),
                                                ALU.mult).then_inc(scaled, 1)

                    gather_rows(pool, pace, index2, index_now, index_ready, table2, rows, 2 * D,
                                arrived, messages_ready, multiplied, scale_down, late=SCALE_LAG)

                @block.vector
                def _(dve):
                    v = nc.vector
                    v.memset(minus_one[:, :], -1.0)
                    v.tensor_scalar(minus_ident[:, :], ident[:, :], -1.0, None, ALU.mult)
                    v.memset(forth[:, 1, :], -BIG)
                    v.memset(guard[:, 1, :], -BIG)
                    v.memset(first_guard[:, :], -BIG)
                    v.memset(AGG[:], 0.0).then_inc(cleared, 1)
                    dve.wait_ge(cleared, 1)
                    v.sem_inc(added, FREE)

                    def step(U):
                        late, done = U.shift(-LAG), U.shift(-LAG - 2)
                        t, o = U.turn, 1 - U.turn
                        if U.exists:
                            dve.wait_ge(queried, U.n + 1)
                            for u in range(STEPS):
                                dve.wait_ge(arrived[U.slot][u], U.fills * 16)
                            v.tensor_tensor(rows[:, U.slot, :, 0:D], rows[:, U.slot, :, 0:D],
                                            q_bank[U.r % 2][:, :].rearrange("p (u c) -> p u c", u=STEPS),
                                            ALU.mult).then_inc(multiplied, 1)
                        if done.exists:
                            agg = AGG[:, done.place(dve, group_slot, NT + STRANDS - 1)].rearrange("p a h w -> p (a h) w")
                        if U.c == 0 and late.exists:
                            dve.wait_ge(guard_ready, U.w)
                            need(dve, first_guarded, U.w - 1)
                            v.scalar_tensor_tensor(first_guard[:, :], guard[:, o, 0:1], late.group(still_first[:, :]),
                                                   first_guard[:, :], ALU.add, ALU.max).then_inc(first_guarded, 1)
                        if done.exists and done.c in VECTOR_SCALES:
                            dve.wait_ge(factors_kept, done.w + 1)
                            need(dve, added, done.n - 1)
                            fac = factors[:, done.turn, done.c * H:(done.c + 1) * H]
                            v.tensor_tensor(agg, agg, fac[:, :, None].to_broadcast([P, H, HW]),
                                            ALU.mult).then_inc(vector_scaled, 1)
                        if U.exists:
                            dve.wait_ge(multiplied, U.n + 1)
                            need(dve, scores_moved, U.w - 1)
                            v.tensor_reduce(scores[:, t, :, U.c, :],
                                            rows[:, U.slot, :, 0:D].rearrange("p u (h d) -> p u h d", h=H),
                                            AX.X, ALU.add).then_inc(scored, 1)
                        if done.exists:
                            if done.c in VECTOR_SCALES:
                                dve.wait_ge(vector_scaled, done.w + 1)
                            else:
                                dve.wait_ge(scaled, done.w * (STRANDS - 1) + done.c + 1)
                            dve.wait_ge(summed, done.n + 1)
                            v.tensor_tensor(agg, agg, sum_bank[done.r % 2][:, 0:H * HW].rearrange("p (h w) -> p h w", h=H),
                                            ALU.add).then_inc(added, 1)
                        if late.exists:
                            dve.wait_ge(weights_ready, late.w + 1)
                            into = weighted[:, late.turn, late.c]
                            v.tensor_tensor(into[:, :, :, 0:DH],
                                            rows[:, late.slot, :, D:2 * D].rearrange("p u (h d) -> p u h d", h=H),
                                            into[:, :, :, DH:HW].to_broadcast([P, STEPS, H, DH]),
                                            ALU.mult).then_inc(messages_ready, 1)
                        if U.c == STRANDS - 1 and U.exists:
                            dve.wait_ge(resets_in[t], (U.fills * 16 * STRANDS))
                            dve.wait_ge(scores_turned, U.w + 1)
                            need(dve, forth_ready, U.w)
                            need(dve, guard_ready, U.w)
                            v.tensor_tensor_scan(forth[:, t, :], resets[:, t, 0:EDGES], score_bank[:, 0:EDGES],
                                                 forth[:, o, EDGES - 1:EDGES], ALU.add, ALU.max).then_inc(forth_ready, 1)
                            dve.wait_ge(forth_ready, U.w + 1)
                            need(dve, guard_turned, U.w - 1)
                            need(dve, change_ready, U.w)
                            v.tensor_tensor_scan(guard[:, t, ::-1], resets[:, t, EDGES:0:-1], forth[:, t, ::-1],
                                                 -BIG, ALU.add, ALU.max).then_inc(guard_ready, 1)
                    over_units(dve, step, late=LAG + 2)
                    v.tensor_copy(last_guard[:, :], guard[:, (LEN - 1) % 2, EDGES - 1:EDGES])

                @block.tensor
                def _(pe):
                    pe.wait_ge(cleared, 1)

                    def step(U):
                        following, ahead, late = U.shift(1), U.shift(2), U.shift(-LAG - 1)
                        t, o = U.turn, 1 - U.turn
                        if following.exists:
                            query = OWN[:, following.place(pe, group_tile, NT), :].rearrange("p a c -> p (a c)")
                            pe.wait_ge(onehot_kept, following.n + 1)
                            need(pe, multiplied, following.n - 1)
                            for u in range(STEPS):
                                last = nc.tensor.matmul(q_bank[following.r % 2][:, u * D:u * D + D],
                                                        turned_onehot[:, following.r % 2, u, :], query,
                                                        start=True, stop=True)
                            last.then_inc(queried, 1)
                        if ahead.exists:
                            pe.wait_ge(onehot_ready, ahead.n + 1)
                            need(pe, onehot_kept, ahead.n)
                            for u in range(STEPS):
                                last = nc.tensor.transpose(onehot_bank[:, u * P:u * P + P],
                                                           onehot[:, ahead.slot, u, :], ident[:, :])
                            last.then_inc(onehot_turned, 1)
                        if U.c == 0 and U.shift(-LAG).exists:
                            pe.wait_ge(guard_ready, U.w)
                            for u in range(STEPS):
                                last = nc.tensor.matmul(guard_bank[:, u * P:u * P + P], guard[:, o, u * P:u * P + P],
                                                        minus_ident[:, :], start=False, stop=(u == STEPS - 1))
                            last.then_inc(guard_turned, 1)
                        if U.c == 0 and U.shift(-LAG).exists:
                            pe.wait_ge(pick_ready, U.w)
                            pe.wait_ge(spread_ready, U.w)
                            need(pe, factors_kept, U.w - 1)
                            nc.tensor.matmul(factor_bank[:, 0:P], pick[:, o, :], spread[:, o, :],
                                             start=True, stop=True).then_inc(factor_spread, 1)
                        if late.exists:
                            pe.wait_ge(messages_ready, late.n + 1)
                            pe.wait_ge(added, FREE + late.n - 1)
                            for u in range(STEPS):
                                last = nc.tensor.matmul(sum_bank[late.r % 2][:, 0:H * HW], onehot[:, late.slot, u, :],
                                                        weighted[:, late.turn, late.c, u].rearrange("p h w -> p (h w)"),
                                                        start=(u == 0), stop=(u == STEPS - 1))
                            last.then_inc(summed, 1)
                        if U.c == STRANDS - 1 and U.exists:
                            pe.wait_ge(scored, U.n + 1)
                            need(pe, forth_ready, U.w)
                            for u in range(STEPS):
                                last = nc.tensor.transpose(score_bank[:, u * P:u * P + P],
                                                           scores[:, t, u].rearrange("p c h -> p (c h)"), ident[:, :])
                            last.then_inc(scores_turned, 1)
                            need(pe, weights_ready, U.w)
                            for u in range(STEPS):
                                last = nc.tensor.matmul(guard_bank[:, u * P:u * P + P], ident[:, :],
                                                        scores[:, t, u].rearrange("p c h -> p (c h)"),
                                                        start=(u == 0), stop=False)
                            last.then_inc(scores_moved, 1)
                    over_units(pe, step, early=2, late=LAG + 1)

                @block.scalar
                def _(act):
                    act.wait_ge(cleared, 1)

                    def step(U):
                        ahead, far = U.shift(2), U.shift(3)
                        t, o = U.turn, 1 - U.turn
                        if U.c == 0 and U.shift(-LAG).exists:
                            act.wait_ge(guard_turned, U.w)
                            need(act, summed, U.n - 2 * STRANDS)
                            nc.scalar.activation(weighted[:, o, :, :, :, DH],
                                                 guard_bank[:, 0:STEPS * P].rearrange(
                                                     "p (u c h) -> p c u h", u=STEPS, c=STRANDS),
                                                 ACT.Exp).then_inc(weights_ready, 1)
                        if ahead.exists:
                            act.wait_ge(onehot_turned, ahead.n + 1)
                            need(act, queried, ahead.n - 1)
                            nc.scalar.copy(turned_onehot[:, ahead.r % 2].rearrange("p u n -> p (u n)"),
                                           onehot_bank[:, 0:STEPS * P]).then_inc(onehot_kept, 1)
                        if U.c == 0 and U.shift(-LAG).exists:
                            act.wait_ge(factor_spread, U.w)
                            need(act, scaled, (U.w - 2) * (STRANDS - 1))
                            need(act, vector_scaled, U.w - 2)
                            nc.scalar.activation(factors[:, o, :], factor_bank[:, 0:P], ACT.Identity,
                                                 bias=1.0).then_inc(factors_kept, 1)
                        if far.exists:
                            need(act, onehot_ready, far.n)
                            for u in range(STEPS):
                                last = nc.scalar.activation(distance[:, u, :], iota_free[:, :], ACT.Abs,
                                                            bias=far.steps(local[:, :])[:, u:u + 1], scale=-1.0)
                            last.then_inc(distance_ready, 1)
                            act.wait_ge(distance_ready, far.n + 1)
                            need(act, summed, far.n - RING + 1)
                            nc.scalar.activation(onehot[:, far.slot].rearrange("p u n -> p (u n)"),
                                                 distance[:].rearrange("p u n -> p (u n)"), ACT.Relu,
                                                 bias=1.0, scale=-1.0).then_inc(onehot_ready, 1)
                        if U.c == STRANDS - 1 and U.exists:
                            act.wait_ge(guard_ready, U.w + 1)
                            nc.scalar.activation(change[:, t:t + 1], guard[:, o, EDGES - 1:EDGES], ACT.Relu,
                                                 bias=guard[:, t, 0:1], scale=-1.0).then_inc(change_ready, 1)
                            act.wait_ge(change_ready, U.w + 1)
                            nc.scalar.activation(factor[:, t:t + 1], change[:, t:t + 1], ACT.Exp,
                                                 scale=-1.0).then_inc(factor_ready, 1)
                            nc.scalar.activation(off_pick[:, t, :], iota_free[:, :], ACT.Abs,
                                                 bias=U.group(first_local[:, :]), scale=-1.0).then_inc(off_pick_ready, 1)
                            act.wait_ge(factor_ready, U.w + 1)
                            nc.scalar.activation(factor[:, t:t + 1], factor[:, t:t + 1], ACT.Identity,
                                                 bias=minus_one[:, 0:1]).then_inc(less_ready, 1)
                            act.wait_ge(off_pick_ready, U.w + 1)
                            need(act, factor_spread, U.w - 1)
                            nc.scalar.activation(pick[:, t, :], off_pick[:, t, :], ACT.Relu,
                                                 bias=1.0, scale=-1.0).then_inc(pick_ready, 1)
                            act.wait_ge(less_ready, U.w + 1)
                            nc.scalar.activation(spread[:, t, :], ident[:, :], ACT.Copy,
                                                 scale=factor[:, t:t + 1]).then_inc(spread_ready, 1)
                    over_units(act, step, early=3, late=LAG)

        def merge(tag, AGG, first_guard, last_guard):
            with phase() as ph:
                def t(name, shape, dt=F32):
                    return sb(f"{tag}_{name}", shape, dt, ph)

                diag = t("diag", [P, 2, P])
                guards = t("guards", [P, ENDS, H])
                same = t("same", [P, ENDS, ENDS])
                shared = t("shared", [P, ENDS, H, ENDS])
                most = t("most", [P, ENDS, H])
                factor = t("factor", [P, ENDS, H])
                chain, diag_ready, turned, less_ready, exp_ready = (
                    sem(f"{tag}_{k}") for k in ("chain", "diag_ready", "turned", "less_ready", "exp_ready"))
                block = ph.enter_context(nc.Block())

                @block.tensor
                def _(pe):
                    pe.wait_ge(diag_ready, 2)
                    for k in range(2):
                        last = nc.tensor.matmul(bank[0][:, k * P:(k + 1) * P], ones[:, :], diag[:, k, :],
                                                start=True, stop=True)
                    last.then_inc(turned, 1)

                @block.scalar
                def _(act):
                    act.wait_ge(less_ready, 1)
                    nc.scalar.activation(factor[:], most[:], ACT.Exp).then_inc(exp_ready, 1)

                @block.vector
                def _(dve):
                    v = nc.vector
                    n = [0]

                    def link(ins):
                        n[0] += 1
                        ins.then_inc(chain, 1)
                        dve.wait_ge(chain, n[0])

                    v.tensor_scalar(diag[:, 0, :], ident[:, :], first_guard[:, 0:1], None, ALU.mult).then_inc(diag_ready, 1)
                    v.tensor_scalar(diag[:, 1, :], ident[:, :], last_guard[:, 0:1], None, ALU.mult).then_inc(diag_ready, 1)
                    ids = end_node[:].rearrange("p k c -> p (k c)")
                    link(v.tensor_tensor(same[:], ids[:, :, None].to_broadcast([P, ENDS, ENDS]),
                                         ids[:, None, :].to_broadcast([P, ENDS, ENDS]), ALU.is_equal))
                    link(v.tensor_scalar(same[:], same[:], -1.0, BIG, ALU.add, ALU.mult))
                    dve.wait_ge(turned, 1)
                    link(v.tensor_copy(guards[:].rearrange("p a h -> p (a h)"), bank[0][:, 0:ENDS * H]))
                    for a in range(ENDS):
                        link(v.tensor_tensor(shared[:, a], guards[:].rearrange("p b h -> p h b"),
                                             same[:, a, None, :].to_broadcast([P, H, ENDS]), ALU.add))
                    link(v.tensor_reduce(most[:], shared[:], AX.X, ALU.max))
                    link(v.tensor_tensor(most[:], guards[:], most[:], ALU.subtract))
                    v.tensor_scalar(most[:], most[:], 0.0, None, ALU.min).then_inc(less_ready, 1)
                    dve.wait_ge(exp_ready, 1)
                    link(v.tensor_scalar(factor[:], factor[:], -1.0, None, ALU.add))
                    link(v.tensor_tensor(factor[:], factor[:], at_end[:].rearrange("p k c -> p (k c)")[:, :, None]
                                         .to_broadcast([P, ENDS, H]), ALU.mult))
                    for k in range(2):
                        for c in range(STRANDS):
                            g = (0, LEN - 1)[k]
                            slot = bass.ds(dve.value_load(group_slot[0:1, c, g:g + 1], min_val=0,
                                                          max_val=NT + STRANDS - 2), 1)
                            agg = AGG[:, slot].rearrange("p a h w -> p (a h) w")
                            link(v.scalar_tensor_tensor(agg, factor[:, k * STRANDS + c, :, None].to_broadcast([P, H, HW]),
                                                        1.0, agg, ALU.add, ALU.mult))
                    for c in range(1, STRANDS):
                        tile = bass.ds(dve.value_load(group_tile[0:1, c, 0:1], min_val=0, max_val=NT - 1), 1)
                        agg = AGG[:, tile].rearrange("p a h w -> p (a h w)")
                        link(v.tensor_tensor(agg, agg, AGG[:, NT - 1 + c].rearrange("p h w -> p (h w)"), ALU.add))

        def norm(tag, A, B, store):
            with phase() as ph:
                stats = sb(f"{tag}_stats", [P, NT, 6], F32, ph)
                mv = sb(f"{tag}_mv", [P, NT, 2], F32, ph)
                rstd = sb(f"{tag}_rstd", [P, NT], F32, ph)
                eps = sb(f"{tag}_eps", [P, 1], F32, ph)
                chain, var_ready, rooted, done, stored = (
                    sem(f"{tag}_{k}") for k in ("chain", "var_ready", "rooted", "done", "stored"))
                block = ph.enter_context(nc.Block())

                @block.vector
                def _(dve):
                    v = nc.vector
                    v.memset(eps[:, :], EPS)
                    v.tensor_tensor(A[:], A[:], B[:], ALU.add).then_inc(chain, 1)
                    dve.wait_ge(chain, 1)
                    with dve.Fori(0, NT) as j:
                        v.bn_stats(stats[:, bass.ds(j, 1), :].rearrange("p a c -> p (a c)"),
                                   A[:, bass.ds(j, 1), :].rearrange("p a c -> p (a c)")).then_inc(chain, 1)
                    dve.wait_ge(chain, 1 + NT)
                    for j in range(NT):
                        v.bn_aggr(mv[:, j, :], stats[:, j, :]).then_inc(var_ready, 1)
                    dve.wait_ge(rooted, 1)
                    v.reciprocal(rstd[:, :], rstd[:, :])
                    shape = [P, NT, D]
                    v.tensor_tensor(A[:], A[:], mv[:, :, 0:1].to_broadcast(shape), ALU.subtract).then_inc(chain, 1)
                    dve.wait_ge(chain, 2 + NT)
                    v.tensor_tensor(A[:], A[:], rstd[:, :, None].to_broadcast(shape), ALU.mult).then_inc(done, 1)

                @block.scalar
                def _(act):
                    act.wait_ge(var_ready, NT)
                    nc.scalar.activation(rstd[:, :], mv[:, :, 1], ACT.Sqrt, bias=eps[:, 0:1]).then_inc(rooted, 1)

                if store:
                    @block.sync
                    def _(sp):
                        sp.wait_ge(done, 1)
                        sp.dma_start(out[0:(NT - 1) * P, :].rearrange("(j p) c -> p j c", p=P),
                                     A[:, 0:NT - 1, :]).then_inc(stored, 16)
                        sp.dma_start(out[(NT - 1) * P:N, :], A[0:LAST, NT - 1, :]).then_inc(stored, 16)
                        sp.wait_ge(stored, 32)

        def conv_layer(tag, xin, W, self_w, b):
            with phase() as ph:
                weights = sb(f"{tag}_weights", [P, KH, T8 + D], F32, ph)
                bias = sb(f"{tag}_bias", [P, D], F32, ph)
                loaded = sem(f"{tag}_loaded")
                with nc.Block() as block:
                    @block.sync
                    def _(sp):
                        for r in range(R8):
                            sp.dma_start(weights[:, :, r * D:(r + 1) * D],
                                         W[r].rearrange("(h p) c -> p h c", p=P)).then_inc(loaded, 16)
                        sp.dma_start(weights[:, :, T8:], self_w.rearrange("(h p) c -> p h c", p=P)).then_inc(loaded, 16)
                        sp.dma_start(bias[:, :], b.rearrange("(o c) -> o c", o=1).to_broadcast([P, D])).then_inc(loaded, 16)
                        sp.wait_ge(loaded, 16 * (R8 + 2))
                dense(tag + "_d", xin, weights, T8, table8, bias)
            convolve(tag + "_c")

        def relu_layer():
            with nc.Block() as block:
                @block.vector
                def _(dve):
                    nc.vector.tensor_scalar(Hs[:], OWN[:], 0.0, None, ALU.max)

        def head_weights(tag, layer, weights):
            with phase() as ph:
                def t(name, shape, dt=F32):
                    return sb(f"{tag}_{name}", shape, dt, ph)

                def s(name):
                    return sem(f"{tag}_{name}")

                NB = H // DH
                plain = t("plain", [P, 2, KH, D])
                wide = t("wide", [P, 2, KH, NB, P])
                turned = t("turned", [P, 2, KH, NB, P])
                small = t("small", [P, 2, NB, DH])
                prior = t("prior", [P, NB])
                blocks = t("blocks", [P, 2, NB, R2, DH, DH])
                loaded, ready, made, moved, kept, multiplied, taken = (
                    s(k) for k in ("loaded", "ready", "made", "moved", "kept", "multiplied", "taken"))
                block = ph.enter_context(nc.Block())
                pri_flat = pri[layer].rearrange("h t -> (h t)")
                PB = DH * R2

                @block.sync
                def _(sp):
                    sp.dma_start(plain[:, 0], Wk[layer].rearrange("(h p) c -> p h c", p=P)).then_inc(loaded, 16)
                    sp.dma_start(plain[:, 1], Wv[layer].rearrange("(h p) c -> p h c", p=P)).then_inc(loaded, 16)
                    sp.dma_start(weights[:, :, T2:], Wq[layer].rearrange("(h p) c -> p h c", p=P)).then_inc(loaded, 16)
                    for i, a in enumerate((Watt, Wmsg)):
                        sp.dma_start(small[:, i], a[layer].rearrange("h t d f -> (h t d) f")
                                     .rearrange("(b p) f -> p b f", p=P)).then_inc(loaded, 16)
                    for b in range(NB):
                        sp.dma_start(prior[:, b:b + 1], pri_flat[b * PB:(b + 1) * PB].rearrange("(k o) -> k o", o=1)
                                     .to_broadcast([PB, DH])).then_inc(loaded, 16)
                    sp.wait_ge(loaded, 16 * (5 + NB))

                @block.vector
                def _(dve):
                    v = nc.vector
                    dve.wait_ge(loaded, 16 * (5 + NB))
                    for i in range(2):
                        for h in range(KH):
                            v.tensor_copy(wide[:, i, h].rearrange("p b (h t d) -> p (b h) t d", h=DH, t=R2),
                                          plain[:, i, h].rearrange("p (h d) -> p h d", h=H)[:, :, None, :]
                                          .to_broadcast([P, H, R2, DH])).then_inc(ready, 1)
                    v.tensor_tensor(small[:, 0], small[:, 0], prior[:, :, None].to_broadcast([P, NB, DH]),
                                    ALU.mult).then_inc(made, 1)
                    dve.wait_ge(made, 1)
                    v.tensor_scalar(small[:, 0], small[:, 0], float(np.float32(1) / np.sqrt(np.float32(DH))), None,
                                    ALU.mult).then_inc(made, 1)
                    dve.wait_ge(made, 2)
                    for i in range(2):
                        for b in range(NB):
                            v.tensor_tensor(blocks[:, i, b].rearrange("p t h f -> p (t h) f"),
                                            blockmask[:].rearrange("p t h -> p (t h)")[:, :, None].to_broadcast([P, PB, DH]),
                                            small[:, i, b, None, :].to_broadcast([P, PB, DH]), ALU.mult).then_inc(made, 1)
                    for n in range(2 * KH):
                        dve.wait_ge(moved, n + 1)
                        v.tensor_copy(turned[:, n // KH, n % KH].rearrange("p b c -> p (b c)"),
                                      bank[n][:, :]).then_inc(kept, 1)
                    for n in range(2 * KH):
                        i, h = n // KH, n % KH
                        dve.wait_ge(multiplied, n + 1)
                        dest = weights[:, h, 0:T2].rearrange("p (t i h f) -> p t i h f", t=R2, i=2, h=H)[:, :, i]
                        for b in range(NB):
                            v.tensor_copy(dest[:, :, b * DH:(b + 1) * DH, :].rearrange("p t h f -> p t (h f)"),
                                          bank[n][:, b * P:(b + 1) * P].rearrange("p (t c) -> p t c", t=R2))

                @block.tensor
                def _(pe):
                    for n in range(2 * KH):
                        i, h = n // KH, n % KH
                        pe.wait_ge(ready, n + 1)
                        for b in range(NB):
                            last = nc.tensor.transpose(bank[n][:, b * P:(b + 1) * P], wide[:, i, h, b, :], ident[:, :])
                        last.then_inc(moved, 1)
                    pe.wait_ge(made, 2 + 2 * NB)
                    for n in range(2 * KH):
                        i, h = n // KH, n % KH
                        pe.wait_ge(kept, n + 1)
                        for b in range(NB):
                            last = nc.tensor.matmul(bank[n][:, b * P:(b + 1) * P], turned[:, i, h, b, :],
                                                    blocks[:, i, b].rearrange("p t h f -> p (t h f)"),
                                                    start=True, stop=True)
                        last.then_inc(multiplied, 1)

        def mix_layer(tag, layer, xin, AGG):
            with phase() as ph:
                def t(name, shape, dt=F32):
                    return sb(f"{tag}_{name}", shape, dt, ph)

                def s(name):
                    return sem(f"{tag}_{name}")

                wa = t("wa", [P, KH, D])
                gate = t("gate", [P, 4])
                attended = t("attended", [P, 2, D])
                below = t("below", [P, 2, H])
                xt = t("xt", [P, 2, KH, P])
                rest = t("rest", [P, 2, D])
                loaded, chain, opened, exped = s("loaded"), s("chain"), s("opened"), s("exped")
                bounded, inverted, divided = s("bounded"), s("inverted"), s("divided")
                turned, kept, multiplied, mixed, scaled = (
                    s("turned"), s("kept"), s("multiplied"), s("mixed"), s("scaled"))
                block = ph.enter_context(nc.Block())

                @block.sync
                def _(sp):
                    sp.dma_start(wa[:], Wa[layer].rearrange("(h p) c -> p h c", p=P)).then_inc(loaded, 16)
                    sp.dma_start(gate[:, 0:1], skip[layer:layer + 1].rearrange("(o c) -> o c", o=1)
                                 .to_broadcast([P, 1])).then_inc(loaded, 16)
                    sp.wait_ge(loaded, 32)

                @block.scalar
                def _(act):
                    act.wait_ge(loaded, 32)
                    nc.scalar.activation(gate[:, 1:2], gate[:, 0:1], ACT.Exp, scale=-1.0).then_inc(exped, 1)

                    def step(j, r):
                        act.wait_ge(turned, j + 1)
                        need(act, multiplied, j - 1)
                        nc.scalar.copy(xt[:, r].rearrange("p h n -> p (h n)"), bank[r][:, 0:D]).then_inc(kept, 1)
                    over_tiles(act, step)

                @block.vector
                def _(dve):
                    v = nc.vector
                    dve.wait_ge(exped, 1)
                    v.tensor_scalar(gate[:, 1:2], gate[:, 1:2], 1.0, None, ALU.add).then_inc(chain, 1)
                    dve.wait_ge(chain, 1)
                    v.reciprocal(gate[:, 2:3], gate[:, 1:2]).then_inc(chain, 1)
                    dve.wait_ge(chain, 2)
                    v.tensor_scalar(gate[:, 3:4], gate[:, 2:3], -1.0, 1.0, ALU.mult, ALU.add).then_inc(chain, 1)
                    dve.wait_ge(chain, 3)

                    def step(j, r):
                        n, k = j + 2, r
                        if is_tile(n):
                            v.tensor_scalar(below[:, k], AGG[:, at(n), :, DH].rearrange("p a h -> p (a h)"),
                                            1e-30, None, ALU.max).then_inc(bounded, 1)
                            dve.wait_ge(bounded, n + 1)
                            v.reciprocal(below[:, k], below[:, k]).then_inc(inverted, 1)
                            dve.wait_ge(inverted, n + 1)
                            need(dve, turned, n - 1)
                            v.tensor_tensor(attended[:, k].rearrange("p (h d) -> p h d", h=H),
                                            AGG[:, at(n), :, 0:DH].rearrange("p a h d -> p (a h) d"),
                                            below[:, k, :, None].to_broadcast([P, H, DH]), ALU.mult).then_inc(divided, 1)
                        if is_tile(j):
                            dve.wait_ge(multiplied, j + 1)
                            dve.wait_ge(scaled, j + 1)
                            v.scalar_tensor_tensor(Hs[:, at(j), :].rearrange("p a c -> p (a c)"), bank[2 + r][:, 0:D],
                                                   gate[:, 2:3], rest[:, r], ALU.mult, ALU.add).then_inc(mixed, 1)
                        if is_tile(n):
                            need(dve, mixed, n - 1)
                            v.tensor_scalar(rest[:, k], xin[:, at(n), :].rearrange("p a c -> p (a c)"),
                                            gate[:, 3:4], None, ALU.mult).then_inc(scaled, 1)
                    over_tiles(dve, step, early=2)

                @block.tensor
                def _(pe):
                    pe.wait_ge(loaded, 32)

                    def step(j, r):
                        if is_tile(j + 1):
                            pe.wait_ge(divided, j + 2)
                            need(pe, kept, j)
                            for h in range(KH):
                                last = nc.tensor.transpose(bank[1 - r][:, h * P:h * P + P],
                                                           attended[:, 1 - r, h * P:h * P + P], ident[:, :])
                            last.then_inc(turned, 1)
                        if is_tile(j):
                            pe.wait_ge(kept, j + 1)
                            need(pe, mixed, j - 1)
                            for h in range(KH):
                                last = nc.tensor.matmul(bank[2 + r][:, 0:D], xt[:, r, h, :], wa[:, h, :],
                                                        start=(h == 0), stop=(h == KH - 1))
                            last.then_inc(multiplied, 1)
                    over_tiles(pe, step, early=1)

        def attention_layer(layer, xin):
            with phase() as ph:
                weights = sb(f"t{layer}_weights", [P, KH, T2 + D], F32, ph)
                head_weights(f"t{layer}w", layer, weights)
                dense(f"t{layer}d", xin, weights, T2, table2, None)
            with phase() as ph:
                AGG = sb(f"t{layer}_AGG", [P, NT + STRANDS - 1, H, HW], F32, ph)
                first_guard = sb(f"t{layer}_first_guard", [P, 1], F32, ph)
                last_guard = sb(f"t{layer}_last_guard", [P, 1], F32, ph)
                attend(f"t{layer}a", AGG, first_guard, last_guard)
                merge(f"t{layer}g", AGG, first_guard, last_guard)
                mix_layer(f"t{layer}m", layer, xin, AGG)

        prepare()
        conv_layer("c1", X, W1, self_w1, b1)
        relu_layer()
        conv_layer("c2", Hs, W2, self_w2, b2)
        norm("n1", X, OWN, False)
        attention_layer(0, X)
        attention_layer(1, Hs)
        norm("n2", X, Hs, True)


_INS = ['x', 'src', 'dst', 'edge_type_2', 'edge_type_8', 'L0_gnn_W1', 'L0_gnn_self_w1', 'L0_gnn_b1', 'L0_gnn_W2',
        'L0_gnn_self_w2', 'L0_gnn_b2', 'L1_gnn_Wk', 'L1_gnn_Wq', 'L1_gnn_Wv', 'L1_gnn_Wa', 'L1_gnn_Watt',
        'L1_gnn_Wmsg', 'L1_gnn_pri', 'L1_gnn_skip']


def kernel(**inputs):
    import numpy as _np
    import concourse.bacc as _bacc
    from concourse import mybir as _mybir
    from concourse.bass_utils import run_bass_kernel_spmd as _run

    nc = _bacc.Bacc("TRN2", target_bir_lowering=False, num_devices=1)
    arrays, args = {}, []
    for name in _INS:
        a = _np.ascontiguousarray(inputs[name])
        arrays[f"in_{name}_dram"] = a
        args.append(nc.dram_tensor(f"in_{name}_dram", a.shape, _mybir.dt.from_np(a.dtype), kind="ExternalInput").ap())
    shape = inputs["x"].shape
    args.append(nc.dram_tensor("out_0_dram", shape, _mybir.dt.float32, kind="ExternalOutput").ap())
    build(nc, *args)
    r = _run(nc, [arrays], core_ids=[0])
    return r.results[0]["out_0_dram"]
```

```python
from contextlib import ExitStack, contextmanager

import numpy as np
import concourse.bass as bass
from concourse import mybir

ALU = mybir.AluOpType
ACT = mybir.ActivationFunctionType
AX = mybir.AxisListType
F32 = mybir.dt.float32
I32 = mybir.dt.int32
STEPS = 2
STRANDS = 4
RING = 2 * STRANDS
BIG = 1e38
MAGIC = 1.5 * 2 ** 23
NO_NODE = 1 << 20


def ceil_div(a, b):
    return -(-a // b)


def need(eng, sem, value):
    if not isinstance(value, int) or value > 0:
        eng.wait_ge(sem, value)


def build(nc, x, src, dst, edge_type_2, edge_type_8, W1, self_w1, b1, W2, self_w2, b2,
          Wk, Wq, Wv, Wa, Watt, Wmsg, pri, skip, out):
    P = 128
    N, D = x.shape
    E = src.shape[0]
    R8 = W1.shape[0]
    H, R2, DH = Watt.shape[1], Watt.shape[2], Watt.shape[3]
    HW = DH + 1
    NT = ceil_div(N, P)
    LAST = N - (NT - 1) * P
    ET = ceil_div(E, P)
    NG = ceil_div((ET + NT - 1 + NT * (STEPS - 1)) // STEPS, RING) * RING
    NS = NG * STEPS
    KB = ceil_div(max(NS, ET + 1), P)
    ROUNDS = NG // RING
    LEN = NG // STRANDS
    ENDS = 2 * STRANDS
    KH = D // P
    T8, T2 = R8 * D, R2 * 2 * D
    LAYERS = Wk.shape[0]
    NB = H // DH
    FULL = E // (P * P)
    EPS = 1e-5

    edge_rows = nc.dram_tensor("edge_rows", (KB * P, 3 * P), F32).ap()
    step_nodes = nc.dram_tensor("step_nodes", (1 + KB * P, P), F32).ap()
    step_resets = nc.dram_tensor("step_resets", (1 + KB * P, P), F32).ap()
    step_tiles = nc.dram_tensor("step_tiles", (1, KB * P), I32).ap()
    table8 = nc.dram_tensor("table8", (NT * P * R8, D), F32).ap()
    table2 = nc.dram_tensor("table2", (NT * P * R2, 2 * D), F32).ap()

    top = ExitStack()

    def sb(name, shape, dt=F32, scope=top):
        return scope.enter_context(nc.sbuf_tensor(name, shape, dt))

    def sem(name):
        return nc.alloc_semaphore(name)

    @contextmanager
    def phase():
        earlier = nc.snapshot_sems()
        with ExitStack() as ph:
            yield ph
        nc.clear_and_free_semaphores(nc.allocated_since(earlier))
        nc.all_engine_barrier()

    with top:
        bank = [top.enter_context(nc.psum_tensor(f"bank{i}", [P, 512], F32)) for i in range(8)]
        X = sb("X", [P, NT, D])
        Hs = sb("Hs", [P, NT, D])
        OWN = sb("OWN", [P, NT, D])
        ident = sb("ident", [P, P])
        ones = sb("ones", [P, P])
        iota_free = sb("iota_free", [P, P])
        blockmask = sb("blockmask", [P, R2, DH])
        plain = sb("plain", [P, 2, KH, D])
        small = sb("small", [P, 2, NB, DH])
        prior = sb("prior", [P, NB])
        head_table = sb("head_table", [P, KH, T2 + D])
        local = sb("local", [P, NS])
        index8 = sb("index8", [P, NS], I32)
        index2 = sb("index2", [P, NS], I32)
        group_tile = sb("group_tile", [P, STRANDS, LEN], I32)
        group_slot = sb("group_slot", [P, STRANDS, LEN], I32)
        first_local = sb("first_local", [P, LEN])
        still_first = sb("still_first", [P, LEN])
        end_node = sb("end_node", [P, 2, STRANDS])
        at_end = sb("at_end", [P, 2, STRANDS])

        def load_list(sp, into, a, first, loaded):
            count = E - first
            blocks, tail, rest = count // (P * P), count // P % P, count % P
            whole, loads = first + blocks * P * P, 1
            sp.dma_start(into[:, 0:blocks, :],
                         a[first:whole].rearrange("(b p e) -> p b e", p=P, e=P)).then_inc(loaded, 16)
            if tail:
                loads += 1
                sp.dma_start(into[0:tail, blocks, :],
                             a[whole:whole + tail * P].rearrange("(p e) -> p e", e=P)).then_inc(loaded, 16)
            if rest:
                loads += 1
                sp.dma_start(into[tail:tail + 1, blocks, 0:rest],
                             a[E - rest:E].rearrange("(p e) -> p e", p=1)).then_inc(loaded, 16)
            return loads

        def load_weights(sp, weights, bias, W, self_w, b, loaded):
            for r in range(R8):
                sp.dma_start(weights[:, :, r * D:(r + 1) * D],
                             W[r].rearrange("(h p) c -> p h c", p=P)).then_inc(loaded, 16)
            sp.dma_start(weights[:, :, T8:], self_w.rearrange("(h p) c -> p h c", p=P)).then_inc(loaded, 16)
            sp.dma_start(bias[:, :], b.rearrange("(o c) -> o c", o=1).to_broadcast([P, D])).then_inc(loaded, 16)
            return R8 + 2

        def read_edges(rows, unsorted, x_loaded, weights, bias, weights_loaded):
            with phase() as ph:
                def s(name):
                    return sem("r_" + name)

                raw = sb("r_raw", [P, 4, KB, P], I32, ph)
                follower = sb("r_follower", [P, KB, P], I32, ph)
                descends = sb("r_descends", [P, KB, P], F32, ph)
                descents = sb("r_descents", [P, 2], F32, ph)
                loaded, padded, made = s("loaded"), s("padded"), s("made")
                rows_ready, rows_out, found, summed, compared = (
                    s("rows_ready"), s("rows_out"), s("found"), s("summed"), s("compared"))
                n_loads = 4 * (1 + (E // P % P > 0) + (E % P > 0)) + 1 + ((E - 1) // P % P > 0) + ((E - 1) % P > 0)
                block = ph.enter_context(nc.Block())

                @block.sync
                def _(sp):
                    sp.wait_ge(padded, 1)
                    for i, a in enumerate((dst, src, edge_type_8, edge_type_2)):
                        load_list(sp, raw[:, i], a, 0, loaded)
                    load_list(sp, follower, dst, 1, loaded)
                    sp.wait_ge(rows_ready, 1)
                    sp.dma_start(edge_rows.rearrange("(b p) c -> p b c", p=P),
                                 rows[:].rearrange("p b i e -> p b (i e)")).then_inc(rows_out, 16)
                    sp.dma_start(X[:, 0:NT - 1, :],
                                 x[0:(NT - 1) * P, :].rearrange("(j p) c -> p j c", p=P)).then_inc(x_loaded, 16)
                    sp.dma_start(X[0:LAST, NT - 1, :], x[(NT - 1) * P:N, :]).then_inc(x_loaded, 16)
                    load_weights(sp, weights, bias, W1, self_w1, b1, weights_loaded)
                    sp.wait_ge(rows_out, 16)

                @block.gpsimd
                def _(pool):
                    nc.gpsimd.iota(iota_free[:, :], pattern=[[1, P]], base=0, channel_multiplier=0,
                                   allow_small_or_imprecise_dtypes=True)
                    nc.gpsimd.memset(ident[:, :], 0.0).then_inc(made, 1)
                    pool.wait_ge(made, 1)
                    nc.gpsimd.affine_select(out=ident[:, :], in_=ident[:, :], compare_op=ALU.not_equal, fill=1.0,
                                            base=0, pattern=[[-1, P]], channel_multiplier=1)

                @block.tensor
                def _(pe):
                    pe.wait_ge(found, 1)
                    nc.tensor.matmul(bank[0][:, 0:1], ones[:, :], descents[:, 0:1], start=True,
                                     stop=True).then_inc(summed, 1)

                @block.vector
                def _(dve):
                    v = nc.vector
                    v.memset(X[:, NT - 1, :], 0.0)
                    v.memset(raw[:, 1:4, FULL:KB, :], 0)
                    v.memset(follower[:, (E - 1) // (P * P):KB, :], NO_NODE)
                    v.memset(ones[:, :], 1.0)
                    v.memset(raw[:, 0, FULL:KB, :], NO_NODE).then_inc(padded, 1)
                    dve.wait_ge(padded, 1)
                    dve.wait_ge(loaded, 16 * n_loads)
                    v.tensor_copy(rows[:, :, 0, :], raw[:, 0])
                    v.scalar_tensor_tensor(rows[:, :, 1, :], raw[:, 1], float(R8), raw[:, 2], ALU.mult, ALU.add)
                    v.scalar_tensor_tensor(rows[:, :, 2, :], raw[:, 1], float(R2), raw[:, 3], ALU.mult,
                                           ALU.add).then_inc(rows_ready, 1)
                    v.tensor_tensor(descends[:], follower[:], raw[:, 0], ALU.is_lt).then_inc(compared, 1)
                    dve.wait_ge(compared, 1)
                    v.tensor_reduce(descents[:, 0:1], descends[:].rearrange("p b e -> p (b e)"), AX.X,
                                    ALU.add).then_inc(found, 1)
                    dve.wait_ge(summed, 1)
                    v.tensor_scalar(unsorted[:, :], bank[0][:, 0:1], 0.5, None, ALU.is_gt)

        def sort_edges(rows):
            with phase() as ph:
                def s(name):
                    return sem("s_" + name)

                def t(name, shape, dt=F32):
                    return sb("s_" + name, shape, dt, ph)

                NODES = NT * P
                assert N < NODES
                CHUNKS = NODES // 512
                columns = t("columns", [P, 3, KB * P])
                node_no = t("node_no", [P, NODES])
                mine = t("mine", [P, NODES])
                places = t("places", [P, NODES])
                taken = t("taken", [P, NODES])
                upto = t("upto", [P, NODES])
                plus = t("plus", [P, NODES])
                now = t("now", [P, 3])
                diag = t("diag", [P, P])
                same = t("same", [P, P])
                earlier = t("earlier", [P, P])
                place = t("place", [P, 4])
                target_i = t("target_i", [P, 3], I32)
                of_kind = t("of_kind", [P, 3])
                consts, turned, kept, chain, onehot_ready, counted, used, placed, scattered, pace = (
                    s(k) for k in ("consts", "turned", "kept", "chain", "onehot_ready", "counted", "used",
                                   "placed", "scattered", "pace"))
                block = ph.enter_context(nc.Block())
                cells = edge_rows.rearrange("k c -> (k c)").rearrange("(k o) -> k o", o=1)
                FIRST, SECOND = 4, 13

                @block.sync
                def _(sp):
                    sp.wait_ge(consts, 3)

                @block.scalar
                def _(act):
                    act.wait_ge(consts, 3)

                @block.gpsimd
                def _(pool):
                    nc.gpsimd.iota(node_no[:, :], pattern=[[1, NODES]], base=0, channel_multiplier=0,
                                   allow_small_or_imprecise_dtypes=True).then_inc(consts, 1)
                    nc.gpsimd.iota(of_kind[:, :], pattern=[[P, 3]], base=0, channel_multiplier=0,
                                   allow_small_or_imprecise_dtypes=True).then_inc(consts, 1)
                    nc.gpsimd.iota(earlier[:, :], pattern=[[-1, P]], base=0, channel_multiplier=1,
                                   allow_small_or_imprecise_dtypes=True).then_inc(consts, 1)
                    with pool.Fori(0, ET) as k:
                        pool.wait_ge(placed, k + 1)
                        nc.gpsimd.sem_inc(pace, 1)
                        for i in range(3):
                            nc.gpsimd.indirect_dma_start(
                                out=cells, out_offset=bass.IndirectOffsetOnAxis(ap=target_i[:, i:i + 1], axis=0),
                                in_=now[:, i:i + 1], in_offset=None).then_inc(scattered, 16)
                    pool.wait_ge(scattered, 48 * ET)

                @block.tensor
                def _(pe):
                    for n in range(3 * KB):
                        if n >= 2:
                            pe.wait_ge(kept, n - 1)
                        nc.tensor.transpose(bank[n % 2][:, 0:P], rows[:, n % KB, n // KB, :], ident[:, :]).then_inc(turned, 1)
                    pe.wait_ge(kept, 3 * KB)

                    def count(k):
                        pe.wait_ge(onehot_ready, k + 1)
                        for c in range(CHUNKS):
                            last = nc.tensor.matmul(bank[c][:, :], ones[:, :], mine[:, c * 512:(c + 1) * 512],
                                                    start=True, stop=True)
                        return last
                    with pe.Fori(0, ET) as k:
                        count(k).then_inc(counted, 1)
                    with pe.Fori(0, ET) as k:
                        count(k + ET)
                        nc.tensor.matmul(bank[CHUNKS][:, 0:P], ones[:, :], diag[:, :], start=True,
                                         stop=True).then_inc(counted, 1)

                @block.vector
                def _(dve):
                    v = nc.vector

                    def link(ins, value):
                        ins.then_inc(chain, 1)
                        dve.wait_ge(chain, value)

                    dve.wait_ge(consts, 3)
                    link(v.tensor_scalar(earlier[:, :], earlier[:, :], 0.5, None, ALU.is_gt), 1)
                    for n in range(3 * KB):
                        dve.wait_ge(turned, n + 1)
                        into = columns[:, n // KB, n % KB * P:(n % KB + 1) * P]
                        if n < KB:
                            v.tensor_scalar(into, bank[n % 2][:, 0:P], float(N), None, ALU.min).then_inc(kept, 1)
                        else:
                            v.tensor_copy(into, bank[n % 2][:, 0:P]).then_inc(kept, 1)
                    dve.wait_ge(kept, 3 * KB)
                    link(v.memset(taken[:, :], 0.0), 2)

                    def start(k, n):
                        link(v.tensor_copy(now[:, :], columns[:, :, bass.ds(k, 1)].rearrange("p i a -> p (i a)")), n + 1)
                        link(v.tensor_scalar(mine[:, :], node_no[:, :], now[:, 0:1], None, ALU.is_equal), n + 2)

                    def add_counts(n):
                        for c in range(CHUNKS):
                            part = slice(c * 512, (c + 1) * 512)
                            ins = v.tensor_tensor(taken[:, part], taken[:, part], bank[c][:, :], ALU.add)
                        link(ins, n)

                    with dve.Fori(0, ET) as k:
                        n = k * FIRST + 2
                        start(k, n)
                        v.sem_inc(onehot_ready, 1)
                        dve.wait_ge(counted, k + 1)
                        add_counts(n + 3)
                        link(v.tensor_copy(place[:, 0:1], now[:, 0:1]), n + 4)
                    n = ET * FIRST + 2
                    link(v.memset(plus[:, :], 1.0), n + 1)
                    link(v.tensor_tensor_scan(upto[:, :], plus[:, :], taken[:, :], 0.0, ALU.mult, ALU.add), n + 2)
                    link(v.tensor_tensor(taken[:, :], upto[:, :], taken[:, :], ALU.subtract), n + 3)
                    base = n + 3
                    with dve.Fori(0, ET) as k:
                        n = k * SECOND + base
                        dve.wait_ge(scattered, k * 48)
                        start(k, n)
                        link(v.tensor_scalar(diag[:, :], ident[:, :], now[:, 0:1], None, ALU.mult), n + 3)
                        v.sem_inc(onehot_ready, 1)
                        link(v.tensor_tensor(places[:, :], mine[:, :], taken[:, :], ALU.mult), n + 4)
                        link(v.tensor_reduce(place[:, 0:1], places[:, :], AX.X, ALU.add), n + 5)
                        dve.wait_ge(counted, k + ET + 1)
                        link(v.scalar_tensor_tensor(same[:, :], bank[CHUNKS][:, 0:P], now[:, 0:1], earlier[:, :],
                                                    ALU.is_equal, ALU.mult), n + 6)
                        link(v.tensor_reduce(place[:, 1:2], same[:, :], AX.X, ALU.add), n + 7)
                        link(v.tensor_tensor(place[:, 2:3], place[:, 0:1], place[:, 1:2], ALU.add), n + 8)
                        link(v.tensor_scalar(place[:, 3:4], place[:, 2:3], 1.0 / P, -(P - 1) / 2 / P, ALU.mult, ALU.add), n + 9)
                        link(v.tensor_scalar(place[:, 3:4], place[:, 3:4], MAGIC, -MAGIC, ALU.add, ALU.add), n + 10)
                        link(v.scalar_tensor_tensor(place[:, 3:4], place[:, 3:4], 2.0 * P, place[:, 2:3],
                                                    ALU.mult, ALU.add), n + 11)
                        link(v.tensor_scalar(target_i[:, :], of_kind[:, :], place[:, 3:4], None, ALU.add), n + 12)
                        v.sem_inc(placed, 1)
                        add_counts(n + 13)

        def prepare(weights, bias):
            with phase() as ph:
                x_loaded, weights_loaded = sem("x_loaded"), sem("weights_loaded")
                rows = sb("rows", [P, KB, 3, P], F32, ph)
                unsorted = sb("unsorted", [P, 1], I32, ph)
                read_edges(rows, unsorted, x_loaded, weights, bias, weights_loaded)
                with nc.If(nc.values_load(unsorted[0:1, 0:1], min_val=0, max_val=1) > 0):
                    sort_edges(rows)
                nc.end_ifs()
                list_steps(rows, x_loaded, weights_loaded)

        def list_steps(rows, x_loaded, weights_loaded):
            with phase() as ph:
                def s(name):
                    return sem("p_" + name)

                def t(name, shape, dt=F32):
                    return sb("p_" + name, shape, dt, ph)

                below = t("below", [P, NT + 1])
                junk = t("junk", [P, 2, KB, P])
                tiles_all = t("tiles_all", [P, NS], I32)
                tile_g = t("tile_g", [P, STRANDS, LEN])
                slot_g = t("slot_g", [P, STRANDS, LEN])
                first_tile = t("first_tile", [P, LEN])
                node_ok = t("node_ok", [P, LEN])
                end_tile = t("end_tile", [P, 2, STRANDS])
                total = t("total", [P, NT + 1])
                wk = t("wk", [P, 12, NT])
                one20 = t("one20", [P, NT])
                step_no = t("step_no", [P, KB])
                group_no = t("group_no", [P, KB])
                past = t("past", [P, KB, NT - 1])
                moved = t("moved", [P, KB, NT - 1])
                tile_f = t("tile_f", [P, KB])
                row_f = t("row_f", [P, KB])
                row_i = t("row_i", [P, KB], I32)
                tile_i = t("tile_i", [P, KB], I32)
                srow = t("srow", [P, KB, 3, P])
                inside = t("inside", [P, KB, P])
                inside2 = t("inside2", [P, KB, P])
                node = t("node", [P, KB, P])
                before = t("before", [P, KB, P])
                reset = t("reset", [P, KB, P])
                minus1 = t("minus1", [1, P])
                firstsel = t("firstsel", [P, P])
                blk = t("blk", [P, P])

                zeroed, made = s("zeroed"), s("made")
                chain, consts, counted = s("chain"), s("consts"), s("counted")
                picked = s("picked")
                got = [s(f"got{b}") for b in range(KB)]
                nodes_ready, nodes_out, shifted = s("nodes_ready"), s("nodes_out"), s("shifted")
                resets_ready, tiles_in = s("resets_ready"), s("tiles_in")
                turned, taken, first_made = s("turned"), s("taken"), s("first_made")
                tail_out, ends_in = s("tail_out"), s("ends_in")
                block = ph.enter_context(nc.Block())

                flat_nodes = step_nodes.rearrange("k e -> (k e)")

                @block.sync
                def _(sp):
                    sp.wait_ge(zeroed, 1)
                    sp.wait_ge(nodes_ready, 1)
                    sp.dma_start(step_nodes[0:1, :], minus1[:, :]).then_inc(nodes_out, 16)
                    sp.dma_start(step_nodes[1:1 + KB * P, :].rearrange("(b p) e -> p b e", p=P),
                                 node[:]).then_inc(nodes_out, 16)
                    sp.wait_ge(nodes_out, 32)
                    sp.dma_start(before[:], flat_nodes[P - 1:P - 1 + KB * P * P].rearrange(
                        "(b p e) -> p b e", p=P, e=P)).then_inc(shifted, 16)
                    sp.dma_start(step_tiles[0, :].rearrange("(b p) -> p b", p=P), tile_i[:, :],
                                 allow_slow_non_contiguous=True).then_inc(tiles_in, 16)
                    sp.wait_ge(tiles_in, 16)
                    sp.dma_start(tiles_all[:, :], step_tiles[:, 0:NS].to_broadcast([P, NS])).then_inc(tiles_in, 16)
                    of_strands = flat_nodes[P:P + NS * P].rearrange("(c f) -> c f", c=STRANDS)
                    for k, edge in enumerate((0, NS * P // STRANDS - 1)):
                        sp.dma_start(end_node[:, k, :], of_strands[:, edge:edge + 1].rearrange("c o -> o c")
                                     .to_broadcast([P, STRANDS]), allow_slow_non_contiguous=True).then_inc(ends_in, 16)
                    sp.wait_ge(resets_ready, 1)
                    sp.dma_start(step_resets[0:KB * P, :].rearrange("(b p) e -> p b e", p=P),
                                 reset[:]).then_inc(tail_out, 16)
                    sp.dma_start(step_resets[KB * P:KB * P + 1, :], minus1[:, :]).then_inc(tail_out, 16)
                    sp.wait_ge(tail_out, 32)
                    sp.wait_ge(x_loaded, 32)
                    sp.wait_ge(weights_loaded, 16 * (R8 + 2))

                @block.gpsimd
                def _(pool):
                    nc.gpsimd.iota(step_no[:, :], pattern=[[P, KB]], base=0, channel_multiplier=1,
                                   allow_small_or_imprecise_dtypes=True).then_inc(consts, 1)
                    nc.gpsimd.memset(firstsel[:, :], 0.0).then_inc(made, 1)
                    nc.gpsimd.iota(blk[:, 0:R2 * DH].rearrange("p (t h) -> p t h", t=R2),
                                   pattern=[[-DH, R2], [-DH * R2, DH]], base=0, channel_multiplier=1,
                                   allow_small_or_imprecise_dtypes=True).then_inc(consts, 1)
                    pool.wait_ge(made, 1)
                    nc.gpsimd.affine_select(out=firstsel[:, :], in_=firstsel[:, :], compare_op=ALU.not_equal,
                                            fill=1.0, base=0, pattern=[[0, P]],
                                            channel_multiplier=1).then_inc(consts, 1)
                    pool.wait_ge(picked, 1)
                    for b in range(KB):
                        nc.gpsimd.indirect_dma_start(
                            out=srow[:, b].rearrange("p i e -> p (i e)"), out_offset=None, in_=edge_rows,
                            in_offset=bass.IndirectOffsetOnAxis(ap=row_i[:, b:b + 1], axis=0)).then_inc(got[b], 16)

                @block.tensor
                def _(pe):
                    pe.wait_ge(counted, 1)
                    nc.tensor.matmul(bank[0][:, 0:NT + 1], ones[:, :], below[:, :], start=True,
                                     stop=True).then_inc(turned, 1)
                    pe.wait_ge(consts, 3)
                    pe.wait_ge(nodes_ready, 1)
                    for i in range(3):
                        for b in range(KB):
                            n = i * KB + b
                            if n >= 4:
                                pe.wait_ge(taken, n - 3)
                            nc.tensor.transpose(bank[1 + n % 4][:, 0:P], srow[:, b, i, :], ident[:, :]).then_inc(turned, 1)
                    pe.wait_ge(taken, KB)
                    nc.tensor.matmul(bank[5][:, 0:NG], firstsel[:, :],
                                     local[:, 0:NS].rearrange("p (g u) -> p g u", u=STEPS)[:, :, 0],
                                     start=True, stop=True).then_inc(first_made, 1)

                @block.vector
                def _(dve):
                    v = nc.vector
                    n = [0]

                    def link(ins):
                        n[0] += 1
                        ins.then_inc(chain, 1)
                        dve.wait_ge(chain, n[0])

                    v.memset(below[:, 0:1], 0.0)
                    v.memset(minus1[:, :], -1.0).then_inc(zeroed, 1)
                    v.memset(one20[:, :], 1.0)
                    for j in range(1, NT + 1):
                        if j > 2:
                            dve.wait_ge(chain, n[0] + j - 2)
                        v.tensor_scalar(junk[:, j % 2], rows[:, :, 0, :], float(min(j * P, N)), 0.0, ALU.is_lt, ALU.add,
                                        accum_out=below[:, j:j + 1]).then_inc(chain, 1)
                    n[0] += NT
                    dve.wait_ge(chain, n[0])
                    v.sem_inc(counted, 1)
                    dve.wait_ge(turned, 1)
                    link(v.tensor_copy(total[:, :], bank[0][:, 0:NT + 1]))
                    lo, hi = total[:, 0:NT], total[:, 1:NT + 1]

                    def whole(o, i, step, shift):
                        link(v.tensor_scalar(o, i, 1.0 / step, (shift - (step - 1) / 2) / step, ALU.mult, ALU.add))
                        link(v.tensor_scalar(o, o, MAGIC, None, ALU.add))
                        link(v.tensor_scalar(o, o, -MAGIC, None, ALU.add))

                    first_row, last_row, some, count, groups, upto, offset = (wk[:, i, :] for i in range(7))
                    whole(first_row, lo, P, 0)
                    whole(last_row, hi, P, -1)
                    link(v.tensor_tensor(some, hi, lo, ALU.is_gt))
                    link(v.tensor_tensor(count, last_row, first_row, ALU.subtract))
                    link(v.scalar_tensor_tensor(count, count, 1.0, some, ALU.add, ALU.mult))
                    whole(groups, count, STEPS, STEPS - 1)
                    link(v.tensor_tensor_scan(upto, one20[:, :], groups, 0.0, ALU.mult, ALU.add))
                    link(v.tensor_tensor(offset, upto, groups, ALU.subtract))
                    link(v.scalar_tensor_tensor(offset, offset, -float(STEPS), first_row, ALU.mult, ALU.add))
                    link(v.tensor_tensor(wk[:, 7, 0:NT - 1], offset[:, 1:NT], offset[:, 0:NT - 1], ALU.subtract))
                    dve.wait_ge(consts, 3)
                    whole(group_no[:, :], step_no[:, :], STEPS, 0)
                    shape = [P, KB, NT - 1]
                    link(v.tensor_tensor(past[:], group_no[:, :, None].to_broadcast(shape),
                                         upto[:, None, 0:NT - 1].to_broadcast(shape), ALU.is_ge))
                    link(v.tensor_tensor(moved[:], past[:], wk[:, 7, None, 0:NT - 1].to_broadcast(shape), ALU.mult))
                    v.tensor_reduce(tile_f[:, :], past[:], AX.X, ALU.add)
                    link(v.tensor_reduce(row_f[:, :], moved[:], AX.X, ALU.add))
                    link(v.tensor_tensor(row_f[:, :], row_f[:, :], step_no[:, :], ALU.add))
                    link(v.tensor_scalar(row_f[:, :], row_f[:, :], offset[:, 0:1], float(ET), ALU.add, ALU.min))
                    v.tensor_copy(tile_i[:, :], tile_f[:, :])
                    v.tensor_copy(row_i[:, :], row_f[:, :]).then_inc(picked, 1)
                    bm = blk[:, 0:R2 * DH].rearrange("p (t h) -> p t h", t=R2)
                    link(v.tensor_scalar(blockmask[:], bm, -0.5, None, ALU.is_gt))
                    link(v.tensor_scalar(bm, bm, DH - 0.5, None, ALU.is_lt))
                    link(v.tensor_tensor(blockmask[:], blockmask[:], bm, ALU.mult))
                    for b in range(KB):
                        dve.wait_ge(got[b], 16)
                    link(v.tensor_scalar(tile_f[:, :], tile_f[:, :], float(P), None, ALU.mult))
                    for b in range(KB):
                        v.tensor_scalar(inside[:, b], srow[:, b, 0, :], tile_f[:, b:b + 1], None, ALU.subtract)
                    link(v.tensor_scalar(node[:], srow[:, :, 0, :], 1.0, None, ALU.add))
                    link(v.tensor_scalar(inside2[:], inside[:], float(P), None, ALU.is_lt))
                    link(v.scalar_tensor_tensor(inside2[:], inside[:], 0.0, inside2[:], ALU.is_ge, ALU.mult))
                    link(v.tensor_tensor(node[:], node[:], inside2[:], ALU.mult))
                    link(v.tensor_scalar(node[:], node[:], -1.0, None, ALU.add))
                    link(v.tensor_copy(srow[:, :, 0, :], inside[:]))
                    v.sem_inc(nodes_ready, 1)
                    dve.wait_ge(shifted, 16)
                    link(v.tensor_tensor(reset[:], node[:], before[:], ALU.not_equal))
                    v.tensor_scalar(reset[:], reset[:], -BIG, None, ALU.mult).then_inc(resets_ready, 1)
                    for i in range(3):
                        for b in range(KB):
                            k = i * KB + b
                            w = min(P, NS - b * P)
                            dve.wait_ge(turned, 2 + k)
                            dest = (local, index8, index2)[i]
                            v.tensor_copy(dest[:, b * P:b * P + w], bank[1 + k % 4][:, 0:w]).then_inc(taken, 1)
                    dve.wait_ge(first_made, 1)
                    for c in range(STRANDS):
                        on = slice(c * H, (c + 1) * H)
                        v.tensor_copy(first_local[on, :], bank[5][on, c * LEN:(c + 1) * LEN]).then_inc(chain, 1)
                    n[0] += STRANDS
                    dve.wait_ge(tiles_in, 32)
                    link(v.tensor_copy(tile_g[:], tiles_all[:].rearrange("p (c g u) -> p c g u", c=STRANDS, u=STEPS)[:, :, :, 0]))
                    for c in range(STRANDS):
                        on = slice(c * H, (c + 1) * H)
                        v.tensor_copy(first_tile[on, :], tile_g[on, c, :])
                        if c:
                            v.tensor_scalar(slot_g[:, c], tile_g[:, c], tile_g[:, c, 0:1], None, ALU.is_equal)
                        else:
                            v.memset(slot_g[:, c], 0.0)
                        for k, g in enumerate((0, LEN - 1)):
                            ins = v.tensor_copy(end_tile[:, k, c:c + 1], tile_g[:, c, g:g + 1])
                    link(ins)
                    for c in range(1, STRANDS):
                        link(v.tensor_scalar(node[:, c, 0:LEN], tile_g[:, c], -1.0, float(NT - 1 + c), ALU.mult, ALU.add))
                        link(v.tensor_tensor(slot_g[:, c], slot_g[:, c], node[:, c, 0:LEN], ALU.mult))
                    link(v.tensor_tensor(slot_g[:], slot_g[:], tile_g[:], ALU.add))
                    v.tensor_copy(group_slot[:], slot_g[:])
                    v.tensor_copy(group_tile[:], tile_g[:])
                    link(v.tensor_scalar(node_ok[:, :], first_local[:, :], float(P), None, ALU.is_lt))
                    link(v.scalar_tensor_tensor(node_ok[:, :], first_local[:, :], 0.0, node_ok[:, :], ALU.is_ge, ALU.mult))
                    link(v.scalar_tensor_tensor(first_tile[:, :], first_tile[:, :], float(P), first_local[:, :],
                                                ALU.mult, ALU.add))
                    link(v.scalar_tensor_tensor(first_tile[:, :], first_tile[:, :], 1.0, node_ok[:, :], ALU.add, ALU.mult))
                    link(v.tensor_scalar(still_first[:, :], first_tile[:, :], first_tile[:, 0:1], None, ALU.is_equal))
                    link(v.tensor_scalar(still_first[:, :], still_first[:, :], -1.0, BIG, ALU.add, ALU.mult))
                    dve.wait_ge(ends_in, 32)
                    link(v.scalar_tensor_tensor(at_end[:], end_tile[:], -float(P), end_node[:], ALU.mult, ALU.add))
                    link(v.tensor_scalar(at_end[:], at_end[:], step_no[:, 0:1], None, ALU.is_equal))
                    link(v.tensor_tensor(end_tile[:, 0], end_node[:, 0], end_node[:, 1], ALU.not_equal))
                    v.tensor_tensor(at_end[:, 1], at_end[:, 1], end_tile[:, 0], ALU.mult)

        def over_tiles(eng, step, early=0):
            for j in range(-early, 2):
                step(j, j % 2)
            with eng.Fori(1, NT // 2 - 1) as i:
                step(i * 2, 0)
                step(i * 2 + 1, 1)
            for j in (NT - 2, NT - 1):
                step(j, j % 2)

        def is_tile(j):
            return not isinstance(j, int) or 0 <= j < NT

        def at(j):
            return slice(j, j + 1) if isinstance(j, int) else bass.ds(j, 1)

        def dense(tag, xin, weights, n_table, table, bias):
            with phase() as ph:
                def s(name):
                    return sem(f"{tag}_{name}")

                xs = sb(f"{tag}_xs", [P, 2, D], F32, ph)
                xt = sb(f"{tag}_xt", [P, 2, KH, P], F32, ph)
                stage = sb(f"{tag}_stage", [P, 2, n_table], F32, ph)
                copied, turned, kept = s("copied"), s("turned"), s("kept")
                multiplied, act_took, dve_took = s("multiplied"), s("act_took"), s("dve_took")
                stored = [s("stored0"), s("stored1")]
                NCH = n_table // 512
                act_chunks = [c for c in range(NCH) if c % 2 == 0]
                dve_chunks = [c for c in range(NCH) if c % 2 == 1]
                rows_out = table.rearrange("(j p r) c -> p j (r c)", p=P, r=n_table // table.shape[1])
                block = ph.enter_context(nc.Block())

                @block.vector
                def _(dve):
                    def step(j, r):
                        if is_tile(j + 2):
                            need(dve, turned, j + 1)
                            nc.vector.tensor_copy(xs[:, r, :], xin[:, at(j + 2), :].rearrange("p a c -> p (a c)")).then_inc(copied, 1)
                        if is_tile(j):
                            for k, c in enumerate(dve_chunks):
                                dve.wait_ge(multiplied, j * (NCH + 1) + c + 1)
                                if k == 0 and (not isinstance(j, int) or j >= 2):
                                    dve.wait_ge(stored[r], (j - r) * 8)
                                nc.vector.tensor_copy(stage[:, r, c * 512:c * 512 + 512], bank[c][:, :]).then_inc(dve_took, 1)
                            dve.wait_ge(multiplied, j * (NCH + 1) + NCH + 1)
                            own = OWN[:, at(j), :].rearrange("p a c -> p (a c)")
                            if bias is None:
                                nc.vector.tensor_copy(own, bank[NCH][:, 0:D]).then_inc(dve_took, 1)
                            else:
                                nc.vector.tensor_tensor(own, bank[NCH][:, 0:D], bias[:, :], ALU.add).then_inc(dve_took, 1)
                    over_tiles(dve, step, early=2)

                @block.tensor
                def _(pe):
                    def step(j, r):
                        if is_tile(j + 1):
                            pe.wait_ge(copied, j + 2)
                            need(pe, kept, j)
                            for h in range(KH):
                                last = nc.tensor.transpose(bank[7 - r][:, h * P:h * P + P],
                                                           xs[:, 1 - r, h * P:h * P + P], ident[:, :])
                            last.then_inc(turned, 1)
                        if is_tile(j):
                            pe.wait_ge(kept, j + 1)
                            for c in range(NCH + 1):
                                w = 512 if c < NCH else D
                                if c in act_chunks:
                                    need(pe, act_took, (j - 1) * len(act_chunks) + c // 2 + 1)
                                else:
                                    need(pe, dve_took, (j - 1) * (len(dve_chunks) + 1)
                                         + (c // 2 if c < NCH else len(dve_chunks)) + 1)
                                for h in range(KH):
                                    last = nc.tensor.matmul(bank[c][:, 0:w], xt[:, r, h, :],
                                                            weights[:, h, c * 512:c * 512 + w],
                                                            start=(h == 0), stop=(h == KH - 1))
                                last.then_inc(multiplied, 1)
                    over_tiles(pe, step, early=1)

                @block.scalar
                def _(act):
                    def step(j, r):
                        if is_tile(j + 1):
                            act.wait_ge(turned, j + 2)
                            need(act, multiplied, j * (NCH + 1))
                            nc.scalar.copy(xt[:, 1 - r].rearrange("p h n -> p (h n)"), bank[7 - r][:, 0:D]).then_inc(kept, 1)
                        if is_tile(j):
                            for k, c in enumerate(act_chunks):
                                act.wait_ge(multiplied, j * (NCH + 1) + c + 1)
                                if k == 0 and (not isinstance(j, int) or j >= 2):
                                    act.wait_ge(stored[r], (j - r) * 8)
                                nc.scalar.copy(stage[:, r, c * 512:c * 512 + 512], bank[c][:, :]).then_inc(act_took, 1)
                    over_tiles(act, step, early=1)

                @block.sync
                def _(sp):
                    def step(j, r):
                        sp.wait_ge(act_took, (j + 1) * len(act_chunks))
                        sp.wait_ge(dve_took, j * (len(dve_chunks) + 1) + len(dve_chunks))
                        sp.dma_start(rows_out[:, at(j), :], stage[:, r:r + 1, :]).then_inc(stored[r], 16)
                    over_tiles(sp, step)
                    sp.wait_ge(stored[0], 16 * (NT // 2))
                    sp.wait_ge(stored[1], 16 * (NT // 2))

        class Unit:

            def __init__(self, i, r):
                self.i, self.r, self.c = i, r, r % STRANDS
                self.n = i * RING + r
                self.w = i * (RING // STRANDS) + r // STRANDS
                self.slot = r % RING
                self.turn = (r // STRANDS) % 2
                self.fills = i + r // RING + 1
                self.fixed = isinstance(i, int)
                self.exists = not self.fixed or 0 <= self.n < NG

            def shift(self, lag):
                return Unit(self.i, self.r + lag)

            def steps(self, columns):
                start = self.w * STEPS
                strand = columns.rearrange("p (c s) -> p c s", c=STRANDS)[:, self.c, :]
                return strand[:, start:start + STEPS] if self.fixed else strand[:, bass.ds(start, STEPS)]

            def group(self, columns):
                return columns[:, self.w:self.w + 1] if self.fixed else columns[:, bass.ds(self.w, 1)]

            def place(self, eng, table, limit):
                entry = table[0:1, self.c, self.w:self.w + 1] if self.fixed else table[0:1, self.c, bass.ds(self.w, 1)]
                return bass.ds(eng.value_load(entry, min_val=0, max_val=limit - 1), 1)

        def over_units(eng, step, early=0, late=0):
            for r in range(-early, RING):
                step(Unit(0, r))
            with eng.Fori(1, ROUNDS - 1) as i:
                for r in range(RING):
                    step(Unit(i, r))
            for r in range(RING + late):
                step(Unit(ROUNDS - 1, r))

        def copy_index(eng, copy, U, index, index_now, index_ready, read):
            soon = U.shift(RING - 1)
            if soon.exists:
                if not soon.fixed or soon.n >= RING:
                    eng.wait_ge(read, soon.n - RING + 1)
                copy(index_now[:, soon.slot, :], soon.steps(index[:, :])).then_inc(index_ready, 1)

        def gather_rows(pool, pace, index_now, index_ready, table, rows, width, arrived, freed,
                        afterwards=None, late=0):
            def step(U):
                if U.exists:
                    gather(U)
                if afterwards:
                    afterwards(U)

            def gather(U):
                pool.wait_ge(index_ready, U.n + 1)
                if not U.fixed or U.n >= RING:
                    pool.wait_ge(freed, U.n - RING + 1)
                nc.gpsimd.sem_inc(pace, 1)
                for u in range(STEPS):
                    nc.gpsimd.indirect_dma_start(
                        out=rows[:, U.slot, u, 0:width], out_offset=None, in_=table,
                        in_offset=bass.IndirectOffsetOnAxis(ap=index_now[:, U.slot, u:u + 1], axis=0)
                    ).then_inc(arrived[U.slot][u], 16)
            over_units(pool, step, late=late)

        def write_onehot(onehot, U, ready):
            shape = [P, STEPS, P]
            nc.vector.tensor_tensor(onehot[:, U.slot], iota_free[:, None, :].to_broadcast(shape),
                                    U.steps(local[:, :])[:, :, None].to_broadcast(shape),
                                    ALU.is_equal).then_inc(ready, 1)

        def convolve(tag, load_next):
            with phase() as ph:
                def s(name):
                    return sem(f"{tag}_{name}")

                rows = sb(f"{tag}_rows", [P, RING, STEPS, D], F32, ph)
                onehot = sb(f"{tag}_onehot", [P, RING, STEPS, P], F32, ph)
                index_now = sb(f"{tag}_index", [P, RING, STEPS], I32, ph)
                pace, index_ready = s("pace"), s("index_ready")
                arrived = [[s(f"arrived{r}_{u}") for u in range(STEPS)] for r in range(RING)]
                onehot_ready, summed, added, loaded = s("onehot_ready"), s("summed"), s("added"), s("loaded")
                block = ph.enter_context(nc.Block())

                @block.gpsimd
                def _(pool):
                    gather_rows(pool, pace, index_now, index_ready, table8, rows, D, arrived, summed)

                @block.sync
                def _(sp):
                    sp.wait_ge(loaded, 16 * load_next(sp, loaded))

                @block.vector
                def _(dve):
                    def step(U):
                        ahead, behind = U.shift(1), U.shift(-1)
                        if ahead.exists:
                            need(dve, summed, ahead.n - RING + 1)
                            write_onehot(onehot, ahead, onehot_ready)
                        if behind.exists:
                            own = OWN[:, behind.place(dve, group_tile, NT), :].rearrange("p a c -> p (a c)")
                            dve.wait_ge(summed, U.n)
                            need(dve, added, U.n - 1)
                            nc.vector.tensor_tensor(own, own, bank[(U.slot - 1) % 2][:, 0:D], ALU.add).then_inc(added, 1)
                        copy_index(dve, nc.vector.tensor_copy, U, index8, index_now, index_ready, summed)
                    over_units(dve, step, early=RING - 1, late=1)

                @block.tensor
                def _(pe):
                    def step(U):
                        pe.wait_ge(onehot_ready, U.n + 1)
                        need(pe, added, U.n - 1)
                        for u in range(STEPS):
                            pe.wait_ge(arrived[U.slot][u], U.fills * 16)
                            last = nc.tensor.matmul(bank[U.slot % 2][:, 0:D], onehot[:, U.slot, u, :],
                                                    rows[:, U.slot, u, :], start=(u == 0), stop=(u == STEPS - 1))
                        last.then_inc(summed, 1)
                    over_units(pe, step)

        def attend(tag, AGG, first_guard, last_guard, load_next):
            with phase() as ph:
                def s(name):
                    return sem(f"{tag}_{name}")

                def t(name, shape, dt=F32):
                    return sb(f"{tag}_{name}", shape, dt, ph)

                EDGES = STEPS * P
                rows = t("rows", [P, RING, STEPS, 2 * D])
                onehot = t("onehot", [P, RING, STEPS, P])
                turned_onehot = t("turned_onehot", [P, 2, STEPS, P])
                index_now = t("index", [P, RING, STEPS], I32)
                resets = t("resets", [P, 2, EDGES + 1])
                scores = t("scores", [P, 2, STEPS, STRANDS, H])
                forth = t("forth", [P, 2, EDGES])
                guard = t("guard", [P, 2, EDGES])
                change = t("change", [P, 2])
                factor = t("factor", [P, 2])
                minus_one = t("minus_one", [P, 1])
                minus_ident = t("minus_ident", [P, P])
                off_pick = t("off_pick", [P, 2, P])
                pick = t("pick", [P, 2, P])
                spread = t("spread", [P, 2, P])
                factors = t("factors", [P, 2, P])
                distance = t("distance", [P, STEPS, P])
                weighted = t("weighted", [P, 2, STRANDS, STEPS, H, HW])
                pace, index_ready = s("pace"), s("index_ready")
                arrived = [[s(f"arrived{r}_{u}") for u in range(STEPS)] for r in range(RING)]
                resets_in = [s(f"resets_in{r}") for r in range(2)]
                onehot_ready, onehot_turned, onehot_kept = s("onehot_ready"), s("onehot_turned"), s("onehot_kept")
                queried, multiplied, scored = s("queried"), s("multiplied"), s("scored")
                messages_ready, summed, scaled, added = s("messages_ready"), s("summed"), s("scaled"), s("added")
                vector_scaled = s("vector_scaled")
                scores_turned, forth_ready, guard_ready = s("scores_turned"), s("forth_ready"), s("guard_ready")
                scores_moved, guard_turned, weights_ready = s("scores_moved"), s("guard_turned"), s("weights_ready")
                change_ready, factor_ready, pick_ready, factor_spread, factors_kept = (
                    s("change_ready"), s("factor_ready"), s("pick_ready"), s("factor_spread"), s("factors_kept"))
                distance_ready, off_pick_ready, less_ready, spread_ready = (
                    s("distance_ready"), s("off_pick_ready"), s("less_ready"), s("spread_ready"))
                first_guarded, cleared, loaded = s("first_guarded"), s("cleared"), s("loaded")
                block = ph.enter_context(nc.Block())

                q_bank, sum_bank = (bank[0], bank[1]), (bank[5], bank[6])
                onehot_bank, score_bank, guard_bank, factor_bank = bank[2], bank[3], bank[4], bank[7]
                flat_resets = step_resets.rearrange("k e -> (k e)").rearrange("(o n) -> o n", o=1)
                FREE = STRANDS - 1
                VECTOR_SCALES = (0,)
                POOL_SCALES = [c for c in range(STRANDS) if c not in VECTOR_SCALES]
                SCALE_LAG = RING - 1
                LAG = STRANDS

                @block.sync
                def _(sp):
                    def step(U):
                        if U.c == 0:
                            need(sp, guard_ready, U.w - 1)
                            for c in range(STRANDS):
                                start = (U.w + c * LEN) * EDGES
                                part = slice(start, start + EDGES + 1) if U.fixed else bass.ds(start, EDGES + 1)
                                sp.dma_start(resets[c * H:(c + 1) * H, U.turn, :],
                                             flat_resets[:, part].to_broadcast([H, EDGES + 1])).then_inc(resets_in[U.turn], 16)
                    loads = load_next(sp, loaded)
                    over_units(sp, step)
                    sp.wait_ge(loaded, 16 * loads)

                @block.gpsimd
                def _(pool):
                    def scale_down(U):
                        done = U.shift(-SCALE_LAG)
                        if not done.exists or done.c in VECTOR_SCALES:
                            return
                        agg = AGG[:, done.place(pool, group_slot, NT + STRANDS - 1)].rearrange("p a h w -> p (a h) w")
                        pool.wait_ge(factors_kept, done.w + 1)
                        pool.wait_ge(added, FREE + done.n - STRANDS + 1)
                        nc.gpsimd.sem_inc(pace, 1)
                        fac = factors[:, done.turn, done.c * H:(done.c + 1) * H]
                        nc.gpsimd.tensor_tensor(agg, agg, fac[:, :, None].to_broadcast([P, H, HW]),
                                                ALU.mult).then_inc(scaled, 1)

                    gather_rows(pool, pace, index_now, index_ready, table2, rows, 2 * D,
                                arrived, messages_ready, scale_down, late=SCALE_LAG)

                @block.vector
                def _(dve):
                    v = nc.vector
                    v.memset(minus_one[:, :], -1.0)
                    v.tensor_scalar(minus_ident[:, :], ident[:, :], -1.0, None, ALU.mult)
                    v.memset(forth[:, 1, :], -BIG)
                    v.memset(guard[:, 1, :], -BIG)
                    v.memset(first_guard[:, :], -BIG)
                    v.memset(AGG[:], 0.0).then_inc(cleared, 1)
                    dve.wait_ge(cleared, 1)
                    v.sem_inc(added, FREE)

                    def step(U):
                        late, done = U.shift(-LAG), U.shift(-LAG - 2)
                        t, o = U.turn, 1 - U.turn
                        if U.exists:
                            dve.wait_ge(queried, U.n + 1)
                            for u in range(STEPS):
                                dve.wait_ge(arrived[U.slot][u], U.fills * 16)
                            v.tensor_tensor(rows[:, U.slot, :, 0:D], rows[:, U.slot, :, 0:D],
                                            q_bank[U.r % 2][:, :].rearrange("p (u c) -> p u c", u=STEPS),
                                            ALU.mult).then_inc(multiplied, 1)
                        if done.exists:
                            agg = AGG[:, done.place(dve, group_slot, NT + STRANDS - 1)].rearrange("p a h w -> p (a h) w")
                        if done.exists and done.c in VECTOR_SCALES:
                            dve.wait_ge(factors_kept, done.w + 1)
                            need(dve, added, done.n - 1)
                            fac = factors[:, done.turn, done.c * H:(done.c + 1) * H]
                            v.tensor_tensor(agg, agg, fac[:, :, None].to_broadcast([P, H, HW]),
                                            ALU.mult).then_inc(vector_scaled, 1)
                        if U.exists:
                            dve.wait_ge(multiplied, U.n + 1)
                            need(dve, scores_moved, U.w - 1)
                            v.tensor_reduce(scores[:, t, :, U.c, :],
                                            rows[:, U.slot, :, 0:D].rearrange("p u (h d) -> p u h d", h=H),
                                            AX.X, ALU.add).then_inc(scored, 1)
                        if U.c == 0 and late.exists:
                            dve.wait_ge(guard_ready, U.w)
                            need(dve, first_guarded, U.w - 1)
                            v.scalar_tensor_tensor(first_guard[:, :], guard[:, o, 0:1], late.group(still_first[:, :]),
                                                   first_guard[:, :], ALU.add, ALU.max).then_inc(first_guarded, 1)
                        if done.exists:
                            if done.c in VECTOR_SCALES:
                                dve.wait_ge(vector_scaled, done.w + 1)
                            else:
                                dve.wait_ge(scaled, done.w * len(POOL_SCALES) + POOL_SCALES.index(done.c) + 1)
                            dve.wait_ge(summed, done.n + 1)
                            v.tensor_tensor(agg, agg, sum_bank[done.r % 2][:, 0:H * HW].rearrange("p (h w) -> p h w", h=H),
                                            ALU.add).then_inc(added, 1)
                        if late.exists:
                            dve.wait_ge(weights_ready, late.w + 1)
                            into = weighted[:, late.turn, late.c]
                            v.tensor_tensor(into[:, :, :, 0:DH],
                                            rows[:, late.slot, :, D:2 * D].rearrange("p u (h d) -> p u h d", h=H),
                                            into[:, :, :, DH:HW].to_broadcast([P, STEPS, H, DH]),
                                            ALU.mult).then_inc(messages_ready, 1)
                        if U.c == STRANDS - 1 and U.exists:
                            dve.wait_ge(resets_in[t], (U.fills * 16 * STRANDS))
                            dve.wait_ge(scores_turned, U.w + 1)
                            need(dve, forth_ready, U.w)
                            need(dve, guard_ready, U.w)
                            v.tensor_tensor_scan(forth[:, t, :], resets[:, t, 0:EDGES], score_bank[:, 0:EDGES],
                                                 forth[:, o, EDGES - 1:EDGES], ALU.add, ALU.max).then_inc(forth_ready, 1)
                            dve.wait_ge(forth_ready, U.w + 1)
                            need(dve, guard_turned, U.w - 1)
                            need(dve, change_ready, U.w)
                            v.tensor_tensor_scan(guard[:, t, ::-1], resets[:, t, EDGES:0:-1], forth[:, t, ::-1],
                                                 -BIG, ALU.add, ALU.max).then_inc(guard_ready, 1)
                    over_units(dve, step, late=LAG + 2)
                    v.tensor_copy(last_guard[:, :], guard[:, (LEN - 1) % 2, EDGES - 1:EDGES])

                @block.tensor
                def _(pe):
                    pe.wait_ge(cleared, 1)

                    def step(U):
                        following, ahead, late = U.shift(1), U.shift(2), U.shift(-LAG - 1)
                        t, o = U.turn, 1 - U.turn
                        if following.exists:
                            query = OWN[:, following.place(pe, group_tile, NT), :].rearrange("p a c -> p (a c)")
                            pe.wait_ge(onehot_kept, following.n + 1)
                            need(pe, multiplied, following.n - 1)
                            for u in range(STEPS):
                                last = nc.tensor.matmul(q_bank[following.r % 2][:, u * D:u * D + D],
                                                        turned_onehot[:, following.r % 2, u, :], query,
                                                        start=True, stop=True)
                            last.then_inc(queried, 1)
                        if ahead.exists:
                            pe.wait_ge(onehot_ready, ahead.n + 1)
                            need(pe, onehot_kept, ahead.n)
                            for u in range(STEPS):
                                last = nc.tensor.transpose(onehot_bank[:, u * P:u * P + P],
                                                           onehot[:, ahead.slot, u, :], ident[:, :])
                            last.then_inc(onehot_turned, 1)
                        if U.c == 0 and U.shift(-LAG).exists:
                            pe.wait_ge(guard_ready, U.w)
                            for u in range(STEPS):
                                last = nc.tensor.matmul(guard_bank[:, u * P:u * P + P], guard[:, o, u * P:u * P + P],
                                                        minus_ident[:, :], start=False, stop=(u == STEPS - 1))
                            last.then_inc(guard_turned, 1)
                        if U.c == 0 and U.shift(-LAG).exists:
                            pe.wait_ge(pick_ready, U.w)
                            pe.wait_ge(spread_ready, U.w)
                            need(pe, factors_kept, U.w - 1)
                            nc.tensor.matmul(factor_bank[:, 0:P], pick[:, o, :], spread[:, o, :],
                                             start=True, stop=True).then_inc(factor_spread, 1)
                        if late.exists:
                            pe.wait_ge(messages_ready, late.n + 1)
                            pe.wait_ge(added, FREE + late.n - 1)
                            for u in range(STEPS):
                                last = nc.tensor.matmul(sum_bank[late.r % 2][:, 0:H * HW], onehot[:, late.slot, u, :],
                                                        weighted[:, late.turn, late.c, u].rearrange("p h w -> p (h w)"),
                                                        start=(u == 0), stop=(u == STEPS - 1))
                            last.then_inc(summed, 1)
                        if U.c == STRANDS - 1 and U.exists:
                            pe.wait_ge(scored, U.n + 1)
                            need(pe, forth_ready, U.w)
                            for u in range(STEPS):
                                last = nc.tensor.transpose(score_bank[:, u * P:u * P + P],
                                                           scores[:, t, u].rearrange("p c h -> p (c h)"), ident[:, :])
                            last.then_inc(scores_turned, 1)
                            need(pe, weights_ready, U.w)
                            for u in range(STEPS):
                                last = nc.tensor.matmul(guard_bank[:, u * P:u * P + P], ident[:, :],
                                                        scores[:, t, u].rearrange("p c h -> p (c h)"),
                                                        start=(u == 0), stop=False)
                            last.then_inc(scores_moved, 1)
                    over_units(pe, step, early=2, late=LAG + 1)

                @block.scalar
                def _(act):
                    act.wait_ge(cleared, 1)

                    def step(U):
                        ahead, far = U.shift(2), U.shift(3)
                        t, o = U.turn, 1 - U.turn
                        if U.c == 0 and U.shift(-LAG).exists:
                            act.wait_ge(guard_turned, U.w)
                            need(act, summed, U.n - 2 * STRANDS)
                            nc.scalar.activation(weighted[:, o, :, :, :, DH],
                                                 guard_bank[:, 0:STEPS * P].rearrange(
                                                     "p (u c h) -> p c u h", u=STEPS, c=STRANDS),
                                                 ACT.Exp).then_inc(weights_ready, 1)
                        if U.c == 0 and U.shift(-LAG).exists:
                            act.wait_ge(factor_spread, U.w)
                            need(act, scaled, (U.w - 2) * len(POOL_SCALES))
                            need(act, vector_scaled, U.w - 2)
                            nc.scalar.activation(factors[:, o, :], factor_bank[:, 0:P], ACT.Identity,
                                                 bias=1.0).then_inc(factors_kept, 1)
                        if ahead.exists:
                            act.wait_ge(onehot_turned, ahead.n + 1)
                            need(act, queried, ahead.n - 1)
                            nc.scalar.copy(turned_onehot[:, ahead.r % 2].rearrange("p u n -> p (u n)"),
                                           onehot_bank[:, 0:STEPS * P]).then_inc(onehot_kept, 1)
                        if far.exists:
                            need(act, onehot_ready, far.n)
                            for u in range(STEPS):
                                last = nc.scalar.activation(distance[:, u, :], iota_free[:, :], ACT.Abs,
                                                            bias=far.steps(local[:, :])[:, u:u + 1], scale=-1.0)
                            last.then_inc(distance_ready, 1)
                            act.wait_ge(distance_ready, far.n + 1)
                            need(act, summed, far.n - RING + 1)
                            nc.scalar.activation(onehot[:, far.slot].rearrange("p u n -> p (u n)"),
                                                 distance[:].rearrange("p u n -> p (u n)"), ACT.Relu,
                                                 bias=1.0, scale=-1.0).then_inc(onehot_ready, 1)
                        if U.c == STRANDS - 1 and U.exists:
                            act.wait_ge(guard_ready, U.w + 1)
                            nc.scalar.activation(change[:, t:t + 1], guard[:, o, EDGES - 1:EDGES], ACT.Relu,
                                                 bias=guard[:, t, 0:1], scale=-1.0).then_inc(change_ready, 1)
                            act.wait_ge(change_ready, U.w + 1)
                            nc.scalar.activation(factor[:, t:t + 1], change[:, t:t + 1], ACT.Exp,
                                                 scale=-1.0).then_inc(factor_ready, 1)
                            nc.scalar.activation(off_pick[:, t, :], iota_free[:, :], ACT.Abs,
                                                 bias=U.group(first_local[:, :]), scale=-1.0).then_inc(off_pick_ready, 1)
                            act.wait_ge(factor_ready, U.w + 1)
                            nc.scalar.activation(factor[:, t:t + 1], factor[:, t:t + 1], ACT.Identity,
                                                 bias=minus_one[:, 0:1]).then_inc(less_ready, 1)
                            act.wait_ge(off_pick_ready, U.w + 1)
                            need(act, factor_spread, U.w - 1)
                            nc.scalar.activation(pick[:, t, :], off_pick[:, t, :], ACT.Relu,
                                                 bias=1.0, scale=-1.0).then_inc(pick_ready, 1)
                            act.wait_ge(less_ready, U.w + 1)
                            nc.scalar.activation(spread[:, t, :], ident[:, :], ACT.Copy,
                                                 scale=factor[:, t:t + 1]).then_inc(spread_ready, 1)
                        copy_index(act, nc.scalar.copy, U, index2, index_now, index_ready, multiplied)
                    over_units(act, step, early=RING - 1, late=LAG)

        def merge(tag, AGG, first_guard, last_guard):
            with phase() as ph:
                def t(name, shape, dt=F32):
                    return sb(f"{tag}_{name}", shape, dt, ph)

                diag = t("diag", [P, 2, P])
                guards = t("guards", [P, ENDS, H])
                same = t("same", [P, ENDS, ENDS])
                shared = t("shared", [P, ENDS, H, ENDS])
                most = t("most", [P, ENDS, H])
                factor = t("factor", [P, ENDS, H])
                chain, diag_ready, turned, less_ready, exp_ready = (
                    sem(f"{tag}_{k}") for k in ("chain", "diag_ready", "turned", "less_ready", "exp_ready"))
                block = ph.enter_context(nc.Block())

                @block.tensor
                def _(pe):
                    pe.wait_ge(diag_ready, 2)
                    for k in range(2):
                        last = nc.tensor.matmul(bank[0][:, k * P:(k + 1) * P], ones[:, :], diag[:, k, :],
                                                start=True, stop=True)
                    last.then_inc(turned, 1)

                @block.scalar
                def _(act):
                    act.wait_ge(less_ready, 1)
                    nc.scalar.activation(factor[:], most[:], ACT.Exp).then_inc(exp_ready, 1)

                @block.vector
                def _(dve):
                    v = nc.vector
                    n = [0]

                    def link(ins):
                        n[0] += 1
                        ins.then_inc(chain, 1)
                        dve.wait_ge(chain, n[0])

                    v.tensor_scalar(diag[:, 0, :], ident[:, :], first_guard[:, 0:1], None, ALU.mult).then_inc(diag_ready, 1)
                    v.tensor_scalar(diag[:, 1, :], ident[:, :], last_guard[:, 0:1], None, ALU.mult).then_inc(diag_ready, 1)
                    ids = end_node[:].rearrange("p k c -> p (k c)")
                    link(v.tensor_tensor(same[:], ids[:, :, None].to_broadcast([P, ENDS, ENDS]),
                                         ids[:, None, :].to_broadcast([P, ENDS, ENDS]), ALU.is_equal))
                    link(v.tensor_scalar(same[:], same[:], -1.0, BIG, ALU.add, ALU.mult))
                    dve.wait_ge(turned, 1)
                    link(v.tensor_copy(guards[:].rearrange("p a h -> p (a h)"), bank[0][:, 0:ENDS * H]))
                    for a in range(ENDS):
                        v.tensor_tensor(shared[:, a], guards[:].rearrange("p b h -> p h b"),
                                        same[:, a, None, :].to_broadcast([P, H, ENDS]), ALU.add).then_inc(chain, 1)
                    n[0] += ENDS
                    slots = [bass.ds(dve.value_load(group_slot[0:1, c, g:g + 1], min_val=0,
                                                    max_val=NT + STRANDS - 2), 1)
                             for g in (0, LEN - 1) for c in range(STRANDS)]
                    dve.wait_ge(chain, n[0])
                    v.tensor_reduce(most[:], shared[:], AX.X, ALU.max).then_inc(chain, 1)
                    n[0] += 1
                    tiles = [bass.ds(dve.value_load(group_tile[0:1, c, 0:1], min_val=0, max_val=NT - 1), 1)
                             for c in range(1, STRANDS)]
                    dve.wait_ge(chain, n[0])
                    link(v.tensor_tensor(most[:], guards[:], most[:], ALU.subtract))
                    v.tensor_scalar(most[:], most[:], 0.0, None, ALU.min).then_inc(less_ready, 1)
                    dve.wait_ge(exp_ready, 1)
                    link(v.tensor_scalar(factor[:], factor[:], -1.0, None, ALU.add))
                    link(v.tensor_tensor(factor[:], factor[:], at_end[:].rearrange("p k c -> p (k c)")[:, :, None]
                                         .to_broadcast([P, ENDS, H]), ALU.mult))
                    for k in range(2):
                        for c in range(STRANDS):
                            slot = slots[k * STRANDS + c]
                            agg = AGG[:, slot].rearrange("p a h w -> p (a h) w")
                            link(v.scalar_tensor_tensor(agg, factor[:, k * STRANDS + c, :, None].to_broadcast([P, H, HW]),
                                                        1.0, agg, ALU.add, ALU.mult))
                    for c in range(1, STRANDS):
                        agg = AGG[:, tiles[c - 1]].rearrange("p a h w -> p (a h w)")
                        link(v.tensor_tensor(agg, agg, AGG[:, NT - 1 + c].rearrange("p h w -> p (h w)"), ALU.add))

        def norm(tag, A, B, store):
            with phase() as ph:
                stats = sb(f"{tag}_stats", [P, NT, 6], F32, ph)
                mv = sb(f"{tag}_mv", [P, NT, 2], F32, ph)
                rstd = sb(f"{tag}_rstd", [P, NT], F32, ph)
                eps = sb(f"{tag}_eps", [P, 1], F32, ph)
                chain, var_ready, rooted, done, stored = (
                    sem(f"{tag}_{k}") for k in ("chain", "var_ready", "rooted", "done", "stored"))
                shift = sb(f"{tag}_shift", [P, NT], F32, ph)
                half_added, shift_ready, act_done = (sem(f"{tag}_{k}") for k in ("half_added", "shift_ready", "act_done"))
                block = ph.enter_context(nc.Block())
                HALF = NT // 2
                QUARTER = NT // 4

                @block.gpsimd
                def _(pool):
                    for k in range(2):
                        part = slice(HALF + k * QUARTER, HALF + (k + 1) * QUARTER)
                        nc.gpsimd.tensor_tensor(A[:, part], A[:, part], B[:, part], ALU.add).then_inc(half_added, 1)

                @block.vector
                def _(dve):
                    v = nc.vector
                    v.memset(eps[:, :], EPS)
                    v.tensor_tensor(A[:, 0:HALF], A[:, 0:HALF], B[:, 0:HALF], ALU.add).then_inc(chain, 1)
                    dve.wait_ge(chain, 1)
                    for j in range(NT):
                        if j >= HALF:
                            dve.wait_ge(half_added, 1 + (j - HALF) // QUARTER)
                        v.bn_stats(stats[:, j, :], A[:, j, :]).then_inc(chain, 1)
                    dve.wait_ge(chain, 1 + NT)
                    for j in range(NT):
                        v.bn_aggr(mv[:, j, :], stats[:, j, :]).then_inc(var_ready, 1)
                    dve.wait_ge(rooted, 1)
                    v.reciprocal(rstd[:, :], rstd[:, :]).then_inc(chain, 1)
                    dve.wait_ge(chain, 2 + NT)
                    v.scalar_tensor_tensor(shift[:, :], mv[:, :, 0], -1.0, rstd[:, :], ALU.mult,
                                           ALU.mult).then_inc(shift_ready, 1)
                    for j in range(0, NT, 2):
                        v.tensor_scalar(A[:, j, :], A[:, j, :], mv[:, j, 0:1], rstd[:, j:j + 1], ALU.subtract,
                                        ALU.mult).then_inc(done, 1)

                @block.scalar
                def _(act):
                    act.wait_ge(var_ready, NT)
                    nc.scalar.activation(rstd[:, :], mv[:, :, 1], ACT.Sqrt, bias=eps[:, 0:1]).then_inc(rooted, 1)
                    act.wait_ge(shift_ready, 1)
                    for j in range(1, NT, 2):
                        nc.scalar.activation(A[:, j, :], A[:, j, :], ACT.Identity, bias=shift[:, j:j + 1],
                                             scale=rstd[:, j:j + 1]).then_inc(act_done, 1)

                if store:
                    @block.sync
                    def _(sp):
                        CUTS = (0, 6, 12, NT - 1)
                        for k in range(len(CUTS) - 1):
                            a, b = CUTS[k], CUTS[k + 1]
                            sp.wait_ge(done, ceil_div(b, 2))
                            sp.wait_ge(act_done, b // 2)
                            sp.dma_start(out[a * P:b * P, :].rearrange("(j p) c -> p j c", p=P),
                                         A[:, a:b, :]).then_inc(stored, 16)
                        sp.wait_ge(done, ceil_div(NT, 2))
                        sp.wait_ge(act_done, NT // 2)
                        sp.dma_start(out[(NT - 1) * P:N, :], A[0:LAST, NT - 1, :]).then_inc(stored, 16)
                        sp.wait_ge(stored, 16 * len(CUTS))

        def relu_layer():
            with nc.Block() as block:
                @block.vector
                def _(dve):
                    nc.vector.tensor_scalar(Hs[:], OWN[:], 0.0, None, ALU.max)

        def load_heads(sp, layer, loaded):
            pri_flat = pri[layer].rearrange("h t -> (h t)")
            PB = DH * R2
            sp.dma_start(plain[:, 0], Wk[layer].rearrange("(h p) c -> p h c", p=P)).then_inc(loaded, 16)
            sp.dma_start(plain[:, 1], Wv[layer].rearrange("(h p) c -> p h c", p=P)).then_inc(loaded, 16)
            sp.dma_start(head_table[:, :, T2:], Wq[layer].rearrange("(h p) c -> p h c", p=P)).then_inc(loaded, 16)
            for i, a in enumerate((Watt, Wmsg)):
                sp.dma_start(small[:, i], a[layer].rearrange("h t d f -> (h t d) f")
                             .rearrange("(b p) f -> p b f", p=P)).then_inc(loaded, 16)
            for b in range(NB):
                sp.dma_start(prior[:, b:b + 1], pri_flat[b * PB:(b + 1) * PB].rearrange("(k o) -> k o", o=1)
                             .to_broadcast([PB, DH])).then_inc(loaded, 16)
            return 5 + NB

        def head_weights(tag, weights):
            with phase() as ph:
                def t(name, shape, dt=F32):
                    return sb(f"{tag}_{name}", shape, dt, ph)

                def s(name):
                    return sem(f"{tag}_{name}")

                wide = t("wide", [P, 2, KH, NB, P])
                turned = t("turned", [P, 2, KH, NB, P])
                blocks = t("blocks", [P, 2, NB, R2, DH, DH])
                ready, made, moved, kept, multiplied = (
                    s(k) for k in ("ready", "made", "moved", "kept", "multiplied"))
                block = ph.enter_context(nc.Block())
                PB = DH * R2

                @block.vector
                def _(dve):
                    v = nc.vector
                    for i in range(2):
                        for h in range(KH):
                            v.tensor_copy(wide[:, i, h].rearrange("p b (h t d) -> p (b h) t d", h=DH, t=R2),
                                          plain[:, i, h].rearrange("p (h d) -> p h d", h=H)[:, :, None, :]
                                          .to_broadcast([P, H, R2, DH])).then_inc(ready, 1)
                    v.tensor_tensor(small[:, 0], small[:, 0], prior[:, :, None].to_broadcast([P, NB, DH]),
                                    ALU.mult).then_inc(made, 1)
                    dve.wait_ge(made, 1)
                    v.tensor_scalar(small[:, 0], small[:, 0], float(np.float32(1) / np.sqrt(np.float32(DH))), None,
                                    ALU.mult).then_inc(made, 1)
                    dve.wait_ge(made, 2)
                    for i in range(2):
                        for b in range(NB):
                            v.tensor_tensor(blocks[:, i, b].rearrange("p t h f -> p (t h) f"),
                                            blockmask[:].rearrange("p t h -> p (t h)")[:, :, None].to_broadcast([P, PB, DH]),
                                            small[:, i, b, None, :].to_broadcast([P, PB, DH]), ALU.mult).then_inc(made, 1)
                    for n in range(2 * KH):
                        dve.wait_ge(moved, n + 1)
                        v.tensor_copy(turned[:, n // KH, n % KH].rearrange("p b c -> p (b c)"),
                                      bank[n][:, :]).then_inc(kept, 1)
                    for n in range(2 * KH):
                        i, h = n // KH, n % KH
                        dve.wait_ge(multiplied, n + 1)
                        dest = weights[:, h, 0:T2].rearrange("p (t i h f) -> p t i h f", t=R2, i=2, h=H)[:, :, i]
                        for b in range(NB):
                            v.tensor_copy(dest[:, :, b * DH:(b + 1) * DH, :].rearrange("p t h f -> p t (h f)"),
                                          bank[n][:, b * P:(b + 1) * P].rearrange("p (t c) -> p t c", t=R2))

                @block.tensor
                def _(pe):
                    for n in range(2 * KH):
                        i, h = n // KH, n % KH
                        pe.wait_ge(ready, n + 1)
                        for b in range(NB):
                            last = nc.tensor.transpose(bank[n][:, b * P:(b + 1) * P], wide[:, i, h, b, :], ident[:, :])
                        last.then_inc(moved, 1)
                    pe.wait_ge(made, 2 + 2 * NB)
                    for n in range(2 * KH):
                        i, h = n // KH, n % KH
                        pe.wait_ge(kept, n + 1)
                        for b in range(NB):
                            last = nc.tensor.matmul(bank[n][:, b * P:(b + 1) * P], turned[:, i, h, b, :],
                                                    blocks[:, i, b].rearrange("p t h f -> p (t h f)"),
                                                    start=True, stop=True)
                        last.then_inc(multiplied, 1)

        def mix_layer(tag, xin, AGG, wa, gate):
            with phase() as ph:
                def t(name, shape, dt=F32):
                    return sb(f"{tag}_{name}", shape, dt, ph)

                def s(name):
                    return sem(f"{tag}_{name}")

                attended = t("attended", [P, 2, D])
                below = t("below", [P, 2, H])
                xt = t("xt", [P, 2, KH, P])
                rest = t("rest", [P, 2, D])
                chain, exped = s("chain"), s("exped")
                bounded, inverted, divided = s("bounded"), s("inverted"), s("divided")
                turned, kept, multiplied, mixed, scaled = (
                    s("turned"), s("kept"), s("multiplied"), s("mixed"), s("scaled"))
                block = ph.enter_context(nc.Block())

                @block.scalar
                def _(act):
                    nc.scalar.activation(gate[:, 1:2], gate[:, 0:1], ACT.Exp, scale=-1.0).then_inc(exped, 1)

                    def step(j, r):
                        act.wait_ge(turned, j + 1)
                        need(act, multiplied, j - 1)
                        nc.scalar.copy(xt[:, r].rearrange("p h n -> p (h n)"), bank[r][:, 0:D]).then_inc(kept, 1)
                    over_tiles(act, step)

                @block.vector
                def _(dve):
                    v = nc.vector
                    dve.wait_ge(exped, 1)
                    v.tensor_scalar(gate[:, 1:2], gate[:, 1:2], 1.0, None, ALU.add).then_inc(chain, 1)
                    dve.wait_ge(chain, 1)
                    v.reciprocal(gate[:, 2:3], gate[:, 1:2]).then_inc(chain, 1)
                    dve.wait_ge(chain, 2)
                    v.tensor_scalar(gate[:, 3:4], gate[:, 2:3], -1.0, 1.0, ALU.mult, ALU.add).then_inc(chain, 1)
                    dve.wait_ge(chain, 3)

                    def step(j, r):
                        n, k = j + 2, r
                        if is_tile(n):
                            v.tensor_scalar(below[:, k], AGG[:, at(n), :, DH].rearrange("p a h -> p (a h)"),
                                            1e-30, None, ALU.max).then_inc(bounded, 1)
                            dve.wait_ge(bounded, n + 1)
                            v.reciprocal(below[:, k], below[:, k]).then_inc(inverted, 1)
                            dve.wait_ge(inverted, n + 1)
                            need(dve, turned, n - 1)
                            v.tensor_tensor(attended[:, k].rearrange("p (h d) -> p h d", h=H),
                                            AGG[:, at(n), :, 0:DH].rearrange("p a h d -> p (a h) d"),
                                            below[:, k, :, None].to_broadcast([P, H, DH]), ALU.mult).then_inc(divided, 1)
                        if is_tile(j):
                            dve.wait_ge(multiplied, j + 1)
                            dve.wait_ge(scaled, j + 1)
                            v.scalar_tensor_tensor(Hs[:, at(j), :].rearrange("p a c -> p (a c)"), bank[2 + r][:, 0:D],
                                                   gate[:, 2:3], rest[:, r], ALU.mult, ALU.add).then_inc(mixed, 1)
                        if is_tile(n):
                            need(dve, mixed, n - 1)
                            v.tensor_scalar(rest[:, k], xin[:, at(n), :].rearrange("p a c -> p (a c)"),
                                            gate[:, 3:4], None, ALU.mult).then_inc(scaled, 1)
                    over_tiles(dve, step, early=2)

                @block.tensor
                def _(pe):
                    def step(j, r):
                        if is_tile(j + 1):
                            pe.wait_ge(divided, j + 2)
                            need(pe, kept, j)
                            for h in range(KH):
                                last = nc.tensor.transpose(bank[1 - r][:, h * P:h * P + P],
                                                           attended[:, 1 - r, h * P:h * P + P], ident[:, :])
                            last.then_inc(turned, 1)
                        if is_tile(j):
                            pe.wait_ge(kept, j + 1)
                            need(pe, mixed, j - 1)
                            for h in range(KH):
                                last = nc.tensor.matmul(bank[2 + r][:, 0:D], xt[:, r, h, :], wa[:, h, :],
                                                        start=(h == 0), stop=(h == KH - 1))
                            last.then_inc(multiplied, 1)
                    over_tiles(pe, step, early=1)

        def attention_layer(layer, xin):
            with phase() as ph:
                head_weights(f"t{layer}w", head_table)
                dense(f"t{layer}d", xin, head_table, T2, table2, None)
            with phase() as ph:
                AGG = sb(f"t{layer}_AGG", [P, NT + STRANDS - 1, H, HW], F32, ph)
                first_guard = sb(f"t{layer}_first_guard", [P, 1], F32, ph)
                last_guard = sb(f"t{layer}_last_guard", [P, 1], F32, ph)
                wa = sb(f"t{layer}_wa", [P, KH, D], F32, ph)
                gate = sb(f"t{layer}_gate", [P, 4], F32, ph)

                def load_next(sp, loaded):
                    sp.dma_start(wa[:], Wa[layer].rearrange("(h p) c -> p h c", p=P)).then_inc(loaded, 16)
                    sp.dma_start(gate[:, 0:1], skip[layer:layer + 1].rearrange("(o c) -> o c", o=1)
                                 .to_broadcast([P, 1])).then_inc(loaded, 16)
                    return 2 + (load_heads(sp, layer + 1, loaded) if layer + 1 < LAYERS else 0)

                attend(f"t{layer}a", AGG, first_guard, last_guard, load_next)
                merge(f"t{layer}g", AGG, first_guard, last_guard)
                mix_layer(f"t{layer}m", xin, AGG, wa, gate)

        with phase() as ph:
            weights = [sb(f"weights{k}", [P, KH, T8 + D], F32, ph) for k in range(2)]
            bias = [sb(f"bias{k}", [P, D], F32, ph) for k in range(2)]
            prepare(weights[0], bias[0])
            dense("c1_d", X, weights[0], T8, table8, bias[0])
            convolve("c1_c", lambda sp, loaded: load_weights(sp, weights[1], bias[1], W2, self_w2, b2, loaded))
            relu_layer()
            dense("c2_d", Hs, weights[1], T8, table8, bias[1])
            convolve("c2_c", lambda sp, loaded: load_heads(sp, 0, loaded))
        norm("n1", X, OWN, False)
        for layer in range(LAYERS):
            attention_layer(layer, Hs if layer else X)
        norm("n2", X, Hs, True)


_INS = ['x', 'src', 'dst', 'edge_type_2', 'edge_type_8', 'L0_gnn_W1', 'L0_gnn_self_w1', 'L0_gnn_b1', 'L0_gnn_W2',
        'L0_gnn_self_w2', 'L0_gnn_b2', 'L1_gnn_Wk', 'L1_gnn_Wq', 'L1_gnn_Wv', 'L1_gnn_Wa', 'L1_gnn_Watt',
        'L1_gnn_Wmsg', 'L1_gnn_pri', 'L1_gnn_skip']


def kernel(**inputs):
    import numpy as _np
    import concourse.bacc as _bacc
    from concourse import mybir as _mybir
    from concourse.bass_utils import run_bass_kernel_spmd as _run

    nc = _bacc.Bacc("TRN2", target_bir_lowering=False, num_devices=1)
    arrays, args = {}, []
    for name in _INS:
        a = _np.ascontiguousarray(inputs[name])
        arrays[f"in_{name}_dram"] = a
        args.append(nc.dram_tensor(f"in_{name}_dram", a.shape, _mybir.dt.from_np(a.dtype), kind="ExternalInput").ap())
    shape = inputs["x"].shape
    args.append(nc.dram_tensor("out_0_dram", shape, _mybir.dt.float32, kind="ExternalOutput").ap())
    build(nc, *args)
    r = _run(nc, [arrays], core_ids=[0])
    return r.results[0]["out_0_dram"]
```
